# Optimizing a Trainium2 kernel written in Bass

```python
import numpy as np
import jax
import jax.numpy as jnp

def _softmax(x, axis=-1):
    return jax.nn.softmax(x, axis=axis)

def _gelu(x):
    return jax.nn.gelu(x, approximate=True)

def _silu(x):
    return jax.nn.silu(x)

def _sigmoid(x):
    return jax.nn.sigmoid(x)

def _layernorm(x, axis=-1, eps=1e-05):
    m = jnp.mean(x, axis=axis, keepdims=True)
    v = jnp.var(x, axis=axis, keepdims=True)
    return (x - m) / jnp.sqrt(v + eps)

def _scatter_add(tgt, idx, src, axis=0):
    return tgt.at[idx].add(src)

def _segment_sum(src, seg, n):
    return jax.ops.segment_sum(src, seg, n)
kernel_name = 'mk_decoder_preln_d1_seqx_r4_f71488'

def setup_inputs(seed: int=0):
    np.random.seed(seed)
    _w = jnp.asarray

    def _rec_inputs():
        import jax
        import jax.numpy as jnp
        _rk = jax.random.key(seed)
        x = -0.0002928 + 1 * jax.random.normal(jax.random.fold_in(_rk, 1), (32, 256, 256), jnp.float32)
        _lenS = 256 - jax.random.randint(jax.random.fold_in(_rk, 7), (32,), 0, max(1, 256 // 4) + 1, jnp.int32)
        _lenS2 = 120 - jax.random.randint(jax.random.fold_in(_rk, 8), (32,), 0, max(1, 120 // 4) + 1, jnp.int32)
        _ctx_1024P = jax.random.normal(jax.random.fold_in(_rk, 11), (32, 16, 256), jnp.float32)
        _ctx_1024c = jax.random.dirichlet(jax.random.fold_in(_rk, 511), 0.3 * jnp.ones((16,), jnp.float32), (32, 120))
        _ctx_1024t = jnp.einsum('bsk,bkd->bsd', _ctx_1024c, _ctx_1024P)
        _ctx_1024t = _ctx_1024t * jax.lax.rsqrt(jnp.mean(jnp.square(_ctx_1024t)) + 1e-12) * 0.953939
        ctx_1024 = 0.000376506 + 0.999991 * (_ctx_1024t + 0.3 * jax.random.normal(jax.random.fold_in(_rk, 611), (32, 120, 256), jnp.float32))
        _validS = jnp.arange(256)[None, :] < _lenS[:, None]
        _validS2 = jnp.arange(120)[None, :] < _lenS2[:, None]
        _causal = jnp.tril(jnp.ones((256, 256), dtype=bool))
        mask_1x1xSxS2_fk1 = jnp.where(jnp.broadcast_to(_validS2[0:1, None, None, :], (1, 1, 256, 120)), 1.0, 0.0).astype(jnp.float32)
        return (x, ctx_1024, mask_1x1xSxS2_fk1)
    x, ctx_1024, mask_1x1xSxS2_fk1 = _rec_inputs()

    def _L0_attn_setup():
        import jax, jax.numpy as jnp
        import numpy as np
        D_MODEL = 256
        N_HEADS = 16
        WINDOW = 64
        SEQ = 1024
        BATCH = 1
        NEG_INF = -1e+30
        key = jax.random.key(seed)
        ks = jax.random.split(key, 5)
        scale = 0.02
        inp = {'x': jax.random.normal(ks[0], (BATCH, SEQ, D_MODEL), jnp.float32)}
        for i, name in enumerate(['Wq', 'Wk', 'Wv', 'Wo']):
            inp[name] = jax.random.normal(ks[1 + i], (D_MODEL, D_MODEL), jnp.float32) * scale
        for name in ['bq', 'bk', 'bv', 'bo']:
            inp[name] = jnp.zeros((D_MODEL,), jnp.float32)
        return inp
    _L0_attn_all = _L0_attn_setup()
    _L0_attn_in = {k: v for k, v in _L0_attn_all.items() if k in ('Wq', 'bq', 'Wk', 'bk', 'Wv', 'bv', 'Wo', 'bo')}
    del _L0_attn_all

    def _L0_xattn_setup():
        import jax, jax.numpy as jnp
        import numpy as np
        D_MODEL = 256
        NUM_HEADS = 16
        DEPTH = D_MODEL // NUM_HEADS
        NEG_INF_SCALE = -1000000000.0

        def _split_heads(x):
            B, S, _ = x.shape
            return x.reshape(B, S, NUM_HEADS, DEPTH).transpose(0, 2, 1, 3)
        key = jax.random.key(seed)
        ks = jax.random.split(key, 12)
        B, S = (2, 512)
        q = jax.random.normal(ks[0], (B, S, D_MODEL), dtype=jnp.float32)
        k = jax.random.normal(ks[1], (B, S, D_MODEL), dtype=jnp.float32)
        v = jax.random.normal(ks[2], (B, S, D_MODEL), dtype=jnp.float32)
        mask = jnp.triu(jnp.ones((S, S), dtype=jnp.float32), k=1)[None, None]
        scale = 1.0 / np.sqrt(D_MODEL)
        Wq = jax.random.normal(ks[3], (D_MODEL, D_MODEL), dtype=jnp.float32) * scale
        bq = jnp.zeros((D_MODEL,), dtype=jnp.float32)
        Wk = jax.random.normal(ks[4], (D_MODEL, D_MODEL), dtype=jnp.float32) * scale
        bk = jnp.zeros((D_MODEL,), dtype=jnp.float32)
        Wv = jax.random.normal(ks[5], (D_MODEL, D_MODEL), dtype=jnp.float32) * scale
        bv = jnp.zeros((D_MODEL,), dtype=jnp.float32)
        Wo = jax.random.normal(ks[6], (D_MODEL, D_MODEL), dtype=jnp.float32) * scale
        bo = jnp.zeros((D_MODEL,), dtype=jnp.float32)
        return {'v': v, 'k': k, 'q': q, 'mask': mask, 'Wq': Wq, 'bq': bq, 'Wk': Wk, 'bk': bk, 'Wv': Wv, 'bv': bv, 'Wo': Wo, 'bo': bo}
    _L0_xattn_all = _L0_xattn_setup()
    _L0_xattn_in = {k: v for k, v in _L0_xattn_all.items() if k in ('Wq', 'bq', 'Wk', 'bk', 'Wv', 'bv', 'Wo', 'bo')}
    del _L0_xattn_all

    def _L0_ffn_setup():
        import jax, jax.numpy as jnp
        import numpy as np
        BLOCK = 32
        W_BITS = 4
        ACT_BITS = 16

        def act_qdq(x):
            qmax = 2.0 ** (ACT_BITS - 1) - 1.0
            scale = jnp.maximum(jnp.max(jnp.abs(x)) / qmax, 1e-12)
            return jnp.clip(jnp.round(x / scale), -qmax - 1.0, qmax) * scale

        def fixed_qdq_u16(x):
            scale = 1.0 / 65536.0
            return jnp.clip(jnp.round(x / scale), 0.0, 65535.0) * scale

        def lpbq_dequant(w):
            O, I = w.shape
            qmax = 2.0 ** (W_BITS - 1) - 1.0
            wb = w.reshape(O, I // BLOCK, BLOCK)
            s = jnp.maximum(jnp.max(jnp.abs(wb), axis=-1, keepdims=True) / qmax, 1e-12)
            wq = jnp.clip(jnp.round(wb / s), -qmax - 1.0, qmax) * s
            return wq.reshape(O, I)
        key = jax.random.key(seed)
        k1, k2, k3, k4 = jax.random.split(key, 4)
        B, S, H, I = (2, 1024, 256, 768)
        x = jax.random.normal(k1, (B, S, H), jnp.float32)
        w_gate = jax.random.normal(k2, (I, H), jnp.float32) * 0.02
        w_up = jax.random.normal(k3, (I, H), jnp.float32) * 0.02
        w_down = jax.random.normal(k4, (H, I), jnp.float32) * 0.02
        return {'x': x, 'w_gate': w_gate, 'w_up': w_up, 'w_down': w_down}
    _L0_ffn_all = _L0_ffn_setup()
    _L0_ffn_in = {k: v for k, v in _L0_ffn_all.items() if k in ('w_gate', 'w_up', 'w_down')}
    del _L0_ffn_all
    return {'x': x, 'ctx_1024': ctx_1024, 'mask_1x1xSxS2_fk1': mask_1x1xSxS2_fk1, 'L0_attn_Wq': _L0_attn_in['Wq'], 'L0_attn_bq': _L0_attn_in['bq'], 'L0_attn_Wk': _L0_attn_in['Wk'], 'L0_attn_bk': _L0_attn_in['bk'], 'L0_attn_Wv': _L0_attn_in['Wv'], 'L0_attn_bv': _L0_attn_in['bv'], 'L0_attn_Wo': _L0_attn_in['Wo'], 'L0_attn_bo': _L0_attn_in['bo'], 'L0_xattn_Wq': _L0_xattn_in['Wq'], 'L0_xattn_bq': _L0_xattn_in['bq'], 'L0_xattn_Wk': _L0_xattn_in['Wk'], 'L0_xattn_bk': _L0_xattn_in['bk'], 'L0_xattn_Wv': _L0_xattn_in['Wv'], 'L0_xattn_bv': _L0_xattn_in['bv'], 'L0_xattn_Wo': _L0_xattn_in['Wo'], 'L0_xattn_bo': _L0_xattn_in['bo'], 'L0_ffn_w_gate': _L0_ffn_in['w_gate'], 'L0_ffn_w_up': _L0_ffn_in['w_up'], 'L0_ffn_w_down': _L0_ffn_in['w_down']}

def reference(x, ctx_1024, mask_1x1xSxS2_fk1, L0_attn_Wq, L0_attn_bq, L0_attn_Wk, L0_attn_bk, L0_attn_Wv, L0_attn_bv, L0_attn_Wo, L0_attn_bo, L0_xattn_Wq, L0_xattn_bq, L0_xattn_Wk, L0_xattn_bk, L0_xattn_Wv, L0_xattn_bv, L0_xattn_Wo, L0_xattn_bo, L0_ffn_w_gate, L0_ffn_w_up, L0_ffn_w_down):
    import jax
    import jax.numpy as jnp

    def _L0_attn_ref(x, Wq, bq, Wk, bk, Wv, bv, Wo, bo):
        import jax, jax.numpy as jnp
        import numpy as np
        D_MODEL = 256
        N_HEADS = 16
        WINDOW = 64
        SEQ = 1024
        BATCH = 1
        NEG_INF = -1e+30
        B, S, D = x.shape
        H = N_HEADS
        hd = D // H
        q = (x @ Wq + bq).reshape(B, S, H, hd).transpose(0, 2, 1, 3)
        k = (x @ Wk + bk).reshape(B, S, H, hd).transpose(0, 2, 1, 3)
        v = (x @ Wv + bv).reshape(B, S, H, hd).transpose(0, 2, 1, 3)
        scale = 1.0 / jnp.sqrt(jnp.asarray(hd, x.dtype))
        scores = jnp.einsum('bhqd,bhkd->bhqk', q, k) * scale
        i = jnp.arange(S)[:, None]
        j = jnp.arange(S)[None, :]
        allowed = (j <= i) & (i - j < WINDOW)
        scores = jnp.where(allowed, scores, NEG_INF)
        attn = jax.nn.softmax(scores, axis=-1)
        out = jnp.einsum('bhqk,bhkd->bhqd', attn, v)
        out = out.transpose(0, 2, 1, 3).reshape(B, S, D)
        return out @ Wo + bo

    def _L0_xattn_ref(v, k, q, mask, Wq, bq, Wk, bk, Wv, bv, Wo, bo):
        import jax, jax.numpy as jnp
        import numpy as np
        D_MODEL = 256
        NUM_HEADS = 16
        DEPTH = D_MODEL // NUM_HEADS
        NEG_INF_SCALE = -1000000000.0

        def _split_heads(x):
            B, S, _ = x.shape
            return x.reshape(B, S, NUM_HEADS, DEPTH).transpose(0, 2, 1, 3)
        B, Sq, _ = q.shape
        qh = _split_heads(q @ Wq + bq)
        kh = _split_heads(k @ Wk + bk)
        vh = _split_heads(v @ Wv + bv)
        logits = jnp.einsum('bhqd,bhkd->bhqk', qh, kh) / jnp.sqrt(jnp.asarray(DEPTH, dtype=jnp.float32))
        logits = logits + mask * NEG_INF_SCALE
        attn = jax.nn.softmax(logits, axis=-1)
        out = jnp.einsum('bhqk,bhkd->bhqd', attn, vh)
        out = out.transpose(0, 2, 1, 3).reshape(B, Sq, D_MODEL)
        return out @ Wo + bo

    def _L0_ffn_ref(x, w_gate, w_up, w_down):
        import jax, jax.numpy as jnp
        import numpy as np
        BLOCK = 32
        W_BITS = 4
        ACT_BITS = 16

        def act_qdq(x):
            qmax = 2.0 ** (ACT_BITS - 1) - 1.0
            scale = jnp.maximum(jnp.max(jnp.abs(x)) / qmax, 1e-12)
            return jnp.clip(jnp.round(x / scale), -qmax - 1.0, qmax) * scale

        def fixed_qdq_u16(x):
            scale = 1.0 / 65536.0
            return jnp.clip(jnp.round(x / scale), 0.0, 65535.0) * scale

        def lpbq_dequant(w):
            O, I = w.shape
            qmax = 2.0 ** (W_BITS - 1) - 1.0
            wb = w.reshape(O, I // BLOCK, BLOCK)
            s = jnp.maximum(jnp.max(jnp.abs(wb), axis=-1, keepdims=True) / qmax, 1e-12)
            wq = jnp.clip(jnp.round(wb / s), -qmax - 1.0, qmax) * s
            return wq.reshape(O, I)
        x = act_qdq(x)
        up = act_qdq(x @ lpbq_dequant(w_up).T)
        gate = act_qdq(x @ lpbq_dequant(w_gate).T)
        sig = fixed_qdq_u16(jax.nn.sigmoid(gate))
        gate = act_qdq(gate * sig)
        o = act_qdq(gate * up)
        return o @ lpbq_dequant(w_down).T
    x = x + _L0_attn_ref(_layernorm(x, axis=-1), L0_attn_Wq, L0_attn_bq, L0_attn_Wk, L0_attn_bk, L0_attn_Wv, L0_attn_bv, L0_attn_Wo, L0_attn_bo)
    x = x + _L0_xattn_ref(ctx_1024, ctx_1024, _layernorm(x, axis=-1), mask_1x1xSxS2_fk1, L0_xattn_Wq, L0_xattn_bq, L0_xattn_Wk, L0_xattn_bk, L0_xattn_Wv, L0_xattn_bv, L0_xattn_Wo, L0_xattn_bo)
    x = x + _L0_ffn_ref(_layernorm(x, axis=-1), L0_ffn_w_gate, L0_ffn_w_up, L0_ffn_w_down)
    return x

_drawn_inputs = setup_inputs


def setup_inputs(seed=0):
    import zlib

    import numpy as np

    out = dict(_drawn_inputs(seed))
    spreads = {'L0_attn_bq': (0.0, 0.8),
     'L0_attn_bk': (0.0, 0.8),
     'L0_attn_bv': (0.0, 0.318),
     'L0_attn_bo': (0.0, 0.1),
     'L0_xattn_bq': (0.0, 0.325),
     'L0_xattn_bk': (0.0, 0.8),
     'L0_xattn_bv': (0.0, 0.1),
     'L0_xattn_bo': (0.0, 0.1)}
    factors = {'L0_attn_Wq': 8.0, 'L0_attn_Wk': 8.0, 'L0_attn_Wv': 4.047}
    for name, (base, spread) in spreads.items():
        noise = np.random.default_rng([zlib.crc32(name.encode()), seed]).standard_normal(out[name].shape)
        drawn = base * np.exp(spread * noise) if base else spread * noise
        out[name] = jnp.asarray(drawn.astype(out[name].dtype))
    for name, factor in factors.items():
        out[name] = (out[name] * factor).astype(out[name].dtype)
    return out
```

```python
from contextlib import ExitStack

import concourse.bass as bass
from concourse import mybir

F32 = mybir.dt.float32
F16 = mybir.dt.float16
U32 = mybir.dt.uint32
BF16 = mybir.dt.bfloat16
ALU = mybir.AluOpType
ACT = mybir.ActivationFunctionType
AX = mybir.AxisListType
RMAX = bass.bass_isa.ReduceOp.max

P = 128
BATCH, SEQ, D = 32, 256, 256
HEADS = 16
HD = D // HEADS
NC = D // P
NT = SEQ // P
HC = HEADS // NC
HU = 4
UNITS = NT * HEADS // HU
WIN = 64
NWIN = SEQ // WIN
CTX = 120
FF = 768
NM = FF // P
QBLOCK = 32
TOK = BATCH * SEQ
GRP = 512
NG = TOK // GRP
EPS = 1e-5

XN = 256.0
WS = 256.0
QK = 8.0
VS = 64.0
LOGIT = 1.0 / (QK * QK * HD ** 0.5)
SHIFT = 10.0
NEG = -1e30
MASK_SCALE = -1e9
MAGIC = 1.5 * 2.0 ** 23
QMAX = 32767.0
TINY = 1e-12
SIG = 65536.0

LOAD, PREP, SELF, MID, CROSS, END = 2, 1, 0, -1, -2, -3
JOBS = [["P1", "X1"], ["P2"], ["P3", "X2"], ["B1", "D1"], ["P4", "P5"], ["B2", "D2"], ["B3"], ["D3", "B4"]]
ORDER = [j for slot in JOBS for j in slot]
STAGE = {"P": PREP, "B": MID, "X": MID, "D": END}
FIRST_IT, LAST_IT = -LOAD, BATCH - 1 - END
LOOP_FROM, LOOP_TO = 4, BATCH - LOAD


class Iteration:

    def __init__(self, pair, parity):
        self.pair, self.parity = pair, parity
        self.i, self.fixed = pair * 2 + parity, isinstance(pair, int)

    def has(self, off):
        return not self.fixed or 0 <= self.i + off < BATCH

    def batch(self, off):
        return self.i + off

    def par(self, off):
        return (self.parity + off) % 2

    def nth(self, off):
        return self.pair + (self.parity + off) // 2


def pipeline(eng, body):
    for i in range(FIRST_IT, LOOP_FROM):
        body(Iteration(i // 2, i % 2))
    with eng.Fori(LOOP_FROM // 2, LOOP_TO // 2, 1) as pair:
        body(Iteration(pair, 0))
        body(Iteration(pair, 1))
    for i in range(LOOP_TO, LAST_IT + 1):
        body(Iteration(i // 2, i % 2))


def lag(stage, k, d):
    return (stage, k - d) if k >= d else (stage - 1, k - d + UNITS)


BANK_JOBS = [["P1", "P2", "X2", "D1", "P5", "D2", "D3"], ["X1", "P3", "B1", "P4", "B2", "B3", "B4"]]


def job_before(it, job):
    jobs = BANK_JOBS[0] if job in BANK_JOBS[0] else BANK_JOBS[1]
    n = jobs.index(job)
    for back in range(1, 8 * len(jobs)):
        name = jobs[(n - back) % len(jobs)]
        stage = STAGE[name[0]] + (n - back) // len(jobs)
        if it.has(stage):
            return name, stage
    return None


def decoder_kernel(nc, x, ctx_in, mask, w_self, b_self, w_cross, b_cross, w_gate, w_up, w_down, out):
    x_d = x.rearrange("b (t p) d -> b p t d", p=P)
    out_g = out.rearrange("b (t p) d -> (b t) p d", p=P)
    x1_d = nc.dram_tensor("x1_scratch", [BATCH, P, NT, D], F32, kind="Internal").ap()
    x2_d = nc.dram_tensor("x2_scratch", [BATCH, P, NT, D], F32, kind="Internal").ap()
    h_d = nc.dram_tensor("h_scratch", [BATCH, P, NC, SEQ], F32, kind="Internal").ap()
    raw_d = nc.dram_tensor("raw_scratch", [2, NG, NM, P, GRP], F32, kind="Internal").ap()
    o_d = nc.dram_tensor("o_scratch", [NG, NM, P, GRP], F32, kind="Internal").ap()

    top = ExitStack()
    with top:
        def sb(name, shape, dt=F32, ctx=top):
            return ctx.enter_context(nc.sbuf_tensor(name, shape, dt))

        def sem(name):
            return top.enter_context(nc.semaphore(name))

        banks = [top.enter_context(nc.psum_tensor(f"bank{n}", [P, 512], F32)) for n in range(8)]

        ident = sb("ident", [P, P])
        w_down_t = sb("w_down_t", [P, NM, 2, D], F16)
        stats = sb("stats", [P, 24])
        magic = sb("magic", [P, 1])
        S_H, I_H, S_U, C_U, S_G, C_G, S_P, C_P, S_O, C_O, RED, ALL, REAL = range(13)

        def st(n):
            return stats[:, n:n + 1]

        mid = top.enter_context(ExitStack())
        w_gu_t = sb("w_gu_t", [P, NC, 2, 2 * FF], F16, mid)
        h_max = sb("h_max", [P, BATCH], F32, mid)

        att = top.enter_context(ExitStack())
        names = ["self_q", "self_k", "self_v", "self_o", "cross_q", "cross_k", "cross_v", "cross_o"]
        SQ, SK, SV, SO, CQ, CK, CV, CO = range(8)
        w16 = sb("w16", [P, 8, NC, 2, D], F16, att)
        bias16 = sb("bias16", [64, 8, D], F16, att)
        ones16 = sb("ones16", [64, 2, SEQ], F16, att)
        ident_b = sb("ident_b", [P, P], BF16, att)
        mask_b = sb("mask_b", [P, NT, P], BF16, att)
        mask_c = sb("mask_c", [P, NT, CTX], F32, att)
        k_blk = sb("k_blk", [P, 2, NC, 2, HC, WIN + SEQ], F16, att)
        k2_blk = sb("k2_blk", [P, 2, NC, 2, HC, CTX], F16, att)
        half = sb("half", [P, NT], F32, att)
        s_wload = sem("weights_loaded")
        s_pool = sem("pool_chain")
        s_const = sem("constants_ready")
        s_dve = sem("dve_chain")
        s_wq = sem("ffn_weight_dequantised")
        s_wt = sem("ffn_weight_transposed")
        s_we = sem("ffn_weight_evacuated")

        with ExitStack() as c0:
            w_raw = sb("w_raw", [P, 8, NC, D], F32, c0)
            b_raw = sb("b_raw", [64, 8, D], F32, c0)
            f_raw = sb("f_raw", [P, 3, 2 * FF], F32, c0)
            f_amax = sb("f_amax", [P, 3, 48], F32, c0)
            f_rec = sb("f_rec", [P, 3, 48], F32, c0)
            tmp_b = sb("tmp_b", [P, P], BF16, c0)
            block = c0.enter_context(nc.Block())

            @block.sync
            def _(sp):
                for n, w in enumerate(w_self + w_cross):
                    sp.dma_start(w_raw[:, n, :, :], w.rearrange("(c p) n -> p c n", p=P)).then_inc(s_wload, 16)
                for n, b in enumerate(b_self + b_cross):
                    row = b.rearrange("(a n) -> a n", a=1)
                    sp.dma_start(b_raw[0:1, n, :], row).then_inc(s_wload, 16)
                    sp.dma_start(b_raw[32:33, n, :], row).then_inc(s_wload, 16)
                for n, w in enumerate((w_up, w_gate)):
                    sp.dma_start(f_raw[:, n, :].rearrange("p (m k) -> p m k", m=NM),
                                 w.rearrange("(m p) k -> p m k", p=P)).then_inc(s_wload, 16)
                sp.dma_start(f_raw[:, 2, :].rearrange("p (r k) -> p r k", r=NC),
                             w_down.rearrange("(r p) k -> p r k", p=P)).then_inc(s_wload, 16)
                sp.dma_start(mask_c[:, :, :],
                             mask.rearrange("a b (t p) k -> p (a b t) k", p=P)).then_inc(s_wload, 16)

            LOADED = 16 * (8 + 16 + 3 + 1)

            @block.gpsimd
            def _(pool):
                n = [0]

                def step(ins):
                    n[0] += 1
                    ins.then_inc(s_pool, 1)
                    pool.wait_ge(s_pool, n[0])

                step(pool.memset(ident[:, :], 0.0))
                step(pool.affine_select(out=ident[:, :], in_=ident[:, :], compare_op=ALU.not_equal, fill=1.0,
                                        base=0, pattern=[[-1, P]], channel_multiplier=1))
                step(pool.tensor_copy(ident_b[:, :], ident[:, :]))
                step(pool.memset(half[:, :], -0.5))
                for m, base in ((mask_b[:, 0, :], 0), (tmp_b[:, :], WIN)):
                    step(pool.memset(m, 0.0))
                    step(pool.affine_select(out=m, in_=m, compare_op=ALU.is_gt, fill=NEG,
                                            base=base, pattern=[[1, P]], channel_multiplier=-1))
                    step(pool.affine_select(out=m, in_=m, compare_op=ALU.is_ge, fill=NEG,
                                            base=WIN - base, pattern=[[-1, P]], channel_multiplier=1))
                step(pool.tensor_copy(mask_b[64:128, 0, :], tmp_b[64:128, :]))
                step(pool.tensor_copy(mask_b[:, 1, :], mask_b[:, 0, :]))
                pool.memset(mask_b[0:64, 0, 0:WIN], NEG).then_inc(s_const, 1)
                for blk in (k_blk, k2_blk):
                    step(pool.memset(blk[:, :, :, :, :, :].rearrange("p a c l h n -> p (a c l h n)").bitcast(U32), 0))

            @block.vector
            def _(dve):
                n = [0]

                def step(ins):
                    n[0] += 1
                    ins.then_inc(s_dve, 1)
                    dve.wait_ge(s_dve, n[0])

                step(dve.memset(bias16[:, :, :], 0.0))
                step(dve.memset(ones16[:, 0, :], XN))
                step(dve.memset(ones16[:, 1, :], VS))
                dve.wait_ge(s_wload, LOADED)
                step(dve.tensor_scalar(mask_c[:, :, :], mask_c[:, :, :], MASK_SCALE, None, ALU.mult))
                for hl in range(2):
                    row = slice(32 * hl, 32 * hl + 1)
                    step(dve.tensor_scalar(bias16[row, :, :], b_raw[row, :, :], WS, None, ALU.mult))
                lo = slice(32, 33)
                step(dve.scalar_tensor_tensor(out=bias16[lo, :, :], in0=b_raw[lo, :, :], scalar=WS,
                                              in1=bias16[lo, :, :], op0=ALU.mult, op1=ALU.subtract))
                for k in range(8):
                    step(dve.tensor_scalar(w16[:, k, :, 0, :], w_raw[:, k, :, :], WS, None, ALU.mult))
                    step(dve.scalar_tensor_tensor(out=w16[:, k, :, 1, :], in0=w_raw[:, k, :, :], scalar=WS,
                                                  in1=w16[:, k, :, 0, :], op0=ALU.mult, op1=ALU.subtract))
                blocks = f_raw[:, :, :].rearrange("p a (n k) -> p (a n) k", k=QBLOCK)
                amax = f_amax[:, :, :].rearrange("p a n -> p (a n)")
                rec = f_rec[:, :, :].rearrange("p a n -> p (a n)")
                wide = [P, 3 * 48, QBLOCK]
                step(dve.tensor_reduce(out=amax, in_=blocks, axis=AX.X, op=ALU.max, apply_absolute_value=True))
                step(dve.tensor_scalar(amax, amax, 1.0 / 7.0, TINY, ALU.mult, ALU.max))
                step(dve.reciprocal(rec, amax))
                step(dve.tensor_tensor(blocks, blocks, rec.unsqueeze(2).to_broadcast(wide), ALU.mult))
                step(dve.tensor_scalar(f_raw[:, :, :], f_raw[:, :, :], MAGIC, MAGIC, ALU.add, ALU.subtract))
                dve.tensor_tensor(blocks, blocks, amax.unsqueeze(2).to_broadcast(wide), ALU.mult).then_inc(s_wq, 1)
                for q in range(9):
                    dve.wait_ge(s_wt, q + 1)
                    bank = banks[q % 8]
                    if q < 6:
                        a, m0 = q // 3, 2 * (q % 3)
                        for hl in range(2):
                            dst = w_gu_t[:, :, hl, a * FF + m0 * P:a * FF + (m0 + 2) * P]
                            src = bank[:, :].rearrange("p (c k) -> p c k", c=NC)
                            hi = w_gu_t[:, :, 0, a * FF + m0 * P:a * FF + (m0 + 2) * P]
                            if hl == 0:
                                step(dve.tensor_scalar(dst, src, WS, None, ALU.mult))
                            else:
                                step(dve.scalar_tensor_tensor(out=dst, in0=src, scalar=WS, in1=hi,
                                                              op0=ALU.mult, op1=ALU.subtract))
                    else:
                        m0 = 2 * (q - 6)
                        src = bank[:, :].rearrange("p (m k) -> p m k", m=2)
                        hi, low = w_down_t[:, m0:m0 + 2, 0, :], w_down_t[:, m0:m0 + 2, 1, :]
                        step(dve.tensor_scalar(hi, src, WS, None, ALU.mult))
                        step(dve.scalar_tensor_tensor(out=low, in0=src, scalar=WS, in1=hi,
                                                      op0=ALU.mult, op1=ALU.subtract))
                    dve.sem_inc(s_we, 1)

            @block.tensor
            def _(pe):
                pe.wait_ge(s_const, 1)
                pe.wait_ge(s_wq, 1)
                for q in range(9):
                    if q >= 8:
                        pe.wait_ge(s_we, q - 7)
                    for j in range(4):
                        if q < 6:
                            a, m, c = q // 3, 2 * (q % 3) + j % 2, j // 2
                            src = f_raw[:, a, m * D + c * P:m * D + (c + 1) * P]
                        else:
                            m, r = 2 * (q - 6) + j // 2, j % 2
                            src = f_raw[:, 2, r * FF + m * P:r * FF + (m + 1) * P]
                        last = pe.transpose(banks[q % 8][:, j * P:(j + 1) * P], src, ident[:, :])
                    last.then_inc(s_wt, 1)

        a = att
        x_in = sb("x_in", [P, 2, NT, D], F32, a)
        xn = sb("xn", [P, NT, D], F32, a)
        xn_t = sb("xn_t", [P, NC, 2, WIN + SEQ], F16, a)
        q_t = sb("q_t", [P, 2, NC, 2, SEQ], F16, a)
        k_t = sb("k_t", [P, NC, 2, SEQ], F16, a)
        v_hi = sb("v_hi", [P, 2, NWIN, HEADS, HD + 1], F16, a)
        v_lo = sb("v_lo", [P, 2, NWIN, HEADS, HD], F16, a)
        x_mid = sb("x_mid", [P, NT, D], F32, a)
        x1 = sb("x1", [P, NT, D], F32, a)
        xn2 = sb("xn2", [P, NT, D], F32, a)
        xn2_t = sb("xn2_t", [P, NC, 2, SEQ], F16, a)
        q2_t = sb("q2_t", [P, 2, NC, 2, SEQ], F16, a)
        ctx_sb = sb("ctx_sb", [CTX, D], F32, a)
        ctx_t = sb("ctx_t", [P, NC, 2, CTX], F16, a)
        k2_t = sb("k2_t", [P, NC, 2, CTX], F16, a)
        v2_hi = sb("v2_hi", [CTX, 2, HEADS, HD + 1], F16, a)
        v2_lo = sb("v2_lo", [CTX, 2, HEADS, HD], F16, a)
        x1_back = sb("x1_back", [P, NT, D], F32, a)
        x2 = sb("x2", [P, NT, D], F32, a)
        h = sb("h", [P, NT, D], F32, a)
        h_t = sb("h_t", [P, NC, SEQ], F32, a)

        class Attention:

            def __init__(self, name, stage, keys, s_bank, t_bank, o_bank):
                self.stage, self.keys, self.cols = stage, keys, HU * keys
                self.s_bank, self.t_bank, self.o_bank = banks[s_bank], banks[t_bank], banks[o_bank]
                self.u = sb(f"{name}_u", [P, 2, HU * keys], F32, a)
                self.p32 = sb(f"{name}_p32", [P, 2, HU * P], F32, a)
                self.p_hi = sb(f"{name}_p_hi", [P, 4, HU * P], F16, a)
                self.p_lo = sb(f"{name}_p_lo", [P, 4, HU * P], F16, a)
                self.mx = sb(f"{name}_mx", [P, 2, HU], F32, a)
                self.mshift = sb(f"{name}_mshift", [P, 2, HU], F32, a)
                self.den = sb(f"{name}_den", [P, HEADS], F32, a)
                self.o = sb(f"{name}_o", [P, NT, D], F32, a)
                self.o_t = sb(f"{name}_o_t", [P, NC, 2, SEQ], F16, a)
                self.s_scores = sem(f"{name}_scores_done")
                self.s_max = sem(f"{name}_max_done")
                self.s_shift = sem(f"{name}_shift_done")
                self.s_u = sem(f"{name}_u_ready")
                self.s_t = sem(f"{name}_transposed")
                self.s_p32 = sem(f"{name}_p32_ready")
                self.s_hi = sem(f"{name}_p_hi_ready")
                self.s_lo = sem(f"{name}_p_lo_ready")
                self.s_pv = sem(f"{name}_pv_done")
                self.s_den = sem(f"{name}_den_ready")
                self.s_o = sem(f"{name}_o_ready")

        A = Attention("self", SELF, P, 0, 2, 4)
        C = Attention("cross", CROSS, CTX, 1, 3, 5)
        C.y = sb("cross_y", [P, 2, HU * CTX], F32, a)
        C.s_y = sem("cross_y_ready")
        job_bank = {j: banks[6 + n] for n in range(2) for j in BANK_JOBS[n]}
        s_job = {j: sem(f"job_{j}_products_done") for j in ORDER}
        s_hi = {j: sem(f"job_{j}_high_part_ready") for j in ORDER}
        s_got = {j: sem(f"job_{j}_evacuated") for j in ORDER}

        class Norm:

            def __init__(self, name):
                self.part = sb(f"{name}_bn_part", [P, NT, 6], F32, a)
                self.mv = sb(f"{name}_mean_var", [P, NT, 2], F32, a)
                self.ve = sb(f"{name}_var_eps", [P, NT], F32, a)
                self.rstd = sb(f"{name}_rstd", [P, NT], F32, a)
                self.s_part = sem(f"{name}_bn_part_ready")
                self.s_seen = sem(f"{name}_bn_parts_complete")
                self.s_mv = sem(f"{name}_mean_var_ready")
                self.s_ve = sem(f"{name}_var_eps_ready")
                self.s_rstd = sem(f"{name}_rstd_ready")
                self.s_done = sem(f"{name}_normalised")

        LN1, LN2, LN3 = Norm("ln1"), Norm("ln2"), Norm("ln3")
        s_x = [sem(f"x_loaded_{n}") for n in range(2)]
        s_xm = sem("x_mid_loaded")
        s_ctx = sem("ctx_loaded")
        s_x1b = sem("x1_reloaded")
        s_x1w = sem("x1_stored")
        s_x2w = sem("x2_stored")
        s_hw = sem("h_stored")
        s_init = sem("attention_buffers_cleared")
        s_kblk = sem("k_block_diagonal_ready")
        s_k2blk = sem("k2_block_diagonal_ready")
        s_hmax = sem("h_max_ready")

        BLK = 16 * HC

        def unit(b, k):
            return b * UNITS + (k + 1)

        with nc.Block() as block:

            @block.sync
            def _(sp):
                def body(it):
                    if it.has(LOAD):
                        b = it.batch(LOAD)
                        if it.has(LOAD - 2):
                            sp.wait_ge(LN1.s_done, it.batch(LOAD - 2) + 1)
                        sp.dma_start(x_in[:, it.par(LOAD), :, :], x_d[b]).then_inc(s_x[it.par(LOAD)], 16)
                    if it.has(SELF):
                        b = it.batch(SELF)
                        if it.has(SELF - 1):
                            sp.wait_ge(s_job["X1"], it.batch(SELF - 1) + 1)
                        sp.dma_start(ctx_sb[:, :], ctx_in[b]).then_inc(s_ctx, 16)
                    if it.has(MID):
                        b = it.batch(MID)
                        if it.has(MID - 1):
                            sp.wait_ge(s_got["B2"], it.batch(MID - 1) + 1)
                        sp.dma_start(x_mid[:, :, :], x_d[b]).then_inc(s_xm, 16)
                    if it.has(END):
                        b = it.batch(END)
                        sp.wait_ge(s_x1w, 16 * (b + 1))
                        sp.dma_start(x1_back[:, :, :], x1_d[b]).then_inc(s_x1b, 16)
                    if it.has(MID):
                        b, par = it.batch(MID), it.par(MID)
                        if it.has(MID - 2):
                            sp.wait_ge(C.s_scores, unit(b - 2, UNITS - 1))
                        sp.wait_ge(s_got["X2"], b + 1)
                        for g in range(HC):
                            rows = slice(HD * g, HD * (g + 1))
                            sp.dma_start(k2_blk[rows, par, :, :, g, :], k2_t[rows, :, :, :]).then_inc(s_k2blk, 16)
                    if it.has(PREP):
                        b, par = it.batch(PREP), it.par(PREP)
                        if it.has(PREP - 2):
                            sp.wait_ge(A.s_scores, unit(b - 2, UNITS - 1))
                        sp.wait_ge(s_got["P3"], b + 1)
                        for g in range(HC):
                            rows = slice(HD * g, HD * (g + 1))
                            sp.dma_start(k_blk[rows, par, :, :, g, WIN:WIN + SEQ],
                                         k_t[rows, :, :, :]).then_inc(s_kblk, 16)
                    if it.has(MID):
                        b = it.batch(MID)
                        sp.wait_ge(s_got["B2"], b + 1)
                        sp.dma_start(x1_d[b], x1[:, :, :]).then_inc(s_x1w, 16)
                    if it.has(END):
                        b = it.batch(END)
                        sp.wait_ge(s_got["D2"], b + 1)
                        sp.dma_start(x2_d[b], x2[:, :, :]).then_inc(s_x2w, 16)
                        sp.wait_ge(s_hi["D3"], b + 1)
                        sp.dma_start(h_d[b], h_t[:, :, :]).then_inc(s_hw, 16)

                pipeline(sp, body)
                sp.wait_ge(s_x1w, 16 * BATCH)
                sp.wait_ge(s_x2w, 16 * BATCH)
                sp.wait_ge(s_hw, 16 * BATCH)

            @block.tensor
            def _(pe):
                def product(dst, lhs, rhs, first=True, last=True):
                    pe.matmul(dst, lhs[0], rhs[0], start=first, stop=False)
                    pe.matmul(dst, lhs[1], rhs[0], start=False, stop=False)
                    return pe.matmul(dst, lhs[0], rhs[1], start=False, stop=last)

                def parts(t):
                    return t(0), t(1)

                def project(dst, w, lhs_is_weight, act, cols, ones):
                    for c in range(NC):
                        wt = parts(lambda hl: w16[:, w, c, hl, cols])
                        at = parts(lambda hl: act(c, hl))
                        product(dst, wt if lhs_is_weight else at, at if lhs_is_weight else wt,
                                first=c == 0, last=False)
                    b, o = bias16[:, w, cols], ones
                    return pe.matmul(dst, b if lhs_is_weight else o, o if lhs_is_weight else b,
                                     start=False, stop=True)

                def scores_self(it, k):
                    b, par = it.batch(SELF), it.par(SELF)
                    t, g = divmod(k, HEADS // HU)
                    c, h0 = divmod(HU * g, HC)
                    if k == 0:
                        pe.wait_ge(s_got["P2"], b + 1)
                        pe.wait_ge(s_kblk, BLK * (b + 1))
                    if k or it.has(SELF - 1):
                        pe.wait_ge(A.s_u, unit(b, k - 1))
                    pe.matmul(A.s_bank[:, :], ident_b[:, :],
                              mask_b[:, t, :].unsqueeze(1).to_broadcast([P, HU, P]), start=True, stop=False)
                    for j in range(2):
                        w = 2 * t + j
                        lhs = parts(lambda hl: q_t[:, par, c, hl, t * P + WIN * j:t * P + WIN * (j + 1)])
                        rhs = parts(lambda hl: k_blk[:, par, c, hl, h0:h0 + HU, WIN * w:WIN * w + P])
                        last = product(A.s_bank[WIN * j:WIN * (j + 1), :], lhs, rhs, first=False)
                    last.then_inc(A.s_scores, 1)

                def scores_cross(it, k):
                    b, par = it.batch(CROSS), it.par(CROSS)
                    t, g = divmod(k, HEADS // HU)
                    c, h0 = divmod(HU * g, HC)
                    if k == 0:
                        pe.wait_ge(s_got["B4"], b + 1)
                        pe.wait_ge(s_k2blk, BLK * (b + 1))
                    if k or it.has(CROSS - 1):
                        pe.wait_ge(C.s_y, unit(b, k - 1))
                    product(C.s_bank[:, 0:HU * CTX],
                            parts(lambda hl: q2_t[:, par, c, hl, t * P:(t + 1) * P]),
                            parts(lambda hl: k2_blk[:, par, c, hl, h0:h0 + HU, :])).then_inc(C.s_scores, 1)

                def transposes(att_, it, k):
                    off, kk = lag(att_.stage, k, 1)
                    if not it.has(off):
                        return
                    b = it.batch(off)
                    pe.wait_ge(att_.s_u, unit(b, kk))
                    if kk or it.has(off - 1):
                        pe.wait_ge(att_.s_hi, unit(b, kk - 1))
                        pe.wait_ge(att_.s_p32, unit(b, kk - 1))
                    n = att_.keys
                    for q in range(HU):
                        last = pe.transpose(att_.t_bank[0:n, q * P:(q + 1) * P],
                                            att_.u[:, kk % 2, q * n:(q + 1) * n], ident[:, :])
                    last.then_inc(att_.s_t, 1)

                def weighted_values(att_, it, k):
                    off, kk = lag(att_.stage, k, 3)
                    if not it.has(off):
                        return
                    b, par = it.batch(off), it.par(off)
                    t, g = divmod(kk, HEADS // HU)
                    pe.wait_ge(att_.s_hi, unit(b, kk))
                    pe.wait_ge(att_.s_lo, unit(b, kk))
                    if g == 0 and (t or it.has(off - 1)):
                        pe.wait_ge(att_.s_o, b * NT + t)
                    for q in range(HU):
                        hd = HU * g + q
                        for j in range(2 if att_ is A else 1):
                            rows = slice(WIN * j, WIN * (j + 1)) if att_ is A else slice(0, P)
                            cols = slice(q * P + rows.start, q * P + rows.stop)
                            if att_ is A:
                                vh, vl = v_hi[:, par, 2 * t + j, hd, :], v_lo[:, par, 2 * t + j, hd, :]
                            else:
                                vh, vl = v2_hi[:, par, hd, :], v2_lo[:, par, hd, :]
                            hi = att_.p_hi[0:att_.keys, kk % 4, cols]
                            lo = att_.p_lo[0:att_.keys, kk % 4, cols]
                            dst = att_.o_bank[rows, hd * (HD + 1):(hd + 1) * (HD + 1)]
                            pe.matmul(dst, hi, vh, start=True, stop=False)
                            pe.matmul(dst[:, 0:HD], hi, vl, start=False, stop=False)
                            last = pe.matmul(dst, lo, vh, start=False, stop=True)
                    last.then_inc(att_.s_pv, 1)

                def transpose_tiles(bank, src):
                    for c in range(NC):
                        for t in range(NT):
                            last = pe.transpose(bank[:, c * SEQ + t * P:c * SEQ + (t + 1) * P],
                                                src[:, t, c * P:(c + 1) * P], ident[:, :])
                    return last

                def job(it, name):
                    off = STAGE[name[0]]
                    if not it.has(off):
                        return
                    b = it.batch(off)
                    bank = job_bank[name]
                    before = job_before(it, name)
                    if before:
                        pe.wait_ge(s_got[before[0]], it.batch(before[1]) + 1)
                    if name == "P1":
                        pe.wait_ge(LN1.s_done, b + 1)
                        last = transpose_tiles(bank, xn)
                    elif name in ("P2", "P3"):
                        if name == "P2":
                            pe.wait_ge(s_got["P1"], b + 1)
                        for m in range(NC):
                            last = project(bank[:, m * SEQ:(m + 1) * SEQ], SQ if name == "P2" else SK, True,
                                           lambda c, hl: xn_t[:, c, hl, WIN:WIN + SEQ],
                                           slice(m * P, (m + 1) * P), ones16[:, 0, :])
                    elif name in ("P4", "P5"):
                        for j in range(2):
                            w = j + (2 if name == "P5" else 0)
                            last = project(bank[:, j * D:(j + 1) * D], SV, False,
                                           lambda c, hl: xn_t[:, c, hl, WIN * w:WIN * w + P],
                                           slice(0, D), ones16[:, 0, 0:P])
                    elif name in ("B1", "D1"):
                        att_ = A if name == "B1" else C
                        pe.wait_ge(att_.s_o, NT * (b + 1))
                        last = transpose_tiles(bank, att_.o)
                    elif name in ("B2", "D2"):
                        att_ = A if name == "B2" else C
                        pe.wait_ge(s_got[name[0] + "1"], b + 1)
                        for t in range(NT):
                            last = project(bank[:, t * D:(t + 1) * D], SO if name == "B2" else CO, False,
                                           lambda c, hl: att_.o_t[:, c, hl, t * P:(t + 1) * P],
                                           slice(0, D), ones16[:, 1, 0:P])
                    elif name == "B3":
                        pe.wait_ge(LN2.s_done, b + 1)
                        last = transpose_tiles(bank, xn2)
                    elif name == "B4":
                        pe.wait_ge(s_got["B3"], b + 1)
                        for m in range(NC):
                            last = project(bank[:, m * SEQ:(m + 1) * SEQ], CQ, True,
                                           lambda c, hl: xn2_t[:, c, hl, :],
                                           slice(m * P, (m + 1) * P), ones16[:, 0, :])
                    elif name == "X1":
                        pe.wait_ge(s_ctx, 16 * (b + 1))
                        for c in range(NC):
                            last = pe.transpose(bank[:, c * CTX:(c + 1) * CTX], ctx_sb[:, c * P:(c + 1) * P],
                                                ident[0:CTX, 0:CTX])
                    elif name == "X2":
                        pe.wait_ge(s_got["X1"], b + 1)
                        for m in range(NC):
                            project(bank[:, m * CTX:(m + 1) * CTX], CK, True, lambda c, hl: ctx_t[:, c, hl, :],
                                    slice(m * P, (m + 1) * P), ones16[:, 1, 0:CTX])
                        last = project(bank[0:CTX, NC * CTX:NC * CTX + D], CV, False,
                                       lambda c, hl: ctx_t[:, c, hl, :], slice(0, D), ones16[:, 1, 0:CTX])
                    elif name == "D3":
                        pe.wait_ge(LN3.s_done, b + 1)
                        last = transpose_tiles(bank, h)
                    last.then_inc(s_job[name], 1)

                def body(it):
                    for k in range(UNITS):
                        for att_, scores in ((A, scores_self), (C, scores_cross)):
                            if it.has(att_.stage):
                                scores(it, k)
                            transposes(att_, it, k)
                            weighted_values(att_, it, k)
                        for name in JOBS[k]:
                            job(it, name)

                pe.wait_ge(s_init, 1)
                pipeline(pe, body)

            @block.scalar
            def _(act):
                def exps(att_, it, k):
                    off, kk = lag(att_.stage, k, 1)
                    if not it.has(off):
                        return
                    b, n = it.batch(off), att_.keys
                    act.wait_ge(att_.s_t, unit(b, kk))
                    if kk >= 4 or it.has(off - 1):
                        act.wait_ge(att_.s_pv, unit(b, kk - 4))
                    if kk >= 2 or it.has(off - 1):
                        act.wait_ge(att_.s_lo, unit(b, kk - 2))
                    act.activation(att_.p_hi[0:n, kk % 4, :], att_.t_bank[0:n, :], ACT.Exp).then_inc(att_.s_hi, 1)
                    act.activation(att_.p32[0:n, kk % 2, :], att_.t_bank[0:n, :], ACT.Exp).then_inc(att_.s_p32, 1)

                def cols(bank, n):
                    return bank[:, 0:NC * n].rearrange("p (c t) -> p c t", c=NC)

                def job(it, name):
                    off = STAGE[name[0]]
                    if not it.has(off) or name in ("B2", "D2"):
                        return
                    b, par, bank = it.batch(off), it.par(off), job_bank[name]
                    act.wait_ge(s_job[name], b + 1)
                    if name == "P1":
                        if it.has(off - 1):
                            act.wait_ge(s_job["P5"], b)
                        last = act.activation(xn_t[:, :, 0, WIN:WIN + SEQ], cols(bank, SEQ), ACT.Copy)
                    elif name == "P2":
                        if it.has(off - 2):
                            act.wait_ge(A.s_scores, unit(b - 2, UNITS - 1))
                        last = act.activation(q_t[:, par, :, 0, :], cols(bank, SEQ), ACT.Copy, scale=QK / (XN * WS))
                    elif name == "P3":
                        if it.has(off - 1):
                            act.wait_ge(s_kblk, BLK * b)
                        last = act.activation(k_t[:, :, 0, :], cols(bank, SEQ), ACT.Copy, scale=QK / (XN * WS))
                    elif name in ("P4", "P5"):
                        if it.has(off - 2):
                            act.wait_ge(A.s_pv, unit(b - 2, UNITS - 1))
                        w = 2 if name == "P5" else 0
                        last = act.activation(v_hi[:, par, w:w + 2, :, 0:HD],
                                              bank[:, :].rearrange("p (w h d) -> p w h d", w=2, h=HEADS),
                                              ACT.Copy, scale=VS / (XN * WS))
                    elif name in ("B1", "D1"):
                        att_ = A if name == "B1" else C
                        if it.has(off - 1):
                            act.wait_ge(s_job[name[0] + "2"], b)
                        last = act.activation(att_.o_t[:, :, 0, :], cols(bank, SEQ), ACT.Copy)
                    elif name == "B3":
                        if it.has(off - 1):
                            act.wait_ge(s_job["B4"], b)
                        last = act.activation(xn2_t[:, :, 0, :], cols(bank, SEQ), ACT.Copy)
                    elif name == "B4":
                        if it.has(off - 2):
                            act.wait_ge(C.s_scores, unit(b - 2, UNITS - 1))
                        last = act.activation(q2_t[:, par, :, 0, :], cols(bank, SEQ), ACT.Copy, scale=QK / (XN * WS))
                    elif name == "X1":
                        if it.has(off - 1):
                            act.wait_ge(s_job["X2"], b)
                        last = act.activation(ctx_t[:, :, 0, :], cols(bank, CTX), ACT.Copy, scale=VS)
                    elif name == "X2":
                        if it.has(off - 1):
                            act.wait_ge(s_k2blk, BLK * b)
                        if it.has(off - 2):
                            act.wait_ge(C.s_pv, unit(b - 2, UNITS - 1))
                        act.activation(k2_t[:, :, 0, :], cols(bank, CTX), ACT.Copy,
                                       scale=QK / (VS * WS)).then_inc(s_hi["X2"], 1)
                        last = act.activation(v2_hi[:, par, :, 0:HD],
                                              bank[0:CTX, NC * CTX:NC * CTX + D].rearrange("p (h d) -> p h d", h=HEADS),
                                              ACT.Copy, scale=VS / (VS * WS))
                    elif name == "D3":
                        if it.has(off - 1):
                            act.wait_ge(s_hw, 16 * b)
                        last = act.activation(h_t[:, :, :], cols(bank, SEQ), ACT.Copy)
                    last.then_inc(s_hi[name], 1)

                def body(it):
                    for k in range(UNITS):
                        exps(A, it, k)
                        exps(C, it, k)
                        for name in JOBS[k]:
                            job(it, name)

                act.wait_ge(s_init, 1)
                pipeline(act, body)

            @block.vector
            def _(dve):
                def wide(v, n):
                    return v.unsqueeze(2).to_broadcast([P, HU, n])

                def shift_self(it, k):
                    b = it.batch(SELF)
                    r = k % 2
                    s3 = A.s_bank[:, :].rearrange("p (h n) -> p h n", h=HU)
                    dve.wait_ge(A.s_scores, unit(b, k))
                    dve.tensor_reduce(out=A.mx[:, r, :], in_=s3, axis=AX.X, op=ALU.max).then_inc(A.s_max, 1)
                    dve.wait_ge(A.s_max, unit(b, k))
                    dve.tensor_scalar(A.mshift[:, r, :], A.mx[:, r, :], LOGIT, SHIFT,
                                      ALU.mult, ALU.subtract).then_inc(A.s_shift, 1)
                    dve.wait_ge(A.s_shift, unit(b, k))
                    if k >= 2 or it.has(SELF - 1):
                        dve.wait_ge(A.s_t, unit(b, k - 2))
                    dve.scalar_tensor_tensor(out=A.u[:, r, :].rearrange("p (h n) -> p h n", h=HU), in0=s3,
                                             scalar=LOGIT, in1=wide(A.mshift[:, r, :], P),
                                             op0=ALU.mult, op1=ALU.subtract).then_inc(A.s_u, 1)

                def shift_cross(it, k):
                    b = it.batch(CROSS)
                    r, t = k % 2, k // (UNITS // NT)
                    y3 = C.y[:, r, :].rearrange("p (h n) -> p h n", h=HU)
                    dve.wait_ge(C.s_scores, unit(b, k))
                    if k >= 2 or it.has(CROSS - 1):
                        dve.wait_ge(C.s_u, unit(b, k - 2))
                    dve.scalar_tensor_tensor(out=y3, in0=C.s_bank[:, 0:HU * CTX].rearrange("p (h n) -> p h n", h=HU),
                                             scalar=LOGIT,
                                             in1=mask_c[:, t, :].unsqueeze(1).to_broadcast([P, HU, CTX]),
                                             op0=ALU.mult, op1=ALU.add).then_inc(C.s_y, 1)
                    dve.wait_ge(C.s_y, unit(b, k))
                    dve.tensor_reduce(out=C.mx[:, r, :], in_=y3, axis=AX.X, op=ALU.max).then_inc(C.s_max, 1)
                    dve.wait_ge(C.s_max, unit(b, k))
                    dve.tensor_scalar(C.mshift[:, r, :], C.mx[:, r, :], SHIFT, None,
                                      ALU.subtract).then_inc(C.s_shift, 1)

                def normalise(att_, it, k):
                    off, kk = lag(att_.stage, k, 3)
                    if not it.has(off) or kk % (UNITS // NT) != UNITS // NT - 1:
                        return
                    b, t = it.batch(off), kk // (UNITS // NT)
                    o3 = att_.o_bank[:, 0:HEADS * (HD + 1)].rearrange("p (h d) -> p h d", h=HEADS)
                    dve.wait_ge(att_.s_pv, unit(b, kk))
                    dve.reciprocal(att_.den[:, :], o3[:, :, HD]).then_inc(att_.s_den, 1)
                    dve.wait_ge(att_.s_den, b * NT + (t + 1))
                    if it.has(off - 1):
                        dve.wait_ge(s_job["B1" if att_ is A else "D1"], b)
                    dve.tensor_tensor(att_.o[:, t, :].rearrange("p (h d) -> p h d", h=HEADS), o3[:, :, 0:HD],
                                      att_.den[:, :].unsqueeze(2).to_broadcast([P, HEADS, HD]),
                                      ALU.mult).then_inc(att_.s_o, 1)

                def statistics(ln, src, b, scale):
                    for t in range(NT):
                        dve.bn_stats(ln.part[:, t, :], src[:, t, :]).then_inc(ln.s_part, 1)
                    dve.wait_ge(ln.s_part, NT * (b + 1))
                    dve.sem_inc(ln.s_seen, 1)
                    for t in range(NT):
                        dve.bn_aggr(ln.mv[:, t, :], ln.part[:, t, :]).then_inc(ln.s_mv, 1)
                    dve.wait_ge(ln.s_mv, NT * (b + 1))
                    dve.tensor_scalar(ln.ve[:, :], ln.mv[:, :, 1], EPS, 1.0 / scale ** 2,
                                      ALU.add, ALU.mult).then_inc(ln.s_ve, 1)

                def apply_norm(ln, dst, src, b):
                    dve.wait_ge(ln.s_rstd, b + 1)
                    for t in range(NT):
                        last = dve.tensor_scalar(dst[:, t, :], src[:, t, :], ln.mv[:, t, 0:1], ln.rstd[:, t:t + 1],
                                                 ALU.subtract, ALU.mult)
                    last.then_inc(ln.s_done, 1)

                def cols(bank, n):
                    return bank[:, 0:NC * n].rearrange("p (c t) -> p c t", c=NC)

                def low(dst, src, hi, scale):
                    return dve.scalar_tensor_tensor(out=dst, in0=src, scalar=scale, in1=hi,
                                                    op0=ALU.mult, op1=ALU.subtract)

                def job(it, name):
                    off = STAGE[name[0]]
                    if not it.has(off):
                        return
                    b, par, bank = it.batch(off), it.par(off), job_bank[name]
                    if name in ("B2", "D2"):
                        dve.wait_ge(s_job[name], b + 1)
                    else:
                        dve.wait_ge(s_hi[name], (2 * b + 2) if name == "X2" else (b + 1))
                    if name == "P1":
                        last = low(xn_t[:, :, 1, WIN:WIN + SEQ], cols(bank, SEQ), xn_t[:, :, 0, WIN:WIN + SEQ], 1.0)
                    elif name == "P2":
                        last = low(q_t[:, par, :, 1, :], cols(bank, SEQ), q_t[:, par, :, 0, :], QK / (XN * WS))
                    elif name == "P3":
                        last = low(k_t[:, :, 1, :], cols(bank, SEQ), k_t[:, :, 0, :], QK / (XN * WS))
                    elif name in ("P4", "P5"):
                        w = 2 if name == "P5" else 0
                        last = low(v_lo[:, par, w:w + 2, :, :].rearrange("p w h d -> p (w h) d"),
                                   bank[:, :].rearrange("p (g d) -> p g d", d=HD),
                                   v_hi[:, par, w:w + 2, :, 0:HD].rearrange("p w h d -> p (w h) d"), VS / (XN * WS))
                    elif name in ("B1", "D1"):
                        o_t = (A if name == "B1" else C).o_t
                        last = low(o_t[:, :, 1, :], cols(bank, SEQ), o_t[:, :, 0, :], 1.0)
                    elif name in ("B2", "D2"):
                        src, dst = (x_mid, x1) if name == "B2" else (x1_back, x2)
                        dve.wait_ge(s_xm if name == "B2" else s_x1b, 16 * (b + 1))
                        if it.has(off - 1):
                            dve.wait_ge(s_x1w if name == "B2" else s_x2w, 16 * b)
                        last = dve.scalar_tensor_tensor(out=dst[:, :, :],
                                                        in0=bank[:, :].rearrange("p (t d) -> p t d", t=NT),
                                                        scalar=1.0 / (VS * WS), in1=src[:, :, :],
                                                        op0=ALU.mult, op1=ALU.add)
                    elif name == "B3":
                        last = low(xn2_t[:, :, 1, :], cols(bank, SEQ), xn2_t[:, :, 0, :], 1.0)
                    elif name == "B4":
                        last = low(q2_t[:, par, :, 1, :], cols(bank, SEQ), q2_t[:, par, :, 0, :], QK / (XN * WS))
                    elif name == "X1":
                        last = low(ctx_t[:, :, 1, :], cols(bank, CTX), ctx_t[:, :, 0, :], VS)
                    elif name == "X2":
                        low(v2_lo[:, par, :, :],
                            bank[0:CTX, NC * CTX:NC * CTX + D].rearrange("p (h d) -> p h d", h=HEADS),
                            v2_hi[:, par, :, 0:HD], VS / (VS * WS))
                        last = low(k2_t[:, :, 1, :], cols(bank, CTX), k2_t[:, :, 0, :], QK / (VS * WS))
                    elif name == "D3":
                        last = dve.tensor_reduce(out=h_max[:, bass.ds(b, 1)], in_=bank[:, :], axis=AX.X, op=ALU.max,
                                                 apply_absolute_value=True)
                    last.then_inc(s_got[name], 1)
                    if name in ("B2", "D2"):
                        dve.wait_ge(s_got[name], b + 1)
                        if name == "B2":
                            statistics(LN2, x1, b, XN)
                        else:
                            statistics(LN3, x2, b, 1.0)

                def body(it):
                    for k in range(UNITS):
                        if it.has(SELF):
                            shift_self(it, k)
                        if it.has(CROSS):
                            shift_cross(it, k)
                        normalise(A, it, k)
                        normalise(C, it, k)
                        for name in JOBS[k]:
                            job(it, name)
                        if k == 4 and it.has(LOAD):
                            b = it.batch(LOAD)
                            dve.wait_ge(s_x[it.par(LOAD)], 16 * (it.nth(LOAD) + 1))
                            statistics(LN1, x_in[:, it.par(LOAD), :, :], b, XN)
                        if k == 5 and it.has(LOAD):
                            b = it.batch(LOAD)
                            if it.has(LOAD - 1):
                                dve.wait_ge(s_job["P1"], b)
                            apply_norm(LN1, xn, x_in[:, it.par(LOAD), :, :], b)
                        if k == 5 and it.has(MID):
                            b = it.batch(MID)
                            if it.has(MID - 1):
                                dve.wait_ge(s_job["B3"], b)
                            apply_norm(LN2, xn2, x1, b)
                        if k == 6 and it.has(END):
                            b = it.batch(END)
                            if it.has(END - 1):
                                dve.wait_ge(s_job["D3"], b)
                            apply_norm(LN3, h, x2, b)

                dve.memset(xn_t[:, :, :, 0:WIN], 0.0)
                dve.memset(v_hi[:, :, :, :, HD:HD + 1].rearrange("p a w h d -> p (a w h) d"), 1.0)
                dve.memset(v2_hi[:, :, :, HD:HD + 1].rearrange("p a h d -> p (a h) d"), 1.0).then_inc(s_init, 1)
                pipeline(dve, body)

            @block.gpsimd
            def _(pool):
                def rstd(ln, b):
                    pool.wait_ge(ln.s_ve, b + 1)
                    pool.tensor_tensor(ln.rstd[:, :], ln.ve[:, :], half[:, :], ALU.pow).then_inc(ln.s_rstd, 1)

                def subtract_cross(it, k):
                    b, r = it.batch(CROSS), k % 2
                    pool.wait_ge(C.s_shift, unit(b, k))
                    if k >= 2 or it.has(CROSS - 1):
                        pool.wait_ge(C.s_t, unit(b, k - 2))
                    pool.tensor_tensor(C.u[:, r, :].rearrange("p (h n) -> p h n", h=HU),
                                       C.y[:, r, :].rearrange("p (h n) -> p h n", h=HU),
                                       C.mshift[:, r, :].unsqueeze(2).to_broadcast([P, HU, CTX]),
                                       ALU.subtract).then_inc(C.s_u, 1)

                def low_part(att_, it, k):
                    off, kk = lag(att_.stage, k, 2)
                    if not it.has(off):
                        return
                    b, n = it.batch(off), att_.keys
                    pool.wait_ge(att_.s_p32, unit(b, kk))
                    pool.wait_ge(att_.s_hi, unit(b, kk))
                    if kk >= 4 or it.has(off - 1):
                        pool.wait_ge(att_.s_pv, unit(b, kk - 4))
                    pool.tensor_tensor(att_.p_lo[0:n, kk % 4, :], att_.p32[0:n, kk % 2, :], att_.p_hi[0:n, kk % 4, :],
                                       ALU.subtract).then_inc(att_.s_lo, 1)

                def body(it):
                    for k in range(UNITS):
                        low_part(A, it, k)
                        low_part(C, it, k)
                        if it.has(CROSS):
                            subtract_cross(it, k)
                        if k == 4 and it.has(LOAD):
                            rstd(LN1, it.batch(LOAD))
                        if k == 5 and it.has(MID):
                            rstd(LN2, it.batch(MID))
                        if k == 5 and it.has(END):
                            rstd(LN3, it.batch(END))

                pipeline(pool, body)

        att.close()

        s_red = sem("maximum_over_free_axis_ready")
        s_all = sem("maximum_over_partitions_ready")
        s_scale = sem("scales_ready")
        chain = [0]

        def step(dve, ins):
            chain[0] += 1
            ins.then_inc(s_scale, 1)
            dve.wait_ge(s_scale, chain[0])

        def quant_scale(dve, s_out, c_out):
            step(dve, dve.tensor_tensor(st(s_out), st(ALL), st(REAL), ALU.mult))
            step(dve, dve.tensor_scalar(st(s_out), st(s_out), 1.0 / QMAX, TINY, ALU.mult, ALU.max))
            step(dve, dve.reciprocal(st(c_out), st(s_out)))
            step(dve, dve.tensor_tensor(st(c_out), st(c_out), st(REAL), ALU.mult))

        reds = [0]

        def global_max(dve, src):
            reds[0] += 1
            dve.tensor_reduce(out=st(RED), in_=src, axis=AX.X, op=ALU.max).then_inc(s_red, 1)
            dve.wait_ge(s_all, reds[0])

        def pool_max(pool, n):
            pool.wait_ge(s_red, n)
            pool.partition_all_reduce(st(ALL), st(RED), P, RMAX).then_inc(s_all, 1)

        with ExitStack() as c1:
            GB = GRP // SEQ
            h_in = sb("h_in", [P, 2, GB, NC, SEQ], F32, c1)
            xt = sb("xt", [P, 2, GB, NC, SEQ], F32, c1)
            x_hi = sb("x_hi", [P, 2, GB, NC, SEQ], F16, c1)
            x_lo = sb("x_lo", [P, 2, GB, NC, SEQ], F16, c1)
            s_hl = [sem(f"h_loaded_{n}") for n in range(2)]
            MB = NM // 2
            NB = 2 * NM // MB
            stage = sb("stage", [P, NB, MB, GRP], F32, c1)
            raw_max = sb("raw_max", [P, 2 * NM, NG], F32, c1)
            s_xt = sem("h_rounded")
            s_xh = sem("x_hi_ready")
            s_xl = sem("x_lo_ready")
            s_raw = sem("raw_product_done")
            s_copy = sem("raw_product_copied")
            s_rmax = sem("raw_product_maximum_ready")
            s_store = [sem(f"raw_stored_{n}") for n in range(NB)]
            M2 = 2 * NM

            with nc.Block() as block:

                @block.vector
                def _(dve):
                    step(dve, dve.memset(magic[:, :], MAGIC))
                    step(dve, dve.memset(st(REAL), 1.0))
                    global_max(dve, h_max[:, :])
                    quant_scale(dve, S_H, I_H)

                    def split(g, q, par, first):
                        dve.wait_ge(s_hl[par], 16 * (q + 1))
                        if not first:
                            dve.wait_ge(s_raw, (g - 1) * M2)
                        dve.tensor_scalar(xt[:, par, :, :, :], h_in[:, par, :, :, :], st(I_H), MAGIC,
                                          ALU.mult, ALU.add).then_inc(s_xt, 1)
                        dve.wait_ge(s_xt, g + 1)
                        dve.tensor_scalar(x_hi[:, par, :, :, :], xt[:, par, :, :, :], MAGIC, None,
                                          ALU.subtract).then_inc(s_xh, 1)
                        dve.wait_ge(s_xh, g + 1)
                        dve.scalar_tensor_tensor(out=x_lo[:, par, :, :, :].rearrange("p b c t -> p (b c t)"),
                                                 in0=xt[:, par, :, :, :].rearrange("p b c t -> p (b c t)"),
                                                 scalar=MAGIC,
                                                 in1=x_hi[:, par, :, :, :].rearrange("p b c t -> p (b c t)"),
                                                 op0=ALU.subtract, op1=ALU.subtract).then_inc(s_xl, 1)

                    def maxima(g, par, ms):
                        for m in ms:
                            dve.wait_ge(s_copy, g * M2 + (m + 1))
                            dve.tensor_reduce(out=raw_max[:, m, bass.ds(g, 1)], in_=stage[:, m // MB, m % MB, :],
                                              axis=AX.X, op=ALU.max, apply_absolute_value=True).then_inc(s_rmax, 1)

                    def reduce_and_split(g, q, par, first=False):
                        maxima(g, par, range(6))
                        split(g + 1, q + par, 1 - par, first)
                        maxima(g, par, range(6, M2))

                    split(0, 0, 0, True)
                    reduce_and_split(0, 0, 0, True)
                    reduce_and_split(1, 0, 1)
                    with dve.Fori(1, NG // 2 - 1, 1) as q:
                        reduce_and_split(q * 2, q, 0)
                        reduce_and_split(q * 2 + 1, q, 1)
                    reduce_and_split(NG - 2, NG // 2 - 1, 0)
                    maxima(NG - 1, 1, range(M2))
                    dve.wait_ge(s_rmax, NG * M2)
                    step(dve, dve.tensor_scalar(st(REAL), st(S_H), 1.0 / WS, None, ALU.mult))
                    flat = raw_max[:, :, :].rearrange("p m g -> p (m g)")
                    for n, (s_out, c_out) in enumerate(((S_U, C_U), (S_G, C_G))):
                        global_max(dve, flat[:, n * NM * NG:(n + 1) * NM * NG])
                        quant_scale(dve, s_out, c_out)

                @block.gpsimd
                def _(pool):
                    for n in range(3):
                        pool_max(pool, n + 1)

                @block.tensor
                def _(pe):
                    def body(g, par):
                        pe.wait_ge(s_xl, g + 1)
                        for m in range(M2):
                            bank = banks[(M2 * par + m) % 8]
                            if not isinstance(g, int) or g * M2 + m >= 8:
                                pe.wait_ge(s_copy, g * M2 + (m - 7))
                            for c in range(NC):
                                cols = slice(m * P, (m + 1) * P)
                                hi, lo = x_hi[:, par, :, c, :], x_lo[:, par, :, c, :]
                                pe.matmul(bank[:, :], w_gu_t[:, c, 0, cols], hi, start=c == 0, stop=False)
                                pe.matmul(bank[:, :], w_gu_t[:, c, 0, cols], lo, start=False, stop=False)
                                last = pe.matmul(bank[:, :], w_gu_t[:, c, 1, cols], hi, start=False, stop=c == NC - 1)
                            last.then_inc(s_raw, 1)

                    body(0, 0)
                    body(1, 1)
                    with pe.Fori(1, NG // 2, 1) as q:
                        body(q * 2, 0)
                        body(q * 2 + 1, 1)

                @block.scalar
                def _(act):
                    def body(g, par, first):
                        for m in range(M2):
                            q, j = divmod(m, MB)
                            act.wait_ge(s_raw, g * M2 + (m + 1))
                            if j == 0 and not first:
                                act.wait_ge(s_store[q], 16 * g)
                                act.wait_ge(s_rmax, (g - 1) * M2 + MB * (q + 1))
                            act.activation(stage[:, q, j, :], banks[(M2 * par + m) % 8][:, :],
                                           ACT.Copy).then_inc(s_copy, 1)

                    body(0, 0, True)
                    body(1, 1, False)
                    with act.Fori(1, NG // 2, 1) as q:
                        body(q * 2, 0, False)
                        body(q * 2 + 1, 1, False)

                @block.sync
                def _(sp):
                    def load(g, par):
                        sp.dma_start(h_in[:, par, :, :, :], h_d[bass.ds(g * GB, GB)]
                                     .rearrange("b p c t -> p b c t")).then_inc(s_hl[par], 16)

                    def store(g):
                        for q in range(NB):
                            sp.wait_ge(s_copy, g * M2 + MB * (q + 1))
                            m0 = MB * (q % 2)
                            sp.dma_start(raw_d[q // 2, g, m0:m0 + MB].rearrange("m p t -> p m t"), stage[:, q, :, :]).then_inc(s_store[q], 16)

                    load(0, 0)
                    load(1, 1)
                    with sp.Fori(0, NG // 2 - 1, 1) as q:
                        for par in range(2):
                            g = q * 2
                            sp.wait_ge(s_xt, g + (par + 1))
                            load(g + (par + 2), par)
                            store(g + par)
                    store(NG - 2)
                    store(NG - 1)
                    for q in range(NB):
                        sp.wait_ge(s_store[q], 16 * NG)

        mid.close()

        PM = NM // 2
        PIECES = 2 * NG
        W = PM * GRP
        up_d, gate_d = (raw_d[n].rearrange("g (h m) p t -> (g h) p m t", h=2) for n in range(2))
        o_pieces = o_d.rearrange("g (h m) p t -> (g h) p m t", h=2)

        def piece(buf, n):
            return buf[:, n, :].rearrange("p (m t) -> p m t", m=PM)

        for with_up in (False, True):
            tag = "o" if with_up else "gate"
            with ExitStack() as c2:
                g_in = sb(f"{tag}_g_in", [P, 2, W], F32, c2)
                g_t = sb(f"{tag}_g_t", [P, W], F32, c2)
                g_n = sb(f"{tag}_g_n", [P, 2, W], F32, c2)
                sg = sb(f"{tag}_sig", [P, 2, W], F32, c2)
                prod = sb(f"{tag}_prod", [P, 2, W], F32, c2)
                p_max = sb(f"{tag}_p_max", [P, PIECES], F32, c2)
                s_gl = [sem(f"{tag}_gate_loaded_{n}") for n in range(2)]
                s_gt = sem(f"{tag}_gate_plus_magic")
                s_gn = sem(f"{tag}_gate_integer")
                s_sg = sem(f"{tag}_sigmoid")
                s_sa = sem(f"{tag}_sigmoid_rounded")
                s_sq = sem(f"{tag}_sigmoid_integer")
                s_pr = sem(f"{tag}_product")
                s_fin = sem(f"{tag}_piece_reduced")
                s_oo = sem(f"{tag}_output_ready")
                if with_up:
                    u_in = sb("u_in", [P, 2, W], F32, c2)
                    u_t = sb("u_t", [P, W], F32, c2)
                    u_n = sb("u_n", [P, W], F32, c2)
                    o_sb = sb("o_sb", [P, 2, W], F32, c2)
                    s_ul = [sem(f"up_loaded_{n}") for n in range(2)]
                    s_ut = sem("up_plus_magic")
                    s_un = sem("up_integer")
                    s_g2 = sem("gate_requantised")
                    s_ow = [sem(f"o_stored_{n}") for n in range(2)]

                def two(eng, body):
                    for n in range(2):
                        body(n, 0, n)
                    with eng.Fori(1, PIECES // 2, 1) as q:
                        for n in range(2):
                            body(q * 2 + n, q, n)

                with nc.Block() as block:

                    @block.sync
                    def _(sp):
                        def body(j, q, n):
                            if not isinstance(j, int):
                                sp.wait_ge(s_ut if with_up else s_gt, j - 1)
                            sp.dma_start(piece(g_in, n), gate_d[j]).then_inc(s_gl[n], 16)
                            if with_up:
                                sp.dma_start(piece(u_in, n), up_d[j]).then_inc(s_ul[n], 16)

                        two(sp, body)

                    @block.scalar
                    def _(act):
                        def sigmoid(j, n):
                            act.wait_ge(s_gn, j + 1)
                            if not isinstance(j, int) or j >= 2:
                                act.wait_ge(s_pr, j - 1)
                            act.activation(sg[:, n, :], g_n[:, n, :], ACT.Sigmoid, scale=st(S_G)).then_inc(s_sg, 1)

                        def body(j, q, n):
                            act.wait_ge(s_gl[n], 16 * (q + 1))
                            if not (isinstance(j, int) and j == 0):
                                act.wait_ge(s_gn, j)
                            act.activation(g_t[:, :], g_in[:, n, :], ACT.Identity, bias=magic[:, 0:1],
                                           scale=st(C_G)).then_inc(s_gt, 1)
                            if with_up:
                                act.wait_ge(s_ul[n], 16 * (q + 1))
                                if not (isinstance(j, int) and j == 0):
                                    act.wait_ge(s_un, j)
                                act.activation(u_t[:, :], u_in[:, n, :], ACT.Identity, bias=magic[:, 0:1],
                                               scale=st(C_U)).then_inc(s_ut, 1)
                            sigmoid(j, n)
                            if with_up and not (isinstance(j, int) and j == 0):
                                store(j - 1, 1 - n)

                        def store(j, n):
                            act.wait_ge(s_fin, j + 1)
                            act.dma_start(o_pieces[j], piece(o_sb, n)).then_inc(s_ow[n], 16)

                        two(act, body)
                        if with_up:
                            store(PIECES - 1, 1)
                            for n in range(2):
                                act.wait_ge(s_ow[n], 16 * (PIECES // 2))

                    @block.gpsimd
                    def _(pool):
                        def body(j, q, n):
                            pool.wait_ge(s_sq, j + 1)
                            if not isinstance(j, int) or j >= 2:
                                pool.wait_ge(s_fin, j - 1)
                            pool.tensor_tensor(prod[:, n, :], g_n[:, n, :], sg[:, n, :],
                                               ALU.mult).then_inc(s_pr, 1)

                        two(pool, body)
                        pool_max(pool, reds[0] + 1)

                    @block.vector
                    def _(dve):
                        def front(j, q, n):
                            dve.wait_ge(s_gt, j + 1)
                            if not isinstance(j, int) or j >= 2:
                                dve.wait_ge(s_pr, j - 1)
                            dve.tensor_scalar(g_n[:, n, :], g_t[:, :], MAGIC, None, ALU.subtract).then_inc(s_gn, 1)

                        def sig(j, q, n):
                            dve.wait_ge(s_sg, j + 1)
                            dve.tensor_scalar(sg[:, n, :], sg[:, n, :], SIG, MAGIC, ALU.mult, ALU.add)\
                               .then_inc(s_sa, 1)
                            dve.wait_ge(s_sa, j + 1)
                            dve.tensor_scalar(sg[:, n, :], sg[:, n, :], MAGIC, SIG - 1, ALU.subtract, ALU.min)\
                               .then_inc(s_sq, 1)

                        def back(j, q, n):
                            dve.wait_ge(s_pr, j + 1)
                            if not with_up:
                                dve.tensor_reduce(out=p_max[:, bass.ds(j, 1)], in_=prod[:, n, :], axis=AX.X,
                                                  op=ALU.max, apply_absolute_value=True).then_inc(s_fin, 1)
                                return
                            dve.tensor_scalar(prod[:, n, :], prod[:, n, :], st(C_P), MAGIC, ALU.mult, ALU.add)\
                               .then_inc(s_g2, 1)
                            dve.wait_ge(s_g2, j + 1)
                            if not (isinstance(j, int) and j < 2):
                                dve.wait_ge(s_ow[n], 16 * q)
                            dve.wait_ge(s_un, j + 1)
                            dve.scalar_tensor_tensor(out=o_sb[:, n, :], in0=prod[:, n, :], scalar=MAGIC,
                                                     in1=u_n[:, :], op0=ALU.subtract,
                                                     op1=ALU.mult).then_inc(s_oo, 1)
                            dve.wait_ge(s_oo, j + 1)
                            dve.tensor_reduce(out=p_max[:, bass.ds(j, 1)], in_=o_sb[:, n, :], axis=AX.X,
                                              op=ALU.max, apply_absolute_value=True).then_inc(s_fin, 1)

                        def up(j, q, n):
                            if with_up:
                                dve.wait_ge(s_ut, j + 1)
                                dve.tensor_scalar(u_n[:, :], u_t[:, :], MAGIC, None, ALU.subtract)\
                                   .then_inc(s_un, 1)

                        def end_and_start(j, q, n):
                            front(j + 1, q + n, 1 - n)
                            up(j, q, n)
                            back(j, q, n)
                            sig(j + 1, q + n, 1 - n)

                        front(0, 0, 0)
                        sig(0, 0, 0)
                        end_and_start(0, 0, 0)
                        end_and_start(1, 0, 1)
                        with dve.Fori(1, PIECES // 2 - 1, 1) as q:
                            end_and_start(q * 2, q, 0)
                            end_and_start(q * 2 + 1, q, 1)
                        q = PIECES // 2 - 1
                        end_and_start(2 * q, q, 0)
                        up(2 * q + 1, q, 1)
                        back(2 * q + 1, q, 1)
                        dve.wait_ge(s_fin, PIECES)
                        if with_up:
                            step(dve, dve.tensor_tensor(st(REAL), st(S_P), st(S_U), ALU.mult))
                            global_max(dve, p_max[:, :])
                            quant_scale(dve, S_O, C_O)
                            step(dve, dve.tensor_scalar(st(S_O), st(S_O), 1.0 / WS, None, ALU.mult))
                        else:
                            step(dve, dve.tensor_scalar(st(REAL), st(S_G), 1.0 / SIG, None, ALU.mult))
                            global_max(dve, p_max[:, :])
                            quant_scale(dve, S_P, C_P)

        GT = GRP // P
        GB = GRP // SEQ
        with ExitStack() as c3:
            o_in = sb("o_in", [P, 2, NM, GRP], F32, c3)
            o_t = sb("o_t", [P, NM, GRP], F32, c3)
            o_hi = sb("o_hi", [P, 2, NM, GRP], F16, c3)
            o_lo = sb("o_lo", [P, 2, NM, GRP], F16, c3)
            x2_in = sb("x2_in", [P, 2, GB, NT, D], F32, c3)
            y = sb("y", [P, 2, GT, D], F32, c3)
            s_ol = [sem(f"o_loaded_{n}") for n in range(2)]
            s_xl2 = [sem(f"x2_loaded_{n}") for n in range(2)]
            s_ot = sem("o_plus_magic")
            s_oh = sem("o_hi_ready")
            s_olo = sem("o_lo_ready")
            s_down = sem("down_product_done")
            s_y = sem("y_ready")
            s_yw = [sem(f"y_stored_{n}") for n in range(2)]

            def pairs(eng, body):
                for n in range(2):
                    body(n, 0, n, True)
                with eng.Fori(1, NG // 2, 1) as q:
                    for n in range(2):
                        body(q * 2 + n, q, n, False)

            with nc.Block() as block:

                @block.sync
                def _(sp):
                    def body(g, q, n, first):
                        if not first:
                            sp.wait_ge(s_ot, g - 1)
                        sp.dma_start(o_in[:, n, :, :], o_d[g].rearrange("m p t -> p m t")).then_inc(s_ol[n], 16)
                        if not first:
                            sp.wait_ge(s_y, (g - 1) * GT)
                        sp.dma_start(x2_in[:, n, :, :, :], x2_d[bass.ds(g * GB, GB)]
                                     .rearrange("b p t d -> p b t d")).then_inc(s_xl2[n], 16)

                    pairs(sp, body)

                @block.scalar
                def _(act):
                    def body(g, q, n, first):
                        act.wait_ge(s_ol[n], 16 * (q + 1))
                        if not (first and n == 0):
                            act.wait_ge(s_olo, g)
                        act.activation(o_t[:, :, :], o_in[:, n, :, :], ACT.Identity, bias=magic[:, 0:1],
                                       scale=st(C_O)).then_inc(s_ot, 1)
                        if not (first and n == 0):
                            store(g - 1, 1 - n)

                    def store(g, n):
                        act.wait_ge(s_y, (g + 1) * GT)
                        act.dma_start(out_g[bass.ds(g * GT, GT)].rearrange("t p d -> p t d"),
                                      y[:, n, :, :]).then_inc(s_yw[n], 16)

                    pairs(act, body)
                    store(NG - 1, 1)
                    for n in range(2):
                        act.wait_ge(s_yw[n], 16 * (NG // 2))

                @block.vector
                def _(dve):
                    def split(g, q, n, first):
                        dve.wait_ge(s_ot, g + 1)
                        if not first:
                            dve.wait_ge(s_down, (g - 1) * GT)
                        dve.tensor_scalar(o_hi[:, n, :, :], o_t[:, :, :], MAGIC, None,
                                          ALU.subtract).then_inc(s_oh, 1)
                        dve.wait_ge(s_oh, g + 1)
                        dve.scalar_tensor_tensor(out=o_lo[:, n, :, :], in0=o_t[:, :, :], scalar=MAGIC,
                                                 in1=o_hi[:, n, :, :], op0=ALU.subtract,
                                                 op1=ALU.subtract).then_inc(s_olo, 1)

                    def add(g, q, n, first):
                        dve.wait_ge(s_xl2[n], 16 * (q + 1))
                        if not first:
                            dve.wait_ge(s_yw[n], 16 * q)
                        for t in range(GT):
                            dve.wait_ge(s_down, g * GT + (t + 1))
                            dve.scalar_tensor_tensor(out=y[:, n, t, :], in0=banks[GT * n + t][:, 0:D],
                                                     scalar=st(S_O), in1=x2_in[:, n, t // NT, t % NT, :],
                                                     op0=ALU.mult, op1=ALU.add).then_inc(s_y, 1)

                    split(0, 0, 0, True)
                    split(1, 0, 1, True)
                    add(0, 0, 0, True)
                    split(2, 1, 0, False)
                    add(1, 0, 1, True)
                    with dve.Fori(1, NG // 2 - 1, 1) as q:
                        split(q * 2 + 1, q, 1, False)
                        add(q * 2, q, 0, False)
                        split(q * 2 + 2, q + 1, 0, False)
                        add(q * 2 + 1, q, 1, False)
                    split(NG - 1, NG // 2 - 1, 1, False)
                    add(NG - 2, NG // 2 - 1, 0, False)
                    add(NG - 1, NG // 2 - 1, 1, False)

                @block.tensor
                def _(pe):
                    def body(g, q, n, first):
                        pe.wait_ge(s_olo, g + 1)
                        for t in range(GT):
                            if not first:
                                pe.wait_ge(s_y, (g - 2) * GT + (t + 1))
                            bank = banks[GT * n + t][:, 0:D]
                            for m in range(NM):
                                hi = o_hi[:, n, m, t * P:(t + 1) * P]
                                lo = o_lo[:, n, m, t * P:(t + 1) * P]
                                pe.matmul(bank, hi, w_down_t[:, m, 0, :], start=m == 0, stop=False)
                                pe.matmul(bank, lo, w_down_t[:, m, 0, :], start=False, stop=False)
                                last = pe.matmul(bank, hi, w_down_t[:, m, 1, :], start=False, stop=m == NM - 1)
                            last.then_inc(s_down, 1)

                    pairs(pe, body)


_SELF = ["L0_attn_Wq", "L0_attn_Wk", "L0_attn_Wv", "L0_attn_Wo"]
_SELF_B = ["L0_attn_bq", "L0_attn_bk", "L0_attn_bv", "L0_attn_bo"]
_CROSS = ["L0_xattn_Wq", "L0_xattn_Wk", "L0_xattn_Wv", "L0_xattn_Wo"]
_CROSS_B = ["L0_xattn_bq", "L0_xattn_bk", "L0_xattn_bv", "L0_xattn_bo"]
_FFN = ["L0_ffn_w_gate", "L0_ffn_w_up", "L0_ffn_w_down"]


def kernel(**inputs):
    import numpy as _np
    import concourse.bacc as _bacc
    from concourse import mybir as _mybir
    from concourse.bass_utils import run_bass_kernel_spmd as _run

    nc = _bacc.Bacc("TRN2", target_bir_lowering=False, num_devices=1)
    arrays, aps = {}, {}
    for name in ["x", "ctx_1024", "mask_1x1xSxS2_fk1"] + _SELF + _SELF_B + _CROSS + _CROSS_B + _FFN:
        a = _np.ascontiguousarray(inputs[name])
        arrays[f"in_{name}_dram"] = a
        aps[name] = nc.dram_tensor(f"in_{name}_dram", a.shape, _mybir.dt.from_np(a.dtype), kind="ExternalInput").ap()
    out = nc.dram_tensor("out_0_dram", (BATCH, SEQ, D), _mybir.dt.float32, kind="ExternalOutput").ap()
    decoder_kernel(nc, aps["x"], aps["ctx_1024"], aps["mask_1x1xSxS2_fk1"],
                   [aps[n] for n in _SELF], [aps[n] for n in _SELF_B],
                   [aps[n] for n in _CROSS], [aps[n] for n in _CROSS_B],
                   *[aps[n] for n in _FFN], out)
    r = _run(nc, [arrays], core_ids=[0])
    return r.results[0]["out_0_dram"]
```

```python
from contextlib import ExitStack

import concourse.bass as bass
from concourse import mybir

F32 = mybir.dt.float32
F16 = mybir.dt.float16
BF16 = mybir.dt.bfloat16
ALU = mybir.AluOpType
ACT = mybir.ActivationFunctionType
AX = mybir.AxisListType
RMAX = bass.bass_isa.ReduceOp.max

P = 128
BATCH, SEQ, D = 32, 256, 256
HEADS = 16
HD = D // HEADS
NC = D // P
NT = SEQ // P
HU = 4
GROUPS = HEADS // HU
HALF = HU * HD
UNITS = NT * HEADS // HU
WIN = 64
NWIN = SEQ // WIN
CTX = 120
FF = 768
NM = FF // P
QBLOCK = 32
TOK = BATCH * SEQ
GRP = 512
NG = TOK // GRP
EPS = 1e-5

XN = 256.0
WS = 256.0
QK = 8.0
VS = 64.0
LOGIT = 1.0 / (QK * QK * HD ** 0.5)
SHIFT = 10.0
NEG = -1e30
MASK_SCALE = -1e9
MAGIC = 1.5 * 2.0 ** 23
QMAX = 32767.0
TINY = 1e-12
SIG = 65536.0

LOAD, PREP, SELF, MID, CROSS, END = 2, 1, 0, -1, -2, -3
JOBS = [["P1", "X1"], ["P3"], ["P2"], ["B1", "D1"], ["X2", "B2"], ["D2"], ["P4", "B3"], ["B4", "D3"]]
ORDER = [j for slot in JOBS for j in slot]
STAGE = {"P": PREP, "B": MID, "X": MID, "D": END}
BLOCKS_FROM = 3
FIRST_IT, LAST_IT = -LOAD, BATCH - 1 - END
LOOP_FROM, LOOP_TO = 4, BATCH - LOAD


class Iteration:

    def __init__(self, pair, parity):
        self.pair, self.parity = pair, parity
        self.i, self.fixed = pair * 2 + parity, isinstance(pair, int)

    def has(self, off):
        return not self.fixed or 0 <= self.i + off < BATCH

    def batch(self, off):
        return self.i + off

    def par(self, off):
        return (self.parity + off) % 2

    def nth(self, off):
        return self.pair + (self.parity + off) // 2


def pipeline(eng, body):
    for i in range(FIRST_IT, LOOP_FROM):
        body(Iteration(i // 2, i % 2))
    with eng.Fori(LOOP_FROM // 2, LOOP_TO // 2, 1) as pair:
        body(Iteration(pair, 0))
        body(Iteration(pair, 1))
    for i in range(LOOP_TO, LAST_IT + 1):
        body(Iteration(i // 2, i % 2))


def lag(stage, k, d):
    return (stage, k - d) if k >= d else (stage - 1, k - d + UNITS)


BANK_JOBS = [["P1", "P3", "B1", "X2", "D2", "B3", "D3"], ["X1", "P2", "D1", "B2", "P4", "B4"]]


def job_before(it, job):
    jobs = BANK_JOBS[0] if job in BANK_JOBS[0] else BANK_JOBS[1]
    n = jobs.index(job)
    for back in range(1, 8 * len(jobs)):
        name = jobs[(n - back) % len(jobs)]
        stage = STAGE[name[0]] + (n - back) // len(jobs)
        if it.has(stage):
            return name, stage
    return None


def decoder_kernel(nc, x, ctx_in, mask, w_self, b_self, w_cross, b_cross, w_gate, w_up, w_down, out):
    x_d = x.rearrange("b (t p) d -> b p t d", p=P)
    out_g = out.rearrange("b (t p) d -> (b t) p d", p=P)
    x1_d = nc.dram_tensor("x1_scratch", [BATCH, P, NT, D], F32, kind="Internal").ap()
    x2_d = nc.dram_tensor("x2_scratch", [BATCH, P, NT, D], F32, kind="Internal").ap()
    h_d = nc.dram_tensor("h_scratch", [BATCH, P, NC, SEQ], F32, kind="Internal").ap()
    raw_d = nc.dram_tensor("raw_scratch", [2, NG, NM, P, GRP], F32, kind="Internal").ap()
    o_d = nc.dram_tensor("o_scratch", [NG, NM, P, GRP], F32, kind="Internal").ap()

    top = ExitStack()
    with top:
        def sb(name, shape, dt=F32, ctx=top):
            return ctx.enter_context(nc.sbuf_tensor(name, shape, dt))

        def sem(name):
            return top.enter_context(nc.semaphore(name))

        banks = [top.enter_context(nc.psum_tensor(f"bank{n}", [P, 512], F32)) for n in range(8)]

        ident = sb("ident", [P, P])
        w_down_t = sb("w_down_t", [P, NM, 2, D], F16)
        stats = sb("stats", [P, 24])
        magic = sb("magic", [P, 1])
        S_H, I_H, S_U, C_U, S_G, C_G, S_P, C_P, S_O, C_O, RED, ALL, REAL = range(13)

        def st(n):
            return stats[:, n:n + 1]

        mid = top.enter_context(ExitStack())
        w_gu_t = sb("w_gu_t", [P, NC, 2, 2 * FF], F16, mid)
        h_max = sb("h_max", [P, BATCH], F32, mid)

        att = top.enter_context(ExitStack())
        names = ["self_q", "self_k", "self_v", "self_o", "cross_q", "cross_k", "cross_v", "cross_o"]
        SQ, SK, SV, SO, CQ, CK, CV, CO = range(8)
        w16 = sb("w16", [P, 8, NC, 2, D], F16, att)
        bias16 = sb("bias16", [64, 8, D], F16, att)
        ones16 = sb("ones16", [64, 2, SEQ], F16, att)
        ident_b = sb("ident_b", [P, P], BF16, att)
        mask_b = sb("mask_b", [P, NT, P], BF16, att)
        mask_c = sb("mask_c", [P, NT, CTX], F32, att)
        k_blk = sb("k_blk", [P, 2, GROUPS, HU, WIN + SEQ], F16, att)
        k2_blk = sb("k2_blk", [P, 2, GROUPS, HU, CTX], F16, att)
        head_rows = sb("head_rows", [P, HU], F32, att)
        heads16 = sb("heads16", [P, 2 * HU], F32, att)
        half = sb("half", [P, NT], F32, att)
        s_wload = sem("weights_loaded")
        s_pool = sem("pool_chain")
        s_const = sem("constants_ready")
        s_dve = sem("dve_chain")
        s_wq = sem("ffn_weight_dequantised")
        s_wt = sem("ffn_weight_transposed")
        s_we = sem("ffn_weight_evacuated")

        with ExitStack() as c0:
            w_raw = sb("w_raw", [P, 8, NC, D], F32, c0)
            b_raw = sb("b_raw", [64, 8, D], F32, c0)
            f_raw = sb("f_raw", [P, 3, 2 * FF], F32, c0)
            f_amax = sb("f_amax", [P, 3, 48], F32, c0)
            f_rec = sb("f_rec", [P, 3, 48], F32, c0)
            tmp_b = sb("tmp_b", [P, P], BF16, c0)
            block = c0.enter_context(nc.Block())

            @block.sync
            def _(sp):
                for n, w in enumerate(w_self + w_cross):
                    sp.dma_start(w_raw[:, n, :, :], w.rearrange("(c p) n -> p c n", p=P)).then_inc(s_wload, 16)
                for n, b in enumerate(b_self + b_cross):
                    row = b.rearrange("(a n) -> a n", a=1)
                    sp.dma_start(b_raw[0:1, n, :], row).then_inc(s_wload, 16)
                    sp.dma_start(b_raw[32:33, n, :], row).then_inc(s_wload, 16)
                for n, w in enumerate((w_up, w_gate)):
                    sp.dma_start(f_raw[:, n, :].rearrange("p (m k) -> p m k", m=NM),
                                 w.rearrange("(m p) k -> p m k", p=P)).then_inc(s_wload, 16)
                sp.dma_start(f_raw[:, 2, :].rearrange("p (r k) -> p r k", r=NC),
                             w_down.rearrange("(r p) k -> p r k", p=P)).then_inc(s_wload, 16)
                sp.dma_start(mask_c[:, :, :],
                             mask.rearrange("a b (t p) k -> p (a b t) k", p=P)).then_inc(s_wload, 16)

            LOADED = 16 * (8 + 16 + 3 + 1)

            @block.gpsimd
            def _(pool):
                n = [0]

                def step(ins):
                    n[0] += 1
                    ins.then_inc(s_pool, 1)
                    pool.wait_ge(s_pool, n[0])

                step(pool.memset(ident[:, :], 0.0))
                step(pool.affine_select(out=ident[:, :], in_=ident[:, :], compare_op=ALU.not_equal, fill=1.0,
                                        base=0, pattern=[[-1, P]], channel_multiplier=1))
                step(pool.tensor_copy(ident_b[:, :], ident[:, :]))
                step(pool.memset(half[:, :], -0.5))
                step(pool.memset(heads16[:, :], 1.0))
                step(pool.affine_select(out=heads16[:, :], in_=heads16[:, :], compare_op=ALU.is_ge, fill=0.0,
                                        base=0, pattern=[[-HD, 2 * HU]], channel_multiplier=1))
                step(pool.affine_select(out=heads16[:, :], in_=heads16[:, :], compare_op=ALU.is_gt, fill=0.0,
                                        base=HD, pattern=[[HD, 2 * HU]], channel_multiplier=-1))
                step(pool.tensor_tensor(head_rows[:, :], heads16[:, 0:HU], heads16[:, HU:2 * HU], ALU.add))
                for m, base in ((mask_b[:, 0, :], 0), (tmp_b[:, :], WIN)):
                    step(pool.memset(m, 0.0))
                    step(pool.affine_select(out=m, in_=m, compare_op=ALU.is_gt, fill=NEG,
                                            base=base, pattern=[[1, P]], channel_multiplier=-1))
                    step(pool.affine_select(out=m, in_=m, compare_op=ALU.is_ge, fill=NEG,
                                            base=WIN - base, pattern=[[-1, P]], channel_multiplier=1))
                step(pool.tensor_copy(mask_b[64:128, 0, :], tmp_b[64:128, :]))
                step(pool.tensor_copy(mask_b[:, 1, :], mask_b[:, 0, :]))
                pool.memset(mask_b[0:64, 0, 0:WIN], NEG).then_inc(s_const, 1)
                step(pool.memset(k_blk[:, :, :, :, 0:WIN].rearrange("p a g h n -> p (a g h) n"), 0.0))

            @block.vector
            def _(dve):
                n = [0]

                def step(ins):
                    n[0] += 1
                    ins.then_inc(s_dve, 1)
                    dve.wait_ge(s_dve, n[0])

                step(dve.memset(bias16[:, :, :], 0.0))
                step(dve.memset(ones16[:, 0, :], XN))
                step(dve.memset(ones16[:, 1, :], VS))
                dve.wait_ge(s_wload, LOADED)
                step(dve.tensor_scalar(mask_c[:, :, :], mask_c[:, :, :], MASK_SCALE, None, ALU.mult))
                for hl in range(2):
                    row = slice(32 * hl, 32 * hl + 1)
                    step(dve.tensor_scalar(bias16[row, :, :], b_raw[row, :, :], WS, None, ALU.mult))
                lo = slice(32, 33)
                step(dve.scalar_tensor_tensor(out=bias16[lo, :, :], in0=b_raw[lo, :, :], scalar=WS,
                                              in1=bias16[lo, :, :], op0=ALU.mult, op1=ALU.subtract))
                for k in range(8):
                    step(dve.tensor_scalar(w16[:, k, :, 0, :], w_raw[:, k, :, :], WS, None, ALU.mult))
                    step(dve.scalar_tensor_tensor(out=w16[:, k, :, 1, :], in0=w_raw[:, k, :, :], scalar=WS,
                                                  in1=w16[:, k, :, 0, :], op0=ALU.mult, op1=ALU.subtract))
                blocks = f_raw[:, :, :].rearrange("p a (n k) -> p (a n) k", k=QBLOCK)
                amax = f_amax[:, :, :].rearrange("p a n -> p (a n)")
                rec = f_rec[:, :, :].rearrange("p a n -> p (a n)")
                wide = [P, 3 * 48, QBLOCK]
                step(dve.tensor_reduce(out=amax, in_=blocks, axis=AX.X, op=ALU.max, apply_absolute_value=True))
                step(dve.tensor_scalar(amax, amax, 1.0 / 7.0, TINY, ALU.mult, ALU.max))
                step(dve.reciprocal(rec, amax))
                step(dve.tensor_tensor(blocks, blocks, rec.unsqueeze(2).to_broadcast(wide), ALU.mult))
                step(dve.tensor_scalar(f_raw[:, :, :], f_raw[:, :, :], MAGIC, MAGIC, ALU.add, ALU.subtract))
                dve.tensor_tensor(blocks, blocks, amax.unsqueeze(2).to_broadcast(wide), ALU.mult).then_inc(s_wq, 1)
                for q in range(9):
                    dve.wait_ge(s_wt, q + 1)
                    bank = banks[q % 8]
                    if q < 6:
                        a, m0 = q // 3, 2 * (q % 3)
                        for hl in range(2):
                            dst = w_gu_t[:, :, hl, a * FF + m0 * P:a * FF + (m0 + 2) * P]
                            src = bank[:, :].rearrange("p (c k) -> p c k", c=NC)
                            hi = w_gu_t[:, :, 0, a * FF + m0 * P:a * FF + (m0 + 2) * P]
                            if hl == 0:
                                step(dve.tensor_scalar(dst, src, WS, None, ALU.mult))
                            else:
                                step(dve.scalar_tensor_tensor(out=dst, in0=src, scalar=WS, in1=hi,
                                                              op0=ALU.mult, op1=ALU.subtract))
                    else:
                        m0 = 2 * (q - 6)
                        src = bank[:, :].rearrange("p (m k) -> p m k", m=2)
                        hi, low = w_down_t[:, m0:m0 + 2, 0, :], w_down_t[:, m0:m0 + 2, 1, :]
                        step(dve.tensor_scalar(hi, src, WS, None, ALU.mult))
                        step(dve.scalar_tensor_tensor(out=low, in0=src, scalar=WS, in1=hi,
                                                      op0=ALU.mult, op1=ALU.subtract))
                    dve.sem_inc(s_we, 1)

            @block.tensor
            def _(pe):
                pe.wait_ge(s_const, 1)
                pe.wait_ge(s_wq, 1)
                for q in range(9):
                    if q >= 8:
                        pe.wait_ge(s_we, q - 7)
                    for j in range(4):
                        if q < 6:
                            a, m, c = q // 3, 2 * (q % 3) + j % 2, j // 2
                            src = f_raw[:, a, m * D + c * P:m * D + (c + 1) * P]
                        else:
                            m, r = 2 * (q - 6) + j // 2, j % 2
                            src = f_raw[:, 2, r * FF + m * P:r * FF + (m + 1) * P]
                        last = pe.transpose(banks[q % 8][:, j * P:(j + 1) * P], src, ident[:, :])
                    last.then_inc(s_wt, 1)

        a = att
        x_in = sb("x_in", [P, 2, NT, D], F32, a)
        xn = sb("xn", [P, NT, D], F32, a)
        xn_t = sb("xn_t", [P, NC, 2, SEQ], F16, a)
        q_hi = sb("q_hi", [P, NC, SEQ], F16, a)
        q_lo = sb("q_lo", [P, 2, NC, SEQ], F16, a)
        q_dup = sb("q_dup", [P, 2, GROUPS, SEQ], F16, a)
        k_t = sb("k_t", [P, NC, 2, SEQ], F16, a)
        k_both = sb("k_both", [P, GROUPS, SEQ], F16, a)
        k2_both = sb("k2_both", [P, GROUPS, CTX], F16, a)
        v = sb("v", [P, 2, 2, NT, HEADS, 2 * HD + 1], F16, a)
        x_mid = sb("x_mid", [P, NT, D], F32, a)
        x1 = sb("x1", [P, NT, D], F32, a)
        xn2 = sb("xn2", [P, NT, D], F32, a)
        xn2_t = sb("xn2_t", [P, NC, 2, SEQ], F16, a)
        q2_hi = sb("q2_hi", [P, NC, SEQ], F16, a)
        q2_lo = sb("q2_lo", [P, 2, NC, SEQ], F16, a)
        q2_dup = sb("q2_dup", [P, 2, GROUPS, SEQ], F16, a)
        ctx_sb = sb("ctx_sb", [CTX, D], F32, a)
        ctx_t = sb("ctx_t", [P, NC, 2, CTX], F16, a)
        k2_t = sb("k2_t", [P, NC, 2, CTX], F16, a)
        v2_hi = sb("v2_hi", [CTX, 2, HEADS, HD + 1], F16, a)
        v2_lo = sb("v2_lo", [CTX, 2, HEADS, HD], F16, a)
        x1_back = sb("x1_back", [P, NT, D], F32, a)
        x2 = sb("x2", [P, NT, D], F32, a)
        h = sb("h", [P, NT, D], F32, a)
        h_t = sb("h_t", [P, NC, SEQ], F32, a)

        class Attention:

            def __init__(self, name, stage, keys, s_bank, t_bank, o_bank):
                self.stage, self.keys, self.cols = stage, keys, HU * keys
                self.s_bank, self.t_bank, self.o_bank = banks[s_bank], banks[t_bank], banks[o_bank]
                self.u = sb(f"{name}_u", [P, 2, HU * keys], F32, a)
                self.p32 = sb(f"{name}_p32", [P, 2, HU * P], F32, a)
                self.p_hi = sb(f"{name}_p_hi", [P, 4, HU * P], F16, a)
                self.p_lo = sb(f"{name}_p_lo", [P, 4, HU * P], F16, a)
                self.mx = sb(f"{name}_mx", [P, 2, HU], F32, a)
                self.mshift = sb(f"{name}_mshift", [P, 2, HU], F32, a)
                self.den = sb(f"{name}_den", [P, HEADS], F32, a)
                self.o = sb(f"{name}_o", [P, NT, D], F32, a)
                self.o_t = sb(f"{name}_o_t", [P, NC, 2, SEQ], F16, a)
                self.s_scores = sem(f"{name}_scores_done")
                self.s_max = sem(f"{name}_max_done")
                self.s_shift = sem(f"{name}_shift_done")
                self.s_u = sem(f"{name}_u_ready")
                self.s_t = sem(f"{name}_transposed")
                self.s_p32 = sem(f"{name}_p32_ready")
                self.s_hi = sem(f"{name}_p_hi_ready")
                self.s_lo = sem(f"{name}_p_lo_ready")
                self.s_pv = sem(f"{name}_pv_done")
                self.s_den = sem(f"{name}_den_ready")
                self.s_o = sem(f"{name}_o_ready")

        A = Attention("self", SELF, P, 0, 2, 4)
        C = Attention("cross", CROSS, CTX, 1, 3, 5)
        C.y = sb("cross_y", [P, 2, HU * CTX], F32, a)
        C.s_y = sem("cross_y_ready")
        job_bank = {j: banks[6 + n] for n in range(2) for j in BANK_JOBS[n]}
        s_job = {j: sem(f"job_{j}_products_done") for j in ORDER}
        s_hi = {j: sem(f"job_{j}_high_part_ready") for j in ORDER if j not in ("B2", "D2")}
        s_got = {j: sem(f"job_{j}_evacuated") for j in ORDER}

        class Norm:

            def __init__(self, name):
                self.part = sb(f"{name}_bn_part", [P, NT, 6], F32, a)
                self.mv = sb(f"{name}_mean_var", [P, NT, 2], F32, a)
                self.ve = sb(f"{name}_var_eps", [P, NT], F32, a)
                self.rstd = sb(f"{name}_rstd", [P, NT], F32, a)
                self.s_part = sem(f"{name}_bn_part_ready")
                self.s_seen = sem(f"{name}_bn_parts_complete")
                self.s_mv = sem(f"{name}_mean_var_ready")
                self.s_ve = sem(f"{name}_var_eps_ready")
                self.s_rstd = sem(f"{name}_rstd_ready")
                self.s_done = sem(f"{name}_normalised")

        LN1, LN2, LN3 = Norm("ln1"), Norm("ln2"), Norm("ln3")
        s_x = [sem(f"x_loaded_{n}") for n in range(2)]
        s_xm = sem("x_mid_loaded")
        s_ctx = sem("ctx_loaded")
        s_x1b = sem("x1_reloaded")
        s_x1w = sem("x1_stored")
        s_x2w = sem("x2_stored")
        s_hw = sem("h_stored")
        s_init = sem("attention_buffers_cleared")
        s_kblk = sem("k_block_diagonal_ready")
        s_k2blk = sem("k2_block_diagonal_ready")
        s_kboth = sem("k_parts_by_group")
        s_k2both = sem("k2_parts_by_group")
        s_qdup = sem("q_duplicated")
        s_q2dup = sem("q2_duplicated")
        s_vwin = sem("v_windows_ready")
        s_hmax = sem("h_max_ready")

        BLK, DUP, VCOPY = HU, 16 * 4, 16 * 2

        def unit(b, k):
            return b * UNITS + (k + 1)

        with nc.Block() as block:

            @block.sync
            def _(sp):
                def duplicate(dst, src, done):
                    for half_of_chunk in range(2):
                        rows = slice(HALF * half_of_chunk, HALF * (half_of_chunk + 1))
                        for side in range(2):
                            sp.dma_start(dst[HALF * side:HALF * (side + 1), half_of_chunk::2, :],
                                         src[rows, :, :]).then_inc(done, 16)

                def both_parts(dst, src, done):
                    for half_of_chunk in range(2):
                        rows = slice(HALF * half_of_chunk, HALF * (half_of_chunk + 1))
                        for part in range(2):
                            side = half_of_chunk if part == 0 else 1 - half_of_chunk
                            sp.dma_start(dst[HALF * side:HALF * (side + 1), half_of_chunk::2, :],
                                         src[rows, :, part, :]).then_inc(done, 16)

                def body(it):
                    if it.has(LOAD):
                        b = it.batch(LOAD)
                        if it.has(LOAD - 2):
                            sp.wait_ge(LN1.s_done, it.batch(LOAD - 2) + 1)
                        sp.dma_start(x_in[:, it.par(LOAD), :, :], x_d[b]).then_inc(s_x[it.par(LOAD)], 16)
                    if it.has(SELF):
                        b = it.batch(SELF)
                        if it.has(SELF - 1):
                            sp.wait_ge(s_job["X1"], it.batch(SELF - 1) + 1)
                        sp.dma_start(ctx_sb[:, :], ctx_in[b]).then_inc(s_ctx, 16)
                    if it.has(MID):
                        b = it.batch(MID)
                        if it.has(MID - 1):
                            sp.wait_ge(s_got["B2"], it.batch(MID - 1) + 1)
                        sp.dma_start(x_mid[:, :, :], x_d[b]).then_inc(s_xm, 16)
                    if it.has(END):
                        b = it.batch(END)
                        sp.wait_ge(s_x1w, 16 * (b + 1))
                        sp.dma_start(x1_back[:, :, :], x1_d[b]).then_inc(s_x1b, 16)
                    if it.has(PREP):
                        b = it.batch(PREP)
                        if it.has(PREP - 1):
                            sp.wait_ge(s_kblk, BLK * b)
                        sp.wait_ge(s_got["P3"], b + 1)
                        both_parts(k_both, k_t, s_kboth)
                    if it.has(MID):
                        b = it.batch(MID)
                        if it.has(MID - 1):
                            sp.wait_ge(s_k2blk, BLK * b)
                        sp.wait_ge(s_got["X2"], b + 1)
                        both_parts(k2_both, k2_t, s_k2both)
                    if it.has(PREP):
                        b, par = it.batch(PREP), it.par(PREP)
                        if it.has(PREP - 2):
                            sp.wait_ge(A.s_scores, unit(b - 2, UNITS - 1))
                        sp.wait_ge(s_hi["P2"], b + 1)
                        duplicate(q_dup[:, par], q_hi, s_qdup)
                    if it.has(MID):
                        b, par = it.batch(MID), it.par(MID)
                        sp.wait_ge(s_got["B2"], b + 1)
                        sp.dma_start(x1_d[b], x1[:, :, :]).then_inc(s_x1w, 16)
                    if it.has(END):
                        b = it.batch(END)
                        sp.wait_ge(s_got["D2"], b + 1)
                        sp.dma_start(x2_d[b], x2[:, :, :]).then_inc(s_x2w, 16)
                    if it.has(PREP):
                        b, par = it.batch(PREP), it.par(PREP)
                        sp.wait_ge(s_got["P4"], b + 1)
                        sp.dma_start(v[0:WIN, par, 1, 1, :, :], v[WIN:P, par, 0, 0, :, :]).then_inc(s_vwin, 16)
                        sp.dma_start(v[WIN:P, par, 1, :, :, :], v[0:WIN, par, 0, :, :, :]).then_inc(s_vwin, 16)
                    if it.has(END):
                        b = it.batch(END)
                        sp.wait_ge(s_hi["D3"], b + 1)
                        sp.dma_start(h_d[b], h_t[:, :, :]).then_inc(s_hw, 16)

                pipeline(sp, body)
                sp.wait_ge(s_x1w, 16 * BATCH)
                sp.wait_ge(s_x2w, 16 * BATCH)
                sp.wait_ge(s_hw, 16 * BATCH)

            @block.tensor
            def _(pe):
                def product(dst, lhs, rhs, first=True, last=True):
                    pe.matmul(dst, lhs[0], rhs[0], start=first, stop=False)
                    pe.matmul(dst, lhs[1], rhs[0], start=False, stop=False)
                    return pe.matmul(dst, lhs[0], rhs[1], start=False, stop=last)

                def parts(t):
                    return t(0), t(1)

                def project(dst, w, lhs_is_weight, act, cols, ones):
                    for c in range(NC):
                        wt = parts(lambda hl: w16[:, w, c, hl, cols])
                        at = parts(lambda hl: act(c, hl))
                        product(dst, wt if lhs_is_weight else at, at if lhs_is_weight else wt,
                                first=c == 0, last=False)
                    b, o = bias16[:, w, cols], ones
                    return pe.matmul(dst, b if lhs_is_weight else o, o if lhs_is_weight else b,
                                     start=False, stop=True)

                def logits(dst, dup, low, keys, g, first):
                    c, side = divmod(g, 2)
                    rows = slice(HALF * side, HALF * (side + 1))
                    pe.matmul(dst, dup, keys[:, g, :, :], start=first, stop=False)
                    return pe.matmul(dst, low[rows, c, :], keys[rows, g, :, :], start=False, stop=True)

                def scores_self(it, k):
                    b, par = it.batch(SELF), it.par(SELF)
                    t, g = divmod(k, GROUPS)
                    if k == 0:
                        pe.wait_ge(s_got["P2"], b + 1)
                        pe.wait_ge(s_qdup, DUP * (b + 1))
                        pe.wait_ge(s_kblk, BLK * (b + 1))
                    if k or it.has(SELF - 1):
                        pe.wait_ge(A.s_u, unit(b, k - 1))
                    pe.matmul(A.s_bank[:, :], ident_b[:, :],
                              mask_b[:, t, :].unsqueeze(1).to_broadcast([P, HU, P]), start=True, stop=False)
                    for j in range(2):
                        w = 2 * t + j
                        tok = slice(t * P + WIN * j, t * P + WIN * (j + 1))
                        last = logits(A.s_bank[WIN * j:WIN * (j + 1), :], q_dup[:, par, g, tok],
                                      q_lo[:, par, :, tok], k_blk[:, par, :, :, WIN * w:WIN * w + P], g, False)
                    last.then_inc(A.s_scores, 1)

                def scores_cross(it, k):
                    b, par = it.batch(CROSS), it.par(CROSS)
                    t, g = divmod(k, GROUPS)
                    if k == 0:
                        pe.wait_ge(s_got["B4"], b + 1)
                        pe.wait_ge(s_q2dup, 4 * (b + 1))
                        pe.wait_ge(s_k2blk, BLK * (b + 1))
                    if k or it.has(CROSS - 1):
                        pe.wait_ge(C.s_y, unit(b, k - 1))
                    tok = slice(t * P, (t + 1) * P)
                    logits(C.s_bank[:, 0:HU * CTX], q2_dup[:, par, g, tok], q2_lo[:, par, :, tok],
                           k2_blk[:, par, :, :, :], g, True).then_inc(C.s_scores, 1)

                def transposes(att_, it, k):
                    off, kk = lag(att_.stage, k, 1)
                    if not it.has(off):
                        return
                    b = it.batch(off)
                    pe.wait_ge(att_.s_u, unit(b, kk))
                    if kk or it.has(off - 1):
                        pe.wait_ge(att_.s_hi, unit(b, kk - 1))
                        pe.wait_ge(att_.s_p32, unit(b, kk - 1))
                    n = att_.keys
                    for q in range(HU):
                        last = pe.transpose(att_.t_bank[0:n, q * P:(q + 1) * P],
                                            att_.u[:, kk % 2, q * n:(q + 1) * n], ident[:, :])
                    last.then_inc(att_.s_t, 1)

                def weighted_values(att_, it, k):
                    off, kk = lag(att_.stage, k, 3)
                    if not it.has(off):
                        return
                    b, par = it.batch(off), it.par(off)
                    t, g = divmod(kk, GROUPS)
                    if att_ is A and kk == 0:
                        pe.wait_ge(s_vwin, VCOPY * (b + 1))
                    pe.wait_ge(att_.s_hi, unit(b, kk))
                    pe.wait_ge(att_.s_lo, unit(b, kk))
                    if g == 0 and (t or it.has(off - 1)):
                        pe.wait_ge(att_.s_o, b * NT + t)
                    for q in range(HU):
                        hd = HU * g + q
                        for j in range(2 if att_ is A else 1):
                            rows = slice(WIN * j, WIN * (j + 1)) if att_ is A else slice(0, P)
                            cols = slice(q * P + rows.start, q * P + rows.stop)
                            if att_ is A:
                                vw = v[:, par, 1 - j, t, hd, :]
                                vh, vl = vw[:, 0:HD + 1], vw[:, HD + 1:]
                            else:
                                vh, vl = v2_hi[:, par, hd, :], v2_lo[:, par, hd, :]
                            hi = att_.p_hi[0:att_.keys, kk % 4, cols]
                            lo = att_.p_lo[0:att_.keys, kk % 4, cols]
                            dst = att_.o_bank[rows, hd * (HD + 1):(hd + 1) * (HD + 1)]
                            pe.matmul(dst, hi, vh, start=True, stop=False)
                            pe.matmul(dst[:, 0:HD], hi, vl, start=False, stop=False)
                            last = pe.matmul(dst, lo, vh, start=False, stop=True)
                    last.then_inc(att_.s_pv, 1)

                def transpose_tiles(bank, src):
                    for c in range(NC):
                        for t in range(NT):
                            last = pe.transpose(bank[:, c * SEQ + t * P:c * SEQ + (t + 1) * P],
                                                src[:, t, c * P:(c + 1) * P], ident[:, :])
                    return last

                def job(it, name):
                    off = STAGE[name[0]]
                    if not it.has(off):
                        return
                    b = it.batch(off)
                    bank = job_bank[name]
                    before = job_before(it, name)
                    if before:
                        pe.wait_ge(s_got[before[0]], it.batch(before[1]) + 1)
                    if name == "P1":
                        pe.wait_ge(LN1.s_done, b + 1)
                        last = transpose_tiles(bank, xn)
                    elif name in ("P2", "P3"):
                        if name == "P2":
                            pe.wait_ge(s_got["P1"], b + 1)
                        for m in range(NC):
                            last = project(bank[:, m * SEQ:(m + 1) * SEQ], SQ if name == "P2" else SK, True,
                                           lambda c, hl: xn_t[:, c, hl, :],
                                           slice(m * P, (m + 1) * P), ones16[:, 0, :])
                    elif name == "P4":
                        for t in range(NT):
                            last = project(bank[:, t * D:(t + 1) * D], SV, False,
                                           lambda c, hl: xn_t[:, c, hl, t * P:(t + 1) * P],
                                           slice(0, D), ones16[:, 0, 0:P])
                    elif name in ("B1", "D1"):
                        att_ = A if name == "B1" else C
                        pe.wait_ge(att_.s_o, NT * (b + 1))
                        last = transpose_tiles(bank, att_.o)
                    elif name in ("B2", "D2"):
                        att_ = A if name == "B2" else C
                        pe.wait_ge(s_got[name[0] + "1"], b + 1)
                        for t in range(NT):
                            last = project(bank[:, t * D:(t + 1) * D], SO if name == "B2" else CO, False,
                                           lambda c, hl: att_.o_t[:, c, hl, t * P:(t + 1) * P],
                                           slice(0, D), ones16[:, 1, 0:P])
                    elif name == "B3":
                        pe.wait_ge(LN2.s_done, b + 1)
                        last = transpose_tiles(bank, xn2)
                    elif name == "B4":
                        pe.wait_ge(s_got["B3"], b + 1)
                        for m in range(NC):
                            last = project(bank[:, m * SEQ:(m + 1) * SEQ], CQ, True,
                                           lambda c, hl: xn2_t[:, c, hl, :],
                                           slice(m * P, (m + 1) * P), ones16[:, 0, :])
                    elif name == "X1":
                        pe.wait_ge(s_ctx, 16 * (b + 1))
                        for c in range(NC):
                            last = pe.transpose(bank[:, c * CTX:(c + 1) * CTX], ctx_sb[:, c * P:(c + 1) * P],
                                                ident[0:CTX, 0:CTX])
                    elif name == "X2":
                        pe.wait_ge(s_got["X1"], b + 1)
                        for m in range(NC):
                            project(bank[:, m * CTX:(m + 1) * CTX], CK, True, lambda c, hl: ctx_t[:, c, hl, :],
                                    slice(m * P, (m + 1) * P), ones16[:, 1, 0:CTX])
                        last = project(bank[0:CTX, NC * CTX:NC * CTX + D], CV, False,
                                       lambda c, hl: ctx_t[:, c, hl, :], slice(0, D), ones16[:, 1, 0:CTX])
                    elif name == "D3":
                        pe.wait_ge(LN3.s_done, b + 1)
                        last = transpose_tiles(bank, h)
                    last.then_inc(s_job[name], 1)

                def body(it):
                    for k in range(UNITS):
                        if it.has(SELF):
                            scores_self(it, k)
                        if it.has(CROSS) and k:
                            scores_cross(it, k)
                        weighted_values(A, it, k)
                        weighted_values(C, it, k)
                        for name in JOBS[k]:
                            job(it, name)
                        if it.has(CROSS) and not k:
                            scores_cross(it, k)
                        transposes(A, it, k)
                        transposes(C, it, k)

                pe.wait_ge(s_init, 1)
                pipeline(pe, body)

            @block.scalar
            def _(act):
                def exps(att_, it, k):
                    off, kk = lag(att_.stage, k, 1)
                    if not it.has(off):
                        return
                    b, n = it.batch(off), att_.keys
                    act.wait_ge(att_.s_t, unit(b, kk))
                    if kk >= 4 or it.has(off - 1):
                        act.wait_ge(att_.s_pv, unit(b, kk - 4))
                    if kk >= 2 or it.has(off - 1):
                        act.wait_ge(att_.s_lo, unit(b, kk - 2))
                    act.activation(att_.p_hi[0:n, kk % 4, :], att_.t_bank[0:n, :], ACT.Exp).then_inc(att_.s_hi, 1)
                    act.activation(att_.p32[0:n, kk % 2, :], att_.t_bank[0:n, :], ACT.Exp).then_inc(att_.s_p32, 1)

                def cols(bank, n):
                    return bank[:, 0:NC * n].rearrange("p (c t) -> p c t", c=NC)

                def job(it, name):
                    off = STAGE[name[0]]
                    if not it.has(off) or name in ("B2", "D2"):
                        return
                    b, par, bank = it.batch(off), it.par(off), job_bank[name]
                    act.wait_ge(s_job[name], b + 1)
                    if name == "P1":
                        if it.has(off - 1):
                            act.wait_ge(s_job["P4"], b)
                        last = act.activation(xn_t[:, :, 0, :], cols(bank, SEQ), ACT.Copy)
                    elif name == "P2":
                        if it.has(off - 1):
                            act.wait_ge(s_qdup, DUP * b)
                            act.wait_ge(s_got["P2"], b)
                        last = act.activation(q_hi[:, :, :], cols(bank, SEQ), ACT.Copy, scale=QK / (XN * WS))
                    elif name == "P3":
                        if it.has(off - 1):
                            act.wait_ge(s_kboth, DUP * b)
                        last = act.activation(k_t[:, :, 0, :], cols(bank, SEQ), ACT.Copy, scale=QK / (XN * WS))
                    elif name == "P4":
                        if it.has(off - 2):
                            act.wait_ge(A.s_pv, unit(b - 2, UNITS - 1))
                        last = act.activation(v[:, par, 0, :, :, 0:HD],
                                              bank[:, :].rearrange("p (w h d) -> p w h d", w=2, h=HEADS),
                                              ACT.Copy, scale=VS / (XN * WS))
                    elif name in ("B1", "D1"):
                        att_ = A if name == "B1" else C
                        if it.has(off - 1):
                            act.wait_ge(s_job[name[0] + "2"], b)
                        last = act.activation(att_.o_t[:, :, 0, :], cols(bank, SEQ), ACT.Copy)
                    elif name == "B3":
                        if it.has(off - 1):
                            act.wait_ge(s_job["B4"], b)
                        last = act.activation(xn2_t[:, :, 0, :], cols(bank, SEQ), ACT.Copy)
                    elif name == "B4":
                        if it.has(off - 1):
                            act.wait_ge(s_q2dup, 4 * b)
                            act.wait_ge(s_got["B4"], b)
                        last = act.activation(q2_hi[:, :, :], cols(bank, SEQ), ACT.Copy, scale=QK / (XN * WS))
                    elif name == "X1":
                        if it.has(off - 1):
                            act.wait_ge(s_job["X2"], b)
                        last = act.activation(ctx_t[:, :, 0, :], cols(bank, CTX), ACT.Copy, scale=VS)
                    elif name == "X2":
                        if it.has(off - 1):
                            act.wait_ge(s_k2both, DUP * b)
                        if it.has(off - 2):
                            act.wait_ge(C.s_pv, unit(b - 2, UNITS - 1))
                        act.activation(k2_t[:, :, 0, :], cols(bank, CTX), ACT.Copy,
                                       scale=QK / (VS * WS)).then_inc(s_hi["X2"], 1)
                        last = act.activation(v2_hi[:, par, :, 0:HD],
                                              bank[0:CTX, NC * CTX:NC * CTX + D].rearrange("p (h d) -> p h d", h=HEADS),
                                              ACT.Copy, scale=VS / (VS * WS))
                    elif name == "D3":
                        if it.has(off - 1):
                            act.wait_ge(s_hw, 16 * b)
                        last = act.activation(h_t[:, :, :], cols(bank, SEQ), ACT.Copy)
                    last.then_inc(s_hi[name], 1)

                def duplicate_cross(it):
                    if not it.has(MID):
                        return
                    b, par = it.batch(MID), it.par(MID)
                    act.wait_ge(s_hi["B4"], b + 1)
                    if it.has(MID - 2):
                        act.wait_ge(C.s_scores, unit(b - 2, UNITS - 1))
                    for half_of_chunk in range(2):
                        rows = slice(HALF * half_of_chunk, HALF * (half_of_chunk + 1))
                        for side in range(2):
                            act.activation(q2_dup[HALF * side:HALF * (side + 1), par, half_of_chunk::2, :],
                                           q2_hi[rows, :, :], ACT.Copy).then_inc(s_q2dup, 1)

                def block_self(it, j):
                    if not it.has(PREP):
                        return
                    b, par = it.batch(PREP), it.par(PREP)
                    if j == 0:
                        act.wait_ge(s_kboth, DUP * (b + 1))
                        if it.has(PREP - 2):
                            act.wait_ge(A.s_scores, unit(b - 2, UNITS - 1))
                    act.activation(k_blk[:, par, :, j, WIN:WIN + SEQ], k_both[:, :, :], ACT.Copy,
                                   scale=head_rows[:, j:j + 1]).then_inc(s_kblk, 1)

                def block_cross(it, j):
                    if not it.has(MID):
                        return
                    b, par = it.batch(MID), it.par(MID)
                    if j == 0:
                        act.wait_ge(s_k2both, DUP * (b + 1))
                        if it.has(MID - 2):
                            act.wait_ge(C.s_scores, unit(b - 2, UNITS - 1))
                    act.activation(k2_blk[:, par, :, j, :], k2_both[:, :, :], ACT.Copy,
                                   scale=head_rows[:, j:j + 1]).then_inc(s_k2blk, 1)

                def body(it):
                    for k in range(UNITS):
                        if k == 7:
                            block_cross(it, 3)
                        for name in JOBS[k]:
                            job(it, name)
                        if k == 7:
                            duplicate_cross(it)
                        exps(A, it, k)
                        exps(C, it, k)
                        if BLOCKS_FROM <= k < BLOCKS_FROM + HU:
                            block_self(it, k - BLOCKS_FROM)
                        for j in {5: [0], 6: [1, 2]}.get(k, []):
                            block_cross(it, j)

                act.wait_ge(s_init, 1)
                pipeline(act, body)

            @block.vector
            def _(dve):
                def wide(v, n):
                    return v.unsqueeze(2).to_broadcast([P, HU, n])

                def shifts(it, k):
                    r, t = k % 2, k // (UNITS // NT)
                    both = it.has(SELF), it.has(CROSS)
                    b, b2 = it.batch(SELF), it.batch(CROSS)
                    s3 = A.s_bank[:, :].rearrange("p (h n) -> p h n", h=HU)
                    y3 = C.y[:, r, :].rearrange("p (h n) -> p h n", h=HU)
                    if both[0]:
                        dve.wait_ge(A.s_scores, unit(b, k))
                        dve.tensor_reduce(out=A.mx[:, r, :], in_=s3, axis=AX.X, op=ALU.max).then_inc(A.s_max, 1)
                    if both[1]:
                        dve.wait_ge(C.s_scores, unit(b2, k))
                        if k >= 2 or it.has(CROSS - 1):
                            dve.wait_ge(C.s_u, unit(b2, k - 2))
                        dve.scalar_tensor_tensor(out=y3,
                                                 in0=C.s_bank[:, 0:HU * CTX].rearrange("p (h n) -> p h n", h=HU),
                                                 scalar=LOGIT,
                                                 in1=mask_c[:, t, :].unsqueeze(1).to_broadcast([P, HU, CTX]),
                                                 op0=ALU.mult, op1=ALU.add).then_inc(C.s_y, 1)
                    if both[0]:
                        dve.wait_ge(A.s_max, unit(b, k))
                        dve.tensor_scalar(A.mshift[:, r, :], A.mx[:, r, :], LOGIT, SHIFT,
                                          ALU.mult, ALU.subtract).then_inc(A.s_shift, 1)
                    if both[1]:
                        dve.wait_ge(C.s_y, unit(b2, k))
                        dve.tensor_reduce(out=C.mx[:, r, :], in_=y3, axis=AX.X, op=ALU.max).then_inc(C.s_max, 1)
                    if both[0]:
                        dve.wait_ge(A.s_shift, unit(b, k))
                        if k >= 2 or it.has(SELF - 1):
                            dve.wait_ge(A.s_t, unit(b, k - 2))
                        dve.scalar_tensor_tensor(out=A.u[:, r, :].rearrange("p (h n) -> p h n", h=HU), in0=s3,
                                                 scalar=LOGIT, in1=wide(A.mshift[:, r, :], P),
                                                 op0=ALU.mult, op1=ALU.subtract).then_inc(A.s_u, 1)
                    if both[1]:
                        dve.wait_ge(C.s_max, unit(b2, k))
                        dve.tensor_scalar(C.mshift[:, r, :], C.mx[:, r, :], SHIFT, None,
                                          ALU.subtract).then_inc(C.s_shift, 1)

                def normalise(it, k):
                    todo = []
                    for att_, job_name in ((A, "B1"), (C, "D1")):
                        off, kk = lag(att_.stage, k, 3)
                        if it.has(off) and kk % (UNITS // NT) == UNITS // NT - 1:
                            todo.append((att_, job_name, off, it.batch(off), kk // (UNITS // NT), kk))
                    o3 = {att_: att_.o_bank[:, 0:HEADS * (HD + 1)].rearrange("p (h d) -> p h d", h=HEADS)
                          for att_ in (A, C)}
                    for att_, job_name, off, b, t, kk in todo:
                        dve.wait_ge(att_.s_pv, unit(b, kk))
                        dve.reciprocal(att_.den[:, :], o3[att_][:, :, HD]).then_inc(att_.s_den, 1)
                    for att_, job_name, off, b, t, kk in todo:
                        dve.wait_ge(att_.s_den, b * NT + (t + 1))
                        if it.has(off - 1):
                            dve.wait_ge(s_job[job_name], b)
                        dve.tensor_tensor(att_.o[:, t, :].rearrange("p (h d) -> p h d", h=HEADS),
                                          o3[att_][:, :, 0:HD],
                                          att_.den[:, :].unsqueeze(2).to_broadcast([P, HEADS, HD]),
                                          ALU.mult).then_inc(att_.s_o, 1)

                def statistics(ln, src, b, scale):
                    for t in range(NT):
                        dve.bn_stats(ln.part[:, t, :], src[:, t, :]).then_inc(ln.s_part, 1)
                    dve.wait_ge(ln.s_part, NT * (b + 1))
                    dve.sem_inc(ln.s_seen, 1)
                    for t in range(NT):
                        dve.bn_aggr(ln.mv[:, t, :], ln.part[:, t, :]).then_inc(ln.s_mv, 1)
                    dve.wait_ge(ln.s_mv, NT * (b + 1))
                    dve.tensor_scalar(ln.ve[:, :], ln.mv[:, :, 1], EPS, 1.0 / scale ** 2,
                                      ALU.add, ALU.mult).then_inc(ln.s_ve, 1)

                def apply_norm(ln, dst, src, b):
                    dve.wait_ge(ln.s_rstd, b + 1)
                    for t in range(NT):
                        last = dve.tensor_scalar(dst[:, t, :], src[:, t, :], ln.mv[:, t, 0:1], ln.rstd[:, t:t + 1],
                                                 ALU.subtract, ALU.mult)
                    last.then_inc(ln.s_done, 1)

                def cols(bank, n):
                    return bank[:, 0:NC * n].rearrange("p (c t) -> p c t", c=NC)

                def low(dst, src, hi, scale):
                    return dve.scalar_tensor_tensor(out=dst, in0=src, scalar=scale, in1=hi,
                                                    op0=ALU.mult, op1=ALU.subtract)

                def job(it, name):
                    off = STAGE[name[0]]
                    if not it.has(off):
                        return
                    b, par, bank = it.batch(off), it.par(off), job_bank[name]
                    if name in ("B2", "D2"):
                        dve.wait_ge(s_job[name], b + 1)
                    else:
                        dve.wait_ge(s_hi[name], (2 * b + 2) if name == "X2" else (b + 1))
                    if name == "P1":
                        last = low(xn_t[:, :, 1, :], cols(bank, SEQ), xn_t[:, :, 0, :], 1.0)
                    elif name == "P2":
                        if it.has(off - 2):
                            dve.wait_ge(A.s_scores, unit(b - 2, UNITS - 1))
                        last = low(q_lo[:, par, :, :], cols(bank, SEQ), q_hi[:, :, :], QK / (XN * WS))
                    elif name == "P3":
                        last = low(k_t[:, :, 1, :], cols(bank, SEQ), k_t[:, :, 0, :], QK / (XN * WS))
                    elif name == "P4":
                        last = low(v[:, par, 0, :, :, HD + 1:].rearrange("p t h d -> p (t h) d"),
                                   bank[:, :].rearrange("p (g d) -> p g d", d=HD),
                                   v[:, par, 0, :, :, 0:HD].rearrange("p t h d -> p (t h) d"), VS / (XN * WS))
                    elif name in ("B1", "D1"):
                        o_t = (A if name == "B1" else C).o_t
                        last = low(o_t[:, :, 1, :], cols(bank, SEQ), o_t[:, :, 0, :], 1.0)
                    elif name in ("B2", "D2"):
                        src, dst = (x_mid, x1) if name == "B2" else (x1_back, x2)
                        dve.wait_ge(s_xm if name == "B2" else s_x1b, 16 * (b + 1))
                        if it.has(off - 1):
                            dve.wait_ge(s_x1w if name == "B2" else s_x2w, 16 * b)
                        last = dve.scalar_tensor_tensor(out=dst[:, :, :],
                                                        in0=bank[:, :].rearrange("p (t d) -> p t d", t=NT),
                                                        scalar=1.0 / (VS * WS), in1=src[:, :, :],
                                                        op0=ALU.mult, op1=ALU.add)
                    elif name == "B3":
                        last = low(xn2_t[:, :, 1, :], cols(bank, SEQ), xn2_t[:, :, 0, :], 1.0)
                    elif name == "B4":
                        if it.has(off - 2):
                            dve.wait_ge(C.s_scores, unit(b - 2, UNITS - 1))
                        last = low(q2_lo[:, par, :, :], cols(bank, SEQ), q2_hi[:, :, :], QK / (XN * WS))
                    elif name == "X1":
                        last = low(ctx_t[:, :, 1, :], cols(bank, CTX), ctx_t[:, :, 0, :], VS)
                    elif name == "X2":
                        low(v2_lo[:, par, :, :],
                            bank[0:CTX, NC * CTX:NC * CTX + D].rearrange("p (h d) -> p h d", h=HEADS),
                            v2_hi[:, par, :, 0:HD], VS / (VS * WS))
                        last = low(k2_t[:, :, 1, :], cols(bank, CTX), k2_t[:, :, 0, :], QK / (VS * WS))
                    elif name == "D3":
                        last = dve.tensor_reduce(out=h_max[:, bass.ds(b, 1)], in_=bank[:, :], axis=AX.X, op=ALU.max,
                                                 apply_absolute_value=True)
                    last.then_inc(s_got[name], 1)
                    if name in ("B2", "D2"):
                        dve.wait_ge(s_got[name], b + 1)
                        if name == "B2":
                            statistics(LN2, x1, b, XN)
                        else:
                            statistics(LN3, x2, b, 1.0)

                def body(it):
                    for k in range(UNITS):
                        shifts(it, k)
                        normalise(it, k)
                        for name in JOBS[k]:
                            job(it, name)
                        if k == 0 and it.has(LOAD):
                            b = it.batch(LOAD)
                            dve.wait_ge(s_x[it.par(LOAD)], 16 * (it.nth(LOAD) + 1))
                            statistics(LN1, x_in[:, it.par(LOAD), :, :], b, XN)
                        if k == 1 and it.has(LOAD):
                            b = it.batch(LOAD)
                            if it.has(LOAD - 1):
                                dve.wait_ge(s_job["P1"], b)
                            apply_norm(LN1, xn, x_in[:, it.par(LOAD), :, :], b)
                        if k == 5 and it.has(MID):
                            b = it.batch(MID)
                            if it.has(MID - 1):
                                dve.wait_ge(s_job["B3"], b)
                            apply_norm(LN2, xn2, x1, b)
                        if k == 6 and it.has(END):
                            b = it.batch(END)
                            if it.has(END - 1):
                                dve.wait_ge(s_job["D3"], b)
                            apply_norm(LN3, h, x2, b)

                dve.memset(v[0:WIN, :, 1, 0, :, :], 0.0)
                for n in range(2):
                    dve.memset(v[:, n, 0, :, :, HD:HD + 1].rearrange("p t h d -> p (t h) d"), 1.0)
                dve.memset(v2_hi[:, :, :, HD:HD + 1].rearrange("p a h d -> p (a h) d"), 1.0).then_inc(s_init, 1)
                pipeline(dve, body)

            @block.gpsimd
            def _(pool):
                def rstd(ln, b):
                    pool.wait_ge(ln.s_ve, b + 1)
                    pool.tensor_tensor(ln.rstd[:, :], ln.ve[:, :], half[:, :], ALU.pow).then_inc(ln.s_rstd, 1)

                def subtract_cross(it, k):
                    b, r = it.batch(CROSS), k % 2
                    pool.wait_ge(C.s_shift, unit(b, k))
                    if k >= 2 or it.has(CROSS - 1):
                        pool.wait_ge(C.s_t, unit(b, k - 2))
                    pool.tensor_tensor(C.u[:, r, :].rearrange("p (h n) -> p h n", h=HU),
                                       C.y[:, r, :].rearrange("p (h n) -> p h n", h=HU),
                                       C.mshift[:, r, :].unsqueeze(2).to_broadcast([P, HU, CTX]),
                                       ALU.subtract).then_inc(C.s_u, 1)

                def low_part(att_, it, k):
                    off, kk = lag(att_.stage, k, 2)
                    if not it.has(off):
                        return
                    b, n = it.batch(off), att_.keys
                    pool.wait_ge(att_.s_p32, unit(b, kk))
                    pool.wait_ge(att_.s_hi, unit(b, kk))
                    if kk >= 4 or it.has(off - 1):
                        pool.wait_ge(att_.s_pv, unit(b, kk - 4))
                    pool.tensor_tensor(att_.p_lo[0:n, kk % 4, :], att_.p32[0:n, kk % 2, :], att_.p_hi[0:n, kk % 4, :],
                                       ALU.subtract).then_inc(att_.s_lo, 1)

                def body(it):
                    for k in range(UNITS):
                        low_part(A, it, k)
                        low_part(C, it, k)
                        if it.has(CROSS):
                            subtract_cross(it, k)
                        if k == 1 and it.has(LOAD):
                            rstd(LN1, it.batch(LOAD))
                        if k == 5 and it.has(MID):
                            rstd(LN2, it.batch(MID))
                        if k == 6 and it.has(END):
                            rstd(LN3, it.batch(END))

                pipeline(pool, body)

        att.close()

        s_red = sem("maximum_over_free_axis_ready")
        s_all = sem("maximum_over_partitions_ready")
        s_scale = sem("scales_ready")
        chain = [0]

        def step(dve, ins):
            chain[0] += 1
            ins.then_inc(s_scale, 1)
            dve.wait_ge(s_scale, chain[0])

        def quant_scale(dve, s_out, c_out):
            step(dve, dve.tensor_tensor(st(s_out), st(ALL), st(REAL), ALU.mult))
            step(dve, dve.tensor_scalar(st(s_out), st(s_out), 1.0 / QMAX, TINY, ALU.mult, ALU.max))
            step(dve, dve.reciprocal(st(c_out), st(s_out)))
            step(dve, dve.tensor_tensor(st(c_out), st(c_out), st(REAL), ALU.mult))

        reds = [0]

        def global_max(dve, src):
            reds[0] += 1
            dve.tensor_reduce(out=st(RED), in_=src, axis=AX.X, op=ALU.max).then_inc(s_red, 1)
            dve.wait_ge(s_all, reds[0])

        def pool_max(pool, n):
            pool.wait_ge(s_red, n)
            pool.partition_all_reduce(st(ALL), st(RED), P, RMAX).then_inc(s_all, 1)

        with ExitStack() as c1:
            GB = GRP // SEQ
            h_in = sb("h_in", [P, 2, GB, NC, SEQ], F32, c1)
            xt = sb("xt", [P, 2, GB, NC, SEQ], F32, c1)
            x_hi = sb("x_hi", [P, 2, GB, NC, SEQ], F16, c1)
            x_lo = sb("x_lo", [P, 2, GB, NC, SEQ], F16, c1)
            s_hl = [sem(f"h_loaded_{n}") for n in range(2)]
            MB = NM // 2
            NB = 2 * NM // MB
            stage = sb("stage", [P, NB, MB, GRP], F32, c1)
            raw_max = sb("raw_max", [P, 2 * NM, NG], F32, c1)
            s_xt = sem("h_rounded")
            s_xh = sem("x_hi_ready")
            s_xl = sem("x_lo_ready")
            s_raw = sem("raw_product_done")
            s_copy = sem("raw_product_copied")
            s_rmax = sem("raw_product_maximum_ready")
            s_store = [sem(f"raw_stored_{n}") for n in range(NB)]
            M2 = 2 * NM

            with nc.Block() as block:

                @block.vector
                def _(dve):
                    step(dve, dve.memset(magic[:, :], MAGIC))
                    step(dve, dve.memset(st(REAL), 1.0))
                    global_max(dve, h_max[:, :])
                    quant_scale(dve, S_H, I_H)

                    def split(g, q, par, first):
                        dve.wait_ge(s_hl[par], 16 * (q + 1))
                        if not first:
                            dve.wait_ge(s_raw, (g - 1) * M2)
                        dve.tensor_scalar(xt[:, par, :, :, :], h_in[:, par, :, :, :], st(I_H), MAGIC,
                                          ALU.mult, ALU.add).then_inc(s_xt, 1)
                        dve.wait_ge(s_xt, g + 1)
                        dve.tensor_scalar(x_hi[:, par, :, :, :], xt[:, par, :, :, :], MAGIC, None,
                                          ALU.subtract).then_inc(s_xh, 1)
                        dve.wait_ge(s_xh, g + 1)
                        dve.scalar_tensor_tensor(out=x_lo[:, par, :, :, :].rearrange("p b c t -> p (b c t)"),
                                                 in0=xt[:, par, :, :, :].rearrange("p b c t -> p (b c t)"),
                                                 scalar=MAGIC,
                                                 in1=x_hi[:, par, :, :, :].rearrange("p b c t -> p (b c t)"),
                                                 op0=ALU.subtract, op1=ALU.subtract).then_inc(s_xl, 1)

                    def maxima(g, par, ms):
                        for m in ms:
                            dve.wait_ge(s_copy, g * M2 + (m + 1))
                            dve.tensor_reduce(out=raw_max[:, m, bass.ds(g, 1)], in_=stage[:, m // MB, m % MB, :],
                                              axis=AX.X, op=ALU.max, apply_absolute_value=True).then_inc(s_rmax, 1)

                    def reduce_and_split(g, q, par, first=False):
                        maxima(g, par, range(6))
                        split(g + 1, q + par, 1 - par, first)
                        maxima(g, par, range(6, M2))

                    split(0, 0, 0, True)
                    reduce_and_split(0, 0, 0, True)
                    reduce_and_split(1, 0, 1)
                    with dve.Fori(1, NG // 2 - 1, 1) as q:
                        reduce_and_split(q * 2, q, 0)
                        reduce_and_split(q * 2 + 1, q, 1)
                    reduce_and_split(NG - 2, NG // 2 - 1, 0)
                    maxima(NG - 1, 1, range(M2))
                    dve.wait_ge(s_rmax, NG * M2)
                    step(dve, dve.tensor_scalar(st(REAL), st(S_H), 1.0 / WS, None, ALU.mult))
                    flat = raw_max[:, :, :].rearrange("p m g -> p (m g)")
                    for n, (s_out, c_out) in enumerate(((S_U, C_U), (S_G, C_G))):
                        global_max(dve, flat[:, n * NM * NG:(n + 1) * NM * NG])
                        quant_scale(dve, s_out, c_out)

                @block.gpsimd
                def _(pool):
                    for n in range(3):
                        pool_max(pool, n + 1)

                @block.tensor
                def _(pe):
                    def body(g, par):
                        pe.wait_ge(s_xl, g + 1)
                        for m in range(M2):
                            bank = banks[(M2 * par + m) % 8]
                            if not isinstance(g, int) or g * M2 + m >= 8:
                                pe.wait_ge(s_copy, g * M2 + (m - 7))
                            for c in range(NC):
                                cols = slice(m * P, (m + 1) * P)
                                hi, lo = x_hi[:, par, :, c, :], x_lo[:, par, :, c, :]
                                pe.matmul(bank[:, :], w_gu_t[:, c, 0, cols], hi, start=c == 0, stop=False)
                                pe.matmul(bank[:, :], w_gu_t[:, c, 0, cols], lo, start=False, stop=False)
                                last = pe.matmul(bank[:, :], w_gu_t[:, c, 1, cols], hi, start=False, stop=c == NC - 1)
                            last.then_inc(s_raw, 1)

                    body(0, 0)
                    body(1, 1)
                    with pe.Fori(1, NG // 2, 1) as q:
                        body(q * 2, 0)
                        body(q * 2 + 1, 1)

                @block.scalar
                def _(act):
                    def body(g, par, first):
                        for m in range(M2):
                            q, j = divmod(m, MB)
                            act.wait_ge(s_raw, g * M2 + (m + 1))
                            if j == 0 and not first:
                                act.wait_ge(s_store[q], 16 * g)
                                act.wait_ge(s_rmax, (g - 1) * M2 + MB * (q + 1))
                            act.activation(stage[:, q, j, :], banks[(M2 * par + m) % 8][:, :],
                                           ACT.Copy).then_inc(s_copy, 1)

                    body(0, 0, True)
                    body(1, 1, False)
                    with act.Fori(1, NG // 2, 1) as q:
                        body(q * 2, 0, False)
                        body(q * 2 + 1, 1, False)

                @block.sync
                def _(sp):
                    def load(g, par):
                        sp.dma_start(h_in[:, par, :, :, :], h_d[bass.ds(g * GB, GB)]
                                     .rearrange("b p c t -> p b c t")).then_inc(s_hl[par], 16)

                    def store(g):
                        for q in range(NB):
                            sp.wait_ge(s_copy, g * M2 + MB * (q + 1))
                            m0 = MB * (q % 2)
                            sp.dma_start(raw_d[q // 2, g, m0:m0 + MB].rearrange("m p t -> p m t"), stage[:, q, :, :]).then_inc(s_store[q], 16)

                    load(0, 0)
                    load(1, 1)
                    with sp.Fori(0, NG // 2 - 1, 1) as q:
                        for par in range(2):
                            g = q * 2
                            sp.wait_ge(s_xt, g + (par + 1))
                            load(g + (par + 2), par)
                            store(g + par)
                    store(NG - 2)
                    store(NG - 1)
                    for q in range(NB):
                        sp.wait_ge(s_store[q], 16 * NG)

        mid.close()

        PM = NM // 2
        PIECES = 2 * NG
        W = PM * GRP
        up_d, gate_d = (raw_d[n].rearrange("g (h m) p t -> (g h) p m t", h=2) for n in range(2))
        o_pieces = o_d.rearrange("g (h m) p t -> (g h) p m t", h=2)

        def piece(buf, n):
            return buf[:, n, :].rearrange("p (m t) -> p m t", m=PM)

        for with_up in (False, True):
            tag = "o" if with_up else "gate"
            with ExitStack() as c2:
                g_in = sb(f"{tag}_g_in", [P, 2, W], F32, c2)
                g_t = sb(f"{tag}_g_t", [P, W], F32, c2)
                g_n = sb(f"{tag}_g_n", [P, 2, W], F32, c2)
                sg = sb(f"{tag}_sig", [P, 2, W], F32, c2)
                prod = sb(f"{tag}_prod", [P, 2, W], F32, c2)
                p_max = sb(f"{tag}_p_max", [P, PIECES], F32, c2)
                s_gl = [sem(f"{tag}_gate_loaded_{n}") for n in range(2)]
                s_gt = sem(f"{tag}_gate_plus_magic")
                s_gn = sem(f"{tag}_gate_integer")
                s_sg = sem(f"{tag}_sigmoid")
                s_sa = sem(f"{tag}_sigmoid_rounded")
                s_sq = sem(f"{tag}_sigmoid_integer")
                s_pr = sem(f"{tag}_product")
                s_fin = sem(f"{tag}_piece_reduced")
                s_oo = sem(f"{tag}_output_ready")
                if with_up:
                    u_in = sb("u_in", [P, 2, W], F32, c2)
                    u_t = sb("u_t", [P, W], F32, c2)
                    u_n = sb("u_n", [P, W], F32, c2)
                    o_sb = sb("o_sb", [P, 2, W], F32, c2)
                    s_ul = [sem(f"up_loaded_{n}") for n in range(2)]
                    s_ut = sem("up_plus_magic")
                    s_un = sem("up_integer")
                    s_g2 = sem("gate_requantised")
                    s_ow = [sem(f"o_stored_{n}") for n in range(2)]

                def two(eng, body):
                    for n in range(2):
                        body(n, 0, n)
                    with eng.Fori(1, PIECES // 2, 1) as q:
                        for n in range(2):
                            body(q * 2 + n, q, n)

                with nc.Block() as block:

                    @block.sync
                    def _(sp):
                        def body(j, q, n):
                            if not isinstance(j, int):
                                sp.wait_ge(s_ut if with_up else s_gt, j - 1)
                            sp.dma_start(piece(g_in, n), gate_d[j]).then_inc(s_gl[n], 16)
                            if with_up:
                                sp.dma_start(piece(u_in, n), up_d[j]).then_inc(s_ul[n], 16)

                        two(sp, body)

                    @block.scalar
                    def _(act):
                        def sigmoid(j, n):
                            act.wait_ge(s_gn, j + 1)
                            if not isinstance(j, int) or j >= 2:
                                act.wait_ge(s_pr, j - 1)
                            act.activation(sg[:, n, :], g_n[:, n, :], ACT.Sigmoid, scale=st(S_G)).then_inc(s_sg, 1)

                        def body(j, q, n):
                            act.wait_ge(s_gl[n], 16 * (q + 1))
                            if not (isinstance(j, int) and j == 0):
                                act.wait_ge(s_gn, j)
                            act.activation(g_t[:, :], g_in[:, n, :], ACT.Identity, bias=magic[:, 0:1],
                                           scale=st(C_G)).then_inc(s_gt, 1)
                            if with_up:
                                act.wait_ge(s_ul[n], 16 * (q + 1))
                                if not (isinstance(j, int) and j == 0):
                                    act.wait_ge(s_un, j)
                                act.activation(u_t[:, :], u_in[:, n, :], ACT.Identity, bias=magic[:, 0:1],
                                               scale=st(C_U)).then_inc(s_ut, 1)
                            sigmoid(j, n)
                            if with_up and not (isinstance(j, int) and j == 0):
                                store(j - 1, 1 - n)

                        def store(j, n):
                            act.wait_ge(s_fin, j + 1)
                            act.dma_start(o_pieces[j], piece(o_sb, n)).then_inc(s_ow[n], 16)

                        two(act, body)
                        if with_up:
                            store(PIECES - 1, 1)
                            for n in range(2):
                                act.wait_ge(s_ow[n], 16 * (PIECES // 2))

                    @block.gpsimd
                    def _(pool):
                        def body(j, q, n):
                            pool.wait_ge(s_sq, j + 1)
                            if not isinstance(j, int) or j >= 2:
                                pool.wait_ge(s_fin, j - 1)
                            pool.tensor_tensor(prod[:, n, :], g_n[:, n, :], sg[:, n, :],
                                               ALU.mult).then_inc(s_pr, 1)

                        two(pool, body)
                        pool_max(pool, reds[0] + 1)

                    @block.vector
                    def _(dve):
                        def front(j, q, n):
                            dve.wait_ge(s_gt, j + 1)
                            if not isinstance(j, int) or j >= 2:
                                dve.wait_ge(s_pr, j - 1)
                            dve.tensor_scalar(g_n[:, n, :], g_t[:, :], MAGIC, None, ALU.subtract).then_inc(s_gn, 1)

                        def sig(j, q, n):
                            dve.wait_ge(s_sg, j + 1)
                            dve.tensor_scalar(sg[:, n, :], sg[:, n, :], SIG, MAGIC, ALU.mult, ALU.add)\
                               .then_inc(s_sa, 1)
                            dve.wait_ge(s_sa, j + 1)
                            dve.tensor_scalar(sg[:, n, :], sg[:, n, :], MAGIC, SIG - 1, ALU.subtract, ALU.min)\
                               .then_inc(s_sq, 1)

                        def back(j, q, n):
                            dve.wait_ge(s_pr, j + 1)
                            if not with_up:
                                dve.tensor_reduce(out=p_max[:, bass.ds(j, 1)], in_=prod[:, n, :], axis=AX.X,
                                                  op=ALU.max, apply_absolute_value=True).then_inc(s_fin, 1)
                                return
                            dve.tensor_scalar(prod[:, n, :], prod[:, n, :], st(C_P), MAGIC, ALU.mult, ALU.add)\
                               .then_inc(s_g2, 1)
                            dve.wait_ge(s_g2, j + 1)
                            if not (isinstance(j, int) and j < 2):
                                dve.wait_ge(s_ow[n], 16 * q)
                            dve.wait_ge(s_un, j + 1)
                            dve.scalar_tensor_tensor(out=o_sb[:, n, :], in0=prod[:, n, :], scalar=MAGIC,
                                                     in1=u_n[:, :], op0=ALU.subtract,
                                                     op1=ALU.mult).then_inc(s_oo, 1)
                            dve.wait_ge(s_oo, j + 1)
                            dve.tensor_reduce(out=p_max[:, bass.ds(j, 1)], in_=o_sb[:, n, :], axis=AX.X,
                                              op=ALU.max, apply_absolute_value=True).then_inc(s_fin, 1)

                        def up(j, q, n):
                            if with_up:
                                dve.wait_ge(s_ut, j + 1)
                                dve.tensor_scalar(u_n[:, :], u_t[:, :], MAGIC, None, ALU.subtract)\
                                   .then_inc(s_un, 1)

                        def end_and_start(j, q, n):
                            front(j + 1, q + n, 1 - n)
                            up(j, q, n)
                            back(j, q, n)
                            sig(j + 1, q + n, 1 - n)

                        front(0, 0, 0)
                        sig(0, 0, 0)
                        end_and_start(0, 0, 0)
                        end_and_start(1, 0, 1)
                        with dve.Fori(1, PIECES // 2 - 1, 1) as q:
                            end_and_start(q * 2, q, 0)
                            end_and_start(q * 2 + 1, q, 1)
                        q = PIECES // 2 - 1
                        end_and_start(2 * q, q, 0)
                        up(2 * q + 1, q, 1)
                        back(2 * q + 1, q, 1)
                        dve.wait_ge(s_fin, PIECES)
                        if with_up:
                            step(dve, dve.tensor_tensor(st(REAL), st(S_P), st(S_U), ALU.mult))
                            global_max(dve, p_max[:, :])
                            quant_scale(dve, S_O, C_O)
                            step(dve, dve.tensor_scalar(st(S_O), st(S_O), 1.0 / WS, None, ALU.mult))
                        else:
                            step(dve, dve.tensor_scalar(st(REAL), st(S_G), 1.0 / SIG, None, ALU.mult))
                            global_max(dve, p_max[:, :])
                            quant_scale(dve, S_P, C_P)

        GT = GRP // P
        GB = GRP // SEQ
        with ExitStack() as c3:
            o_in = sb("o_in", [P, 2, NM, GRP], F32, c3)
            o_t = sb("o_t", [P, NM, GRP], F32, c3)
            o_hi = sb("o_hi", [P, 2, NM, GRP], F16, c3)
            o_lo = sb("o_lo", [P, 2, NM, GRP], F16, c3)
            x2_in = sb("x2_in", [P, 2, GB, NT, D], F32, c3)
            y = sb("y", [P, 2, GT, D], F32, c3)
            s_ol = [sem(f"o_loaded_{n}") for n in range(2)]
            s_xl2 = [sem(f"x2_loaded_{n}") for n in range(2)]
            s_ot = sem("o_plus_magic")
            s_oh = sem("o_hi_ready")
            s_olo = sem("o_lo_ready")
            s_down = sem("down_product_done")
            s_y = sem("y_ready")
            s_yw = [sem(f"y_stored_{n}") for n in range(2)]

            def pairs(eng, body):
                for n in range(2):
                    body(n, 0, n, True)
                with eng.Fori(1, NG // 2, 1) as q:
                    for n in range(2):
                        body(q * 2 + n, q, n, False)

            with nc.Block() as block:

                @block.sync
                def _(sp):
                    def body(g, q, n, first):
                        if not first:
                            sp.wait_ge(s_ot, g - 1)
                        sp.dma_start(o_in[:, n, :, :], o_d[g].rearrange("m p t -> p m t")).then_inc(s_ol[n], 16)
                        if not first:
                            sp.wait_ge(s_y, (g - 1) * GT)
                        sp.dma_start(x2_in[:, n, :, :, :], x2_d[bass.ds(g * GB, GB)]
                                     .rearrange("b p t d -> p b t d")).then_inc(s_xl2[n], 16)

                    pairs(sp, body)

                @block.scalar
                def _(act):
                    def body(g, q, n, first):
                        act.wait_ge(s_ol[n], 16 * (q + 1))
                        if not (first and n == 0):
                            act.wait_ge(s_olo, g)
                        act.activation(o_t[:, :, :], o_in[:, n, :, :], ACT.Identity, bias=magic[:, 0:1],
                                       scale=st(C_O)).then_inc(s_ot, 1)
                        if not (first and n == 0):
                            store(g - 1, 1 - n)

                    def store(g, n):
                        act.wait_ge(s_y, (g + 1) * GT)
                        act.dma_start(out_g[bass.ds(g * GT, GT)].rearrange("t p d -> p t d"),
                                      y[:, n, :, :]).then_inc(s_yw[n], 16)

                    pairs(act, body)
                    store(NG - 1, 1)
                    for n in range(2):
                        act.wait_ge(s_yw[n], 16 * (NG // 2))

                @block.vector
                def _(dve):
                    def split(g, q, n, first):
                        dve.wait_ge(s_ot, g + 1)
                        if not first:
                            dve.wait_ge(s_down, (g - 1) * GT)
                        dve.tensor_scalar(o_hi[:, n, :, :], o_t[:, :, :], MAGIC, None,
                                          ALU.subtract).then_inc(s_oh, 1)
                        dve.wait_ge(s_oh, g + 1)
                        dve.scalar_tensor_tensor(out=o_lo[:, n, :, :], in0=o_t[:, :, :], scalar=MAGIC,
                                                 in1=o_hi[:, n, :, :], op0=ALU.subtract,
                                                 op1=ALU.subtract).then_inc(s_olo, 1)

                    def add(g, q, n, first):
                        dve.wait_ge(s_xl2[n], 16 * (q + 1))
                        if not first:
                            dve.wait_ge(s_yw[n], 16 * q)
                        for t in range(GT):
                            dve.wait_ge(s_down, g * GT + (t + 1))
                            dve.scalar_tensor_tensor(out=y[:, n, t, :], in0=banks[GT * n + t][:, 0:D],
                                                     scalar=st(S_O), in1=x2_in[:, n, t // NT, t % NT, :],
                                                     op0=ALU.mult, op1=ALU.add).then_inc(s_y, 1)

                    split(0, 0, 0, True)
                    split(1, 0, 1, True)
                    add(0, 0, 0, True)
                    split(2, 1, 0, False)
                    add(1, 0, 1, True)
                    with dve.Fori(1, NG // 2 - 1, 1) as q:
                        split(q * 2 + 1, q, 1, False)
                        add(q * 2, q, 0, False)
                        split(q * 2 + 2, q + 1, 0, False)
                        add(q * 2 + 1, q, 1, False)
                    split(NG - 1, NG // 2 - 1, 1, False)
                    add(NG - 2, NG // 2 - 1, 0, False)
                    add(NG - 1, NG // 2 - 1, 1, False)

                @block.tensor
                def _(pe):
                    def body(g, q, n, first):
                        pe.wait_ge(s_olo, g + 1)
                        for t in range(GT):
                            if not first:
                                pe.wait_ge(s_y, (g - 2) * GT + (t + 1))
                            bank = banks[GT * n + t][:, 0:D]
                            for m in range(NM):
                                hi = o_hi[:, n, m, t * P:(t + 1) * P]
                                lo = o_lo[:, n, m, t * P:(t + 1) * P]
                                pe.matmul(bank, hi, w_down_t[:, m, 0, :], start=m == 0, stop=False)
                                pe.matmul(bank, lo, w_down_t[:, m, 0, :], start=False, stop=False)
                                last = pe.matmul(bank, hi, w_down_t[:, m, 1, :], start=False, stop=m == NM - 1)
                            last.then_inc(s_down, 1)

                    pairs(pe, body)


_SELF = ["L0_attn_Wq", "L0_attn_Wk", "L0_attn_Wv", "L0_attn_Wo"]
_SELF_B = ["L0_attn_bq", "L0_attn_bk", "L0_attn_bv", "L0_attn_bo"]
_CROSS = ["L0_xattn_Wq", "L0_xattn_Wk", "L0_xattn_Wv", "L0_xattn_Wo"]
_CROSS_B = ["L0_xattn_bq", "L0_xattn_bk", "L0_xattn_bv", "L0_xattn_bo"]
_FFN = ["L0_ffn_w_gate", "L0_ffn_w_up", "L0_ffn_w_down"]


def kernel(**inputs):
    import numpy as _np
    import concourse.bacc as _bacc
    from concourse import mybir as _mybir
    from concourse.bass_utils import run_bass_kernel_spmd as _run

    nc = _bacc.Bacc("TRN2", target_bir_lowering=False, num_devices=1)
    arrays, aps = {}, {}
    for name in ["x", "ctx_1024", "mask_1x1xSxS2_fk1"] + _SELF + _SELF_B + _CROSS + _CROSS_B + _FFN:
        a = _np.ascontiguousarray(inputs[name])
        arrays[f"in_{name}_dram"] = a
        aps[name] = nc.dram_tensor(f"in_{name}_dram", a.shape, _mybir.dt.from_np(a.dtype), kind="ExternalInput").ap()
    out = nc.dram_tensor("out_0_dram", (BATCH, SEQ, D), _mybir.dt.float32, kind="ExternalOutput").ap()
    decoder_kernel(nc, aps["x"], aps["ctx_1024"], aps["mask_1x1xSxS2_fk1"],
                   [aps[n] for n in _SELF], [aps[n] for n in _SELF_B],
                   [aps[n] for n in _CROSS], [aps[n] for n in _CROSS_B],
                   *[aps[n] for n in _FFN], out)
    r = _run(nc, [arrays], core_ids=[0])
    return r.results[0]["out_0_dram"]
```

```python
from contextlib import ExitStack, nullcontext

import concourse.bass as bass
from concourse import mybir

F32 = mybir.dt.float32
F16 = mybir.dt.float16
I32 = mybir.dt.int32
BF16 = mybir.dt.bfloat16
ALU = mybir.AluOpType
ACT = mybir.ActivationFunctionType
AX = mybir.AxisListType
RMAX = bass.bass_isa.ReduceOp.max

P = 128
BATCH, SEQ, D = 32, 256, 256
HEADS = 16
HD = D // HEADS
NC = D // P
NT = SEQ // P
HU = 4
GROUPS = HEADS // HU
HALF = HU * HD
UNITS = NT * HEADS // HU
WIN = 64
CTX = 120
FF = 768
NM = FF // P
QBLOCK = 32
TOK = BATCH * SEQ
GRP = 512
NG = TOK // GRP
EPS = 1e-5

XN = 256.0
WS = 256.0
QK = 8.0
VS = 64.0
LOGIT = 1.0 / (QK * QK * HD ** 0.5)
SHIFT = 10.0
NEG = -1e30
MASK_SCALE = -1e9
MAGIC = 1.5 * 2.0 ** 23
QMAX = 32767.0
TINY = 1e-12
SIG = 65536.0
NEG_BOUND = -0.3

LOAD, PREP, SELF, MID, CROSS, END = 2, 1, 0, -1, -2, -3
JOBS = [["P1", "X1"], ["P3"], ["P2"], ["B1", "D1"], ["X2", "B2"], ["D2"], ["P4", "B3"], ["B4", "D3"]]
ORDER = [j for slot in JOBS for j in slot]
STAGE = {"P": PREP, "B": MID, "X": MID, "D": END}
BLOCKS_FROM = 3
FIRST_IT, LAST_IT = -LOAD, BATCH - 1 - END
LOOP_FROM, LOOP_TO = 4, BATCH - LOAD


class Iteration:

    def __init__(self, pair, parity):
        self.pair, self.parity = pair, parity
        self.i, self.fixed = pair * 2 + parity, isinstance(pair, int)

    def has(self, off):
        return not self.fixed or 0 <= self.i + off < BATCH

    def batch(self, off):
        return self.i + off

    def par(self, off):
        return (self.parity + off) % 2

    def nth(self, off):
        return self.pair + (self.parity + off) // 2


def pipeline(eng, body):
    for i in range(FIRST_IT, LOOP_FROM):
        body(Iteration(i // 2, i % 2))
    with eng.Fori(LOOP_FROM // 2, LOOP_TO // 2, 1) as pair:
        body(Iteration(pair, 0))
        body(Iteration(pair, 1))
    for i in range(LOOP_TO, LAST_IT + 1):
        body(Iteration(i // 2, i % 2))


def lag(stage, k, d):
    return (stage, k - d) if k >= d else (stage - 1, k - d + UNITS)


BANK_JOBS = [["P1", "P3", "B1", "X2", "D2", "B3", "D3"], ["X1", "P2", "D1", "B2", "P4", "B4"]]


def job_before(it, job):
    jobs = BANK_JOBS[0] if job in BANK_JOBS[0] else BANK_JOBS[1]
    n = jobs.index(job)
    for back in range(1, 8 * len(jobs)):
        name = jobs[(n - back) % len(jobs)]
        stage = STAGE[name[0]] + (n - back) // len(jobs)
        if it.has(stage):
            return name, stage
    return None


def decoder_kernel(nc, x, ctx_in, mask, w_self, b_self, w_cross, b_cross, w_gate, w_up, w_down, out):
    x_d = x.rearrange("b (t p) d -> b p t d", p=P)
    out_g = out.rearrange("b (t p) d -> (b t) p d", p=P)
    x1_d = nc.dram_tensor("x1_scratch", [BATCH, P, NT, D], F32, kind="Internal").ap()
    x2_d = nc.dram_tensor("x2_scratch", [BATCH, P, NT, D], F32, kind="Internal").ap()
    h_d = nc.dram_tensor("h_scratch", [BATCH, P, NC, SEQ], F32, kind="Internal").ap()
    raw_d = nc.dram_tensor("raw_scratch", [2, NG, NM, P, GRP], F32, kind="Internal").ap()
    o_d = nc.dram_tensor("o_scratch", [NG, NM, P, GRP], F32, kind="Internal").ap()

    top = ExitStack()
    with top:
        def sb(name, shape, dt=F32, ctx=top):
            return ctx.enter_context(nc.sbuf_tensor(name, shape, dt))

        def sem(name):
            return top.enter_context(nc.semaphore(name))

        banks = [top.enter_context(nc.psum_tensor(f"bank{n}", [P, 512], F32)) for n in range(8)]

        ident = sb("ident", [P, P])
        w_down_t = sb("w_down_t", [P, NM, 2, D], F16)
        stats = sb("stats", [P, 24])
        magic = sb("magic", [P, 1])
        minus_magic = sb("minus_magic", [P, 1])
        needed = sb("needed", [P, 1], I32)
        S_H, I_H, S_U, C_U, S_G, C_G, S_P, C_P, S_O, C_O, RED, ALL, REAL, TOP, TSIG = range(15)

        def st(n):
            return stats[:, n:n + 1]

        mid = top.enter_context(ExitStack())
        w_gu_t = sb("w_gu_t", [P, NC, 2, 2 * FF], F16, mid)
        h_max = sb("h_max", [P, BATCH], F32, mid)

        att = top.enter_context(ExitStack())
        names = ["self_q", "self_k", "self_v", "self_o", "cross_q", "cross_k", "cross_v", "cross_o"]
        SQ, SK, SV, SO, CQ, CK, CV, CO = range(8)
        w16 = sb("w16", [P, 8, NC, 2, D], F16, att)
        bias16 = sb("bias16", [64, 8, D], F16, att)
        ones16 = sb("ones16", [64, 2, SEQ], F16, att)
        ident_b = sb("ident_b", [P, P], BF16, att)
        mask_b = sb("mask_b", [P, NT, P], BF16, att)
        mask_c = sb("mask_c", [P, NT, CTX], F32, att)
        k_blk = sb("k_blk", [P, 2, GROUPS, HU, WIN + SEQ], F16, att)
        k2_blk = sb("k2_blk", [P, 2, GROUPS, HU, CTX], F16, att)
        head_rows = sb("head_rows", [P, HU], F32, att)
        heads16 = sb("heads16", [P, 2 * HU], F32, att)
        half = sb("half", [P, NT], F32, att)
        s_wload = sem("weights_loaded")
        s_pool = sem("pool_chain")
        s_const = sem("constants_ready")
        s_dve = sem("dve_chain")
        s_wq = sem("ffn_weight_dequantised")
        s_wt = sem("ffn_weight_transposed")
        s_we = sem("ffn_weight_evacuated")

        with ExitStack() as c0:
            w_raw = sb("w_raw", [P, 8, NC, D], F32, c0)
            b_raw = sb("b_raw", [64, 8, D], F32, c0)
            f_raw = sb("f_raw", [P, 3, 2 * FF], F32, c0)
            f_amax = sb("f_amax", [P, 3, 48], F32, c0)
            f_rec = sb("f_rec", [P, 3, 48], F32, c0)
            tmp_b = sb("tmp_b", [P, P], BF16, c0)
            block = c0.enter_context(nc.Block())

            @block.sync
            def _(sp):
                for n, w in enumerate(w_self + w_cross):
                    sp.dma_start(w_raw[:, n, :, :], w.rearrange("(c p) n -> p c n", p=P)).then_inc(s_wload, 16)
                for n, b in enumerate(b_self + b_cross):
                    row = b.rearrange("(a n) -> a n", a=1)
                    sp.dma_start(b_raw[0:1, n, :], row).then_inc(s_wload, 16)
                    sp.dma_start(b_raw[32:33, n, :], row).then_inc(s_wload, 16)
                for n, w in enumerate((w_up, w_gate)):
                    sp.dma_start(f_raw[:, n, :].rearrange("p (m k) -> p m k", m=NM),
                                 w.rearrange("(m p) k -> p m k", p=P)).then_inc(s_wload, 16)
                sp.dma_start(f_raw[:, 2, :].rearrange("p (r k) -> p r k", r=NC),
                             w_down.rearrange("(r p) k -> p r k", p=P)).then_inc(s_wload, 16)
                sp.dma_start(mask_c[:, :, :],
                             mask.rearrange("a b (t p) k -> p (a b t) k", p=P)).then_inc(s_wload, 16)

            LOADED = 16 * (8 + 16 + 3 + 1)

            @block.gpsimd
            def _(pool):
                n = [0]

                def step(ins):
                    n[0] += 1
                    ins.then_inc(s_pool, 1)
                    pool.wait_ge(s_pool, n[0])

                step(pool.memset(ident[:, :], 0.0))
                step(pool.affine_select(out=ident[:, :], in_=ident[:, :], compare_op=ALU.not_equal, fill=1.0,
                                        base=0, pattern=[[-1, P]], channel_multiplier=1))
                step(pool.tensor_copy(ident_b[:, :], ident[:, :]))
                step(pool.memset(half[:, :], -0.5))
                step(pool.memset(heads16[:, :], 1.0))
                step(pool.affine_select(out=heads16[:, :], in_=heads16[:, :], compare_op=ALU.is_ge, fill=0.0,
                                        base=0, pattern=[[-HD, 2 * HU]], channel_multiplier=1))
                step(pool.affine_select(out=heads16[:, :], in_=heads16[:, :], compare_op=ALU.is_gt, fill=0.0,
                                        base=HD, pattern=[[HD, 2 * HU]], channel_multiplier=-1))
                step(pool.tensor_tensor(head_rows[:, :], heads16[:, 0:HU], heads16[:, HU:2 * HU], ALU.add))
                for m, base in ((mask_b[:, 0, :], 0), (tmp_b[:, :], WIN)):
                    step(pool.memset(m, 0.0))
                    step(pool.affine_select(out=m, in_=m, compare_op=ALU.is_gt, fill=NEG,
                                            base=base, pattern=[[1, P]], channel_multiplier=-1))
                    step(pool.affine_select(out=m, in_=m, compare_op=ALU.is_ge, fill=NEG,
                                            base=WIN - base, pattern=[[-1, P]], channel_multiplier=1))
                step(pool.tensor_copy(mask_b[64:128, 0, :], tmp_b[64:128, :]))
                step(pool.tensor_copy(mask_b[:, 1, :], mask_b[:, 0, :]))
                pool.memset(mask_b[0:64, 0, 0:WIN], NEG).then_inc(s_const, 1)
                step(pool.memset(k_blk[:, :, :, :, 0:WIN].rearrange("p a g h n -> p (a g h) n"), 0.0))

            @block.vector
            def _(dve):
                n = [0]

                def step(ins):
                    n[0] += 1
                    ins.then_inc(s_dve, 1)
                    dve.wait_ge(s_dve, n[0])

                step(dve.memset(bias16[:, :, :], 0.0))
                step(dve.memset(ones16[:, 0, :], XN))
                step(dve.memset(ones16[:, 1, :], VS))
                dve.wait_ge(s_wload, LOADED)
                step(dve.tensor_scalar(mask_c[:, :, :], mask_c[:, :, :], MASK_SCALE, None, ALU.mult))
                for hl in range(2):
                    row = slice(32 * hl, 32 * hl + 1)
                    step(dve.tensor_scalar(bias16[row, :, :], b_raw[row, :, :], WS, None, ALU.mult))
                lo = slice(32, 33)
                step(dve.scalar_tensor_tensor(out=bias16[lo, :, :], in0=b_raw[lo, :, :], scalar=WS,
                                              in1=bias16[lo, :, :], op0=ALU.mult, op1=ALU.subtract))
                for k in range(8):
                    step(dve.tensor_scalar(w16[:, k, :, 0, :], w_raw[:, k, :, :], WS, None, ALU.mult))
                    step(dve.scalar_tensor_tensor(out=w16[:, k, :, 1, :], in0=w_raw[:, k, :, :], scalar=WS,
                                                  in1=w16[:, k, :, 0, :], op0=ALU.mult, op1=ALU.subtract))
                blocks = f_raw[:, :, :].rearrange("p a (n k) -> p (a n) k", k=QBLOCK)
                amax = f_amax[:, :, :].rearrange("p a n -> p (a n)")
                rec = f_rec[:, :, :].rearrange("p a n -> p (a n)")
                wide = [P, 3 * 48, QBLOCK]
                step(dve.tensor_reduce(out=amax, in_=blocks, axis=AX.X, op=ALU.max, apply_absolute_value=True))
                step(dve.tensor_scalar(amax, amax, 1.0 / 7.0, TINY, ALU.mult, ALU.max))
                step(dve.reciprocal(rec, amax))
                step(dve.tensor_tensor(blocks, blocks, rec.unsqueeze(2).to_broadcast(wide), ALU.mult))
                step(dve.tensor_scalar(f_raw[:, :, :], f_raw[:, :, :], MAGIC, MAGIC, ALU.add, ALU.subtract))
                dve.tensor_tensor(blocks, blocks, amax.unsqueeze(2).to_broadcast(wide), ALU.mult).then_inc(s_wq, 1)
                for q in range(9):
                    dve.wait_ge(s_wt, q + 1)
                    bank = banks[q % 8]
                    if q < 6:
                        a, m0 = q // 3, 2 * (q % 3)
                        for hl in range(2):
                            dst = w_gu_t[:, :, hl, a * FF + m0 * P:a * FF + (m0 + 2) * P]
                            src = bank[:, :].rearrange("p (c k) -> p c k", c=NC)
                            hi = w_gu_t[:, :, 0, a * FF + m0 * P:a * FF + (m0 + 2) * P]
                            if hl == 0:
                                step(dve.tensor_scalar(dst, src, WS, None, ALU.mult))
                            else:
                                step(dve.scalar_tensor_tensor(out=dst, in0=src, scalar=WS, in1=hi,
                                                              op0=ALU.mult, op1=ALU.subtract))
                    else:
                        m0 = 2 * (q - 6)
                        src = bank[:, :].rearrange("p (m k) -> p m k", m=2)
                        hi, low = w_down_t[:, m0:m0 + 2, 0, :], w_down_t[:, m0:m0 + 2, 1, :]
                        step(dve.tensor_scalar(hi, src, WS, None, ALU.mult))
                        step(dve.scalar_tensor_tensor(out=low, in0=src, scalar=WS, in1=hi,
                                                      op0=ALU.mult, op1=ALU.subtract))
                    dve.sem_inc(s_we, 1)

            @block.tensor
            def _(pe):
                pe.wait_ge(s_const, 1)
                pe.wait_ge(s_wq, 1)
                for q in range(9):
                    if q >= 8:
                        pe.wait_ge(s_we, q - 7)
                    for j in range(4):
                        if q < 6:
                            a, m, c = q // 3, 2 * (q % 3) + j % 2, j // 2
                            src = f_raw[:, a, m * D + c * P:m * D + (c + 1) * P]
                        else:
                            m, r = 2 * (q - 6) + j // 2, j % 2
                            src = f_raw[:, 2, r * FF + m * P:r * FF + (m + 1) * P]
                        last = pe.transpose(banks[q % 8][:, j * P:(j + 1) * P], src, ident[:, :])
                    last.then_inc(s_wt, 1)

        a = att
        x_in = sb("x_in", [P, 2, NT, D], F32, a)
        xn = sb("xn", [P, NT, D], F32, a)
        xn_t = sb("xn_t", [P, NC, 2, SEQ], F16, a)
        q_hi = sb("q_hi", [P, NC, SEQ], F16, a)
        q_lo = sb("q_lo", [P, 2, NC, SEQ], F16, a)
        q_dup = sb("q_dup", [P, 2, GROUPS, SEQ], F16, a)
        k_t = sb("k_t", [P, NC, 2, SEQ], F16, a)
        k_both = sb("k_both", [P, GROUPS, SEQ], F16, a)
        k2_both = sb("k2_both", [P, GROUPS, CTX], F16, a)
        v = sb("v", [P, 2, 2, NT, HEADS, 2 * HD + 1], F16, a)
        x_mid = sb("x_mid", [P, NT, D], F32, a)
        x1 = sb("x1", [P, NT, D], F32, a)
        xn2 = sb("xn2", [P, NT, D], F32, a)
        xn2_t = sb("xn2_t", [P, NC, 2, SEQ], F16, a)
        q2_hi = sb("q2_hi", [P, NC, SEQ], F16, a)
        q2_lo = sb("q2_lo", [P, 2, NC, SEQ], F16, a)
        q2_dup = sb("q2_dup", [P, 2, GROUPS, SEQ], F16, a)
        ctx_sb = sb("ctx_sb", [CTX, D], F32, a)
        ctx_t = sb("ctx_t", [P, NC, 2, CTX], F16, a)
        k2_t = sb("k2_t", [P, NC, 2, CTX], F16, a)
        v2_hi = sb("v2_hi", [CTX, 2, HEADS, HD + 1], F16, a)
        v2_lo = sb("v2_lo", [CTX, 2, HEADS, HD], F16, a)
        x1_back = sb("x1_back", [P, NT, D], F32, a)
        x2 = sb("x2", [P, NT, D], F32, a)
        h = sb("h", [P, NT, D], F32, a)
        h_t = sb("h_t", [P, NC, SEQ], F32, a)

        class Attention:

            def __init__(self, name, stage, keys, s_bank, t_bank, o_bank):
                self.stage, self.keys, self.cols = stage, keys, HU * keys
                self.s_bank, self.t_bank, self.o_bank = banks[s_bank], banks[t_bank], banks[o_bank]
                self.u = sb(f"{name}_u", [P, 2, HU * keys], F32, a)
                self.p32 = sb(f"{name}_p32", [P, 2, HU * P], F32, a)
                self.p_hi = sb(f"{name}_p_hi", [P, 4, HU * P], F16, a)
                self.p_lo = sb(f"{name}_p_lo", [P, 4, HU * P], F16, a)
                self.mx = sb(f"{name}_mx", [P, 2, HU], F32, a)
                self.mshift = sb(f"{name}_mshift", [P, 2, HU], F32, a)
                self.den = sb(f"{name}_den", [P, HEADS], F32, a)
                self.o = sb(f"{name}_o", [P, NT, D], F32, a)
                self.o_t = sb(f"{name}_o_t", [P, NC, 2, SEQ], F16, a)
                self.s_scores = sem(f"{name}_scores_done")
                self.s_max = sem(f"{name}_max_done")
                self.s_shift = sem(f"{name}_shift_done")
                self.s_u = sem(f"{name}_u_ready")
                self.s_t = sem(f"{name}_transposed")
                self.s_p32 = sem(f"{name}_p32_ready")
                self.s_hi = sem(f"{name}_p_hi_ready")
                self.s_lo = sem(f"{name}_p_lo_ready")
                self.s_pv = sem(f"{name}_pv_done")
                self.s_den = sem(f"{name}_den_ready")
                self.s_o = sem(f"{name}_o_ready")

        A = Attention("self", SELF, P, 0, 2, 4)
        C = Attention("cross", CROSS, CTX, 1, 3, 5)
        C.y = sb("cross_y", [P, 2, HU * CTX], F32, a)
        C.s_y = sem("cross_y_ready")
        job_bank = {j: banks[6 + n] for n in range(2) for j in BANK_JOBS[n]}
        s_job = {j: sem(f"job_{j}_products_done") for j in ORDER}
        s_hi = {j: sem(f"job_{j}_high_part_ready") for j in ORDER if j not in ("B2", "D2")}
        s_got = {j: sem(f"job_{j}_evacuated") for j in ORDER}

        class Norm:

            STEPS = 2 * NT + 1

            def __init__(self, name):
                self.part = sb(f"{name}_bn_part", [P, NT, 6], F32, a)
                self.mv = sb(f"{name}_mean_var", [P, NT, 2], F32, a)
                self.ve = sb(f"{name}_var_eps", [P, NT], F32, a)
                self.rstd = sb(f"{name}_rstd", [P, NT], F32, a)
                self.s_stats = sem(f"{name}_statistics_steps")
                self.s_seen = sem(f"{name}_bn_parts_complete")
                self.s_rstd = sem(f"{name}_rstd_ready")
                self.s_done = sem(f"{name}_normalised")

        LN1, LN2, LN3 = Norm("ln1"), Norm("ln2"), Norm("ln3")
        s_x = [sem(f"x_loaded_{n}") for n in range(2)]
        s_xm = sem("x_mid_loaded")
        s_ctx = sem("ctx_loaded")
        s_x1b = sem("x1_reloaded")
        s_x1w = sem("x1_stored")
        s_x2w = sem("x2_stored")
        s_hw = sem("h_stored")
        s_init = sem("attention_buffers_cleared")
        s_kblk = sem("k_block_diagonal_ready")
        s_k2blk = sem("k2_block_diagonal_ready")
        s_kboth = sem("k_parts_by_group")
        s_k2both = sem("k2_parts_by_group")
        s_qdup = sem("q_duplicated")
        s_q2dup = sem("q2_duplicated")
        s_vwin = sem("v_windows_ready")
        s_hmax = sem("h_max_ready")

        BLK, DUP, VCOPY = HU, 16 * 4, 16 * 2

        def unit(b, k):
            return b * UNITS + (k + 1)

        with nc.Block() as block:

            @block.sync
            def _(sp):
                def duplicate(dst, src, done):
                    for half_of_chunk in range(2):
                        rows = slice(HALF * half_of_chunk, HALF * (half_of_chunk + 1))
                        for side in range(2):
                            sp.dma_start(dst[HALF * side:HALF * (side + 1), half_of_chunk::2, :],
                                         src[rows, :, :]).then_inc(done, 16)

                def both_parts(dst, src, done):
                    for half_of_chunk in range(2):
                        rows = slice(HALF * half_of_chunk, HALF * (half_of_chunk + 1))
                        for part in range(2):
                            side = half_of_chunk if part == 0 else 1 - half_of_chunk
                            sp.dma_start(dst[HALF * side:HALF * (side + 1), half_of_chunk::2, :],
                                         src[rows, :, part, :]).then_inc(done, 16)

                def body(it):
                    if it.has(LOAD):
                        b = it.batch(LOAD)
                        if it.has(LOAD - 2):
                            sp.wait_ge(LN1.s_done, it.batch(LOAD - 2) + 1)
                        sp.dma_start(x_in[:, it.par(LOAD), :, :], x_d[b]).then_inc(s_x[it.par(LOAD)], 16)
                    if it.has(SELF):
                        b = it.batch(SELF)
                        if it.has(SELF - 1):
                            sp.wait_ge(s_job["X1"], it.batch(SELF - 1) + 1)
                        sp.dma_start(ctx_sb[:, :], ctx_in[b]).then_inc(s_ctx, 16)
                    if it.has(MID):
                        b = it.batch(MID)
                        if it.has(MID - 1):
                            sp.wait_ge(s_got["B2"], it.batch(MID - 1) + 1)
                        sp.dma_start(x_mid[:, :, :], x_d[b]).then_inc(s_xm, 16)
                    if it.has(END):
                        b = it.batch(END)
                        sp.wait_ge(s_x1w, 16 * (b + 1))
                        sp.dma_start(x1_back[:, :, :], x1_d[b]).then_inc(s_x1b, 16)
                    if it.has(PREP):
                        b = it.batch(PREP)
                        if it.has(PREP - 1):
                            sp.wait_ge(s_kblk, BLK * b)
                        sp.wait_ge(s_got["P3"], b + 1)
                        both_parts(k_both, k_t, s_kboth)
                    if it.has(MID):
                        b = it.batch(MID)
                        if it.has(MID - 1):
                            sp.wait_ge(s_k2blk, BLK * b)
                        sp.wait_ge(s_got["X2"], b + 1)
                        both_parts(k2_both, k2_t, s_k2both)
                    if it.has(PREP):
                        b, par = it.batch(PREP), it.par(PREP)
                        if it.has(PREP - 2):
                            sp.wait_ge(A.s_scores, unit(b - 2, UNITS - 1))
                        sp.wait_ge(s_hi["P2"], b + 1)
                        duplicate(q_dup[:, par], q_hi, s_qdup)
                    if it.has(MID):
                        b, par = it.batch(MID), it.par(MID)
                        sp.wait_ge(s_got["B2"], b + 1)
                        sp.dma_start(x1_d[b], x1[:, :, :]).then_inc(s_x1w, 16)
                    if it.has(END):
                        b = it.batch(END)
                        sp.wait_ge(s_got["D2"], b + 1)
                        sp.dma_start(x2_d[b], x2[:, :, :]).then_inc(s_x2w, 16)
                    if it.has(PREP):
                        b, par = it.batch(PREP), it.par(PREP)
                        sp.wait_ge(s_got["P4"], b + 1)
                        sp.dma_start(v[0:WIN, par, 1, 1, :, :], v[WIN:P, par, 0, 0, :, :]).then_inc(s_vwin, 16)
                        sp.dma_start(v[WIN:P, par, 1, :, :, :], v[0:WIN, par, 0, :, :, :]).then_inc(s_vwin, 16)
                    if it.has(END):
                        b = it.batch(END)
                        sp.wait_ge(s_hi["D3"], b + 1)
                        sp.dma_start(h_d[b], h_t[:, :, :]).then_inc(s_hw, 16)

                pipeline(sp, body)
                sp.wait_ge(s_x1w, 16 * BATCH)
                sp.wait_ge(s_x2w, 16 * BATCH)
                sp.wait_ge(s_hw, 16 * BATCH)

            @block.tensor
            def _(pe):
                def product(dst, lhs, rhs, first=True, last=True):
                    pe.matmul(dst, lhs[0], rhs[0], start=first, stop=False)
                    pe.matmul(dst, lhs[1], rhs[0], start=False, stop=False)
                    return pe.matmul(dst, lhs[0], rhs[1], start=False, stop=last)

                def parts(t):
                    return t(0), t(1)

                def project(dst, w, lhs_is_weight, act, cols, ones):
                    for c in range(NC):
                        wt = parts(lambda hl: w16[:, w, c, hl, cols])
                        at = parts(lambda hl: act(c, hl))
                        product(dst, wt if lhs_is_weight else at, at if lhs_is_weight else wt,
                                first=c == 0, last=False)
                    b, o = bias16[:, w, cols], ones
                    return pe.matmul(dst, b if lhs_is_weight else o, o if lhs_is_weight else b,
                                     start=False, stop=True)

                def logits(dst, dup, low, keys, g, first):
                    c, side = divmod(g, 2)
                    rows = slice(HALF * side, HALF * (side + 1))
                    pe.matmul(dst, dup, keys[:, g, :, :], start=first, stop=False)
                    return pe.matmul(dst, low[rows, c, :], keys[rows, g, :, :], start=False, stop=True)

                def scores_self(it, k):
                    b, par = it.batch(SELF), it.par(SELF)
                    t, g = divmod(k, GROUPS)
                    if k == 0:
                        pe.wait_ge(s_got["P2"], b + 1)
                        pe.wait_ge(s_qdup, DUP * (b + 1))
                        pe.wait_ge(s_kblk, BLK * (b + 1))
                    if k or it.has(SELF - 1):
                        pe.wait_ge(A.s_u, unit(b, k - 1))
                    pe.matmul(A.s_bank[:, :], ident_b[:, :],
                              mask_b[:, t, :].unsqueeze(1).to_broadcast([P, HU, P]), start=True, stop=False)
                    for j in range(2):
                        w = 2 * t + j
                        tok = slice(t * P + WIN * j, t * P + WIN * (j + 1))
                        last = logits(A.s_bank[WIN * j:WIN * (j + 1), :], q_dup[:, par, g, tok],
                                      q_lo[:, par, :, tok], k_blk[:, par, :, :, WIN * w:WIN * w + P], g, False)
                    last.then_inc(A.s_scores, 1)

                def scores_cross(it, k):
                    b, par = it.batch(CROSS), it.par(CROSS)
                    t, g = divmod(k, GROUPS)
                    if k == 0:
                        pe.wait_ge(s_got["B4"], b + 1)
                        pe.wait_ge(s_q2dup, 4 * (b + 1))
                        pe.wait_ge(s_k2blk, BLK * (b + 1))
                    if k or it.has(CROSS - 1):
                        pe.wait_ge(C.s_y, unit(b, k - 1))
                    tok = slice(t * P, (t + 1) * P)
                    logits(C.s_bank[:, 0:HU * CTX], q2_dup[:, par, g, tok], q2_lo[:, par, :, tok],
                           k2_blk[:, par, :, :, :], g, True).then_inc(C.s_scores, 1)

                def transposes(att_, it, k):
                    off, kk = lag(att_.stage, k, 1)
                    if not it.has(off):
                        return
                    b = it.batch(off)
                    pe.wait_ge(att_.s_u, unit(b, kk))
                    if kk or it.has(off - 1):
                        pe.wait_ge(att_.s_hi, unit(b, kk - 1))
                        pe.wait_ge(att_.s_p32, unit(b, kk - 1))
                    n = att_.keys
                    for q in range(HU):
                        last = pe.transpose(att_.t_bank[0:n, q * P:(q + 1) * P],
                                            att_.u[:, kk % 2, q * n:(q + 1) * n], ident[:, :])
                    last.then_inc(att_.s_t, 1)

                def weighted_values(att_, it, k):
                    off, kk = lag(att_.stage, k, 3)
                    if not it.has(off):
                        return
                    b, par = it.batch(off), it.par(off)
                    t, g = divmod(kk, GROUPS)
                    if att_ is A and kk == 0:
                        pe.wait_ge(s_vwin, VCOPY * (b + 1))
                    pe.wait_ge(att_.s_hi, unit(b, kk))
                    pe.wait_ge(att_.s_lo, unit(b, kk))
                    if g == 0 and (t or it.has(off - 1)):
                        pe.wait_ge(att_.s_o, b * NT + t)
                    for q in range(HU):
                        hd = HU * g + q
                        for j in range(2 if att_ is A else 1):
                            rows = slice(WIN * j, WIN * (j + 1)) if att_ is A else slice(0, P)
                            cols = slice(q * P + rows.start, q * P + rows.stop)
                            if att_ is A:
                                vw = v[:, par, 1 - j, t, hd, :]
                                vh, vl = vw[:, 0:HD + 1], vw[:, HD + 1:]
                            else:
                                vh, vl = v2_hi[:, par, hd, :], v2_lo[:, par, hd, :]
                            hi = att_.p_hi[0:att_.keys, kk % 4, cols]
                            lo = att_.p_lo[0:att_.keys, kk % 4, cols]
                            dst = att_.o_bank[rows, hd * (HD + 1):(hd + 1) * (HD + 1)]
                            pe.matmul(dst, hi, vh, start=True, stop=False)
                            pe.matmul(dst[:, 0:HD], hi, vl, start=False, stop=False)
                            last = pe.matmul(dst, lo, vh, start=False, stop=True)
                    last.then_inc(att_.s_pv, 1)

                def transpose_tiles(bank, src):
                    for c in range(NC):
                        for t in range(NT):
                            last = pe.transpose(bank[:, c * SEQ + t * P:c * SEQ + (t + 1) * P],
                                                src[:, t, c * P:(c + 1) * P], ident[:, :])
                    return last

                def job(it, name):
                    off = STAGE[name[0]]
                    if not it.has(off):
                        return
                    b = it.batch(off)
                    bank = job_bank[name]
                    before = job_before(it, name)
                    if before:
                        pe.wait_ge(s_got[before[0]], it.batch(before[1]) + 1)
                    if name == "P1":
                        pe.wait_ge(LN1.s_done, b + 1)
                        last = transpose_tiles(bank, xn)
                    elif name in ("P2", "P3"):
                        if name == "P2":
                            pe.wait_ge(s_got["P1"], b + 1)
                        for m in range(NC):
                            last = project(bank[:, m * SEQ:(m + 1) * SEQ], SQ if name == "P2" else SK, True,
                                           lambda c, hl: xn_t[:, c, hl, :],
                                           slice(m * P, (m + 1) * P), ones16[:, 0, :])
                    elif name == "P4":
                        for t in range(NT):
                            last = project(bank[:, t * D:(t + 1) * D], SV, False,
                                           lambda c, hl: xn_t[:, c, hl, t * P:(t + 1) * P],
                                           slice(0, D), ones16[:, 0, 0:P])
                    elif name in ("B1", "D1"):
                        att_ = A if name == "B1" else C
                        pe.wait_ge(att_.s_o, NT * (b + 1))
                        last = transpose_tiles(bank, att_.o)
                    elif name in ("B2", "D2"):
                        att_ = A if name == "B2" else C
                        pe.wait_ge(s_got[name[0] + "1"], b + 1)
                        for t in range(NT):
                            last = project(bank[:, t * D:(t + 1) * D], SO if name == "B2" else CO, False,
                                           lambda c, hl: att_.o_t[:, c, hl, t * P:(t + 1) * P],
                                           slice(0, D), ones16[:, 1, 0:P])
                    elif name == "B3":
                        pe.wait_ge(LN2.s_done, b + 1)
                        last = transpose_tiles(bank, xn2)
                    elif name == "B4":
                        pe.wait_ge(s_got["B3"], b + 1)
                        for m in range(NC):
                            last = project(bank[:, m * SEQ:(m + 1) * SEQ], CQ, True,
                                           lambda c, hl: xn2_t[:, c, hl, :],
                                           slice(m * P, (m + 1) * P), ones16[:, 0, :])
                    elif name == "X1":
                        pe.wait_ge(s_ctx, 16 * (b + 1))
                        for c in range(NC):
                            last = pe.transpose(bank[:, c * CTX:(c + 1) * CTX], ctx_sb[:, c * P:(c + 1) * P],
                                                ident[0:CTX, 0:CTX])
                    elif name == "X2":
                        pe.wait_ge(s_got["X1"], b + 1)
                        for m in range(NC):
                            project(bank[:, m * CTX:(m + 1) * CTX], CK, True, lambda c, hl: ctx_t[:, c, hl, :],
                                    slice(m * P, (m + 1) * P), ones16[:, 1, 0:CTX])
                        last = project(bank[0:CTX, NC * CTX:NC * CTX + D], CV, False,
                                       lambda c, hl: ctx_t[:, c, hl, :], slice(0, D), ones16[:, 1, 0:CTX])
                    elif name == "D3":
                        pe.wait_ge(LN3.s_done, b + 1)
                        last = transpose_tiles(bank, h)
                    last.then_inc(s_job[name], 1)

                def body(it):
                    for k in range(UNITS):
                        if it.has(SELF):
                            scores_self(it, k)
                        if it.has(CROSS) and k:
                            scores_cross(it, k)
                        weighted_values(A, it, k)
                        weighted_values(C, it, k)
                        for name in JOBS[k]:
                            job(it, name)
                        if it.has(CROSS) and not k:
                            scores_cross(it, k)
                        transposes(A, it, k)
                        transposes(C, it, k)

                pe.wait_ge(s_init, 1)
                pipeline(pe, body)

            @block.scalar
            def _(act):
                def exps(att_, it, k):
                    off, kk = lag(att_.stage, k, 1)
                    if not it.has(off):
                        return
                    b, n = it.batch(off), att_.keys
                    act.wait_ge(att_.s_t, unit(b, kk))
                    if kk >= 4 or it.has(off - 1):
                        act.wait_ge(att_.s_pv, unit(b, kk - 4))
                    if kk >= 2 or it.has(off - 1):
                        act.wait_ge(att_.s_lo, unit(b, kk - 2))
                    act.activation(att_.p_hi[0:n, kk % 4, :], att_.t_bank[0:n, :], ACT.Exp).then_inc(att_.s_hi, 1)
                    act.activation(att_.p32[0:n, kk % 2, :], att_.t_bank[0:n, :], ACT.Exp).then_inc(att_.s_p32, 1)

                def cols(bank, n):
                    return bank[:, 0:NC * n].rearrange("p (c t) -> p c t", c=NC)

                def job(it, name):
                    off = STAGE[name[0]]
                    if not it.has(off) or name in ("B2", "D2"):
                        return
                    b, par, bank = it.batch(off), it.par(off), job_bank[name]
                    act.wait_ge(s_job[name], b + 1)
                    if name == "P1":
                        if it.has(off - 1):
                            act.wait_ge(s_job["P4"], b)
                        last = act.activation(xn_t[:, :, 0, :], cols(bank, SEQ), ACT.Copy)
                    elif name == "P2":
                        if it.has(off - 1):
                            act.wait_ge(s_qdup, DUP * b)
                            act.wait_ge(s_got["P2"], b)
                        last = act.activation(q_hi[:, :, :], cols(bank, SEQ), ACT.Copy, scale=QK / (XN * WS))
                    elif name == "P3":
                        if it.has(off - 1):
                            act.wait_ge(s_kboth, DUP * b)
                        last = act.activation(k_t[:, :, 0, :], cols(bank, SEQ), ACT.Copy, scale=QK / (XN * WS))
                    elif name == "P4":
                        if it.has(off - 2):
                            act.wait_ge(A.s_pv, unit(b - 2, UNITS - 1))
                        last = act.activation(v[:, par, 0, :, :, 0:HD],
                                              bank[:, :].rearrange("p (w h d) -> p w h d", w=2, h=HEADS),
                                              ACT.Copy, scale=VS / (XN * WS))
                    elif name in ("B1", "D1"):
                        att_ = A if name == "B1" else C
                        if it.has(off - 1):
                            act.wait_ge(s_job[name[0] + "2"], b)
                        last = act.activation(att_.o_t[:, :, 0, :], cols(bank, SEQ), ACT.Copy)
                    elif name == "B3":
                        if it.has(off - 1):
                            act.wait_ge(s_job["B4"], b)
                        last = act.activation(xn2_t[:, :, 0, :], cols(bank, SEQ), ACT.Copy)
                    elif name == "B4":
                        if it.has(off - 1):
                            act.wait_ge(s_q2dup, 4 * b)
                            act.wait_ge(s_got["B4"], b)
                        last = act.activation(q2_hi[:, :, :], cols(bank, SEQ), ACT.Copy, scale=QK / (XN * WS))
                    elif name == "X1":
                        if it.has(off - 1):
                            act.wait_ge(s_job["X2"], b)
                        last = act.activation(ctx_t[:, :, 0, :], cols(bank, CTX), ACT.Copy, scale=VS)
                    elif name == "X2":
                        if it.has(off - 1):
                            act.wait_ge(s_k2both, DUP * b)
                        if it.has(off - 2):
                            act.wait_ge(C.s_pv, unit(b - 2, UNITS - 1))
                        act.activation(k2_t[:, :, 0, :], cols(bank, CTX), ACT.Copy,
                                       scale=QK / (VS * WS)).then_inc(s_hi["X2"], 1)
                        last = act.activation(v2_hi[:, par, :, 0:HD],
                                              bank[0:CTX, NC * CTX:NC * CTX + D].rearrange("p (h d) -> p h d", h=HEADS),
                                              ACT.Copy, scale=VS / (VS * WS))
                    elif name == "D3":
                        if it.has(off - 1):
                            act.wait_ge(s_hw, 16 * b)
                        last = act.activation(h_t[:, :, :], cols(bank, SEQ), ACT.Copy)
                    last.then_inc(s_hi[name], 1)

                def duplicate_cross(it):
                    if not it.has(MID):
                        return
                    b, par = it.batch(MID), it.par(MID)
                    act.wait_ge(s_hi["B4"], b + 1)
                    if it.has(MID - 2):
                        act.wait_ge(C.s_scores, unit(b - 2, UNITS - 1))
                    for half_of_chunk in range(2):
                        rows = slice(HALF * half_of_chunk, HALF * (half_of_chunk + 1))
                        for side in range(2):
                            act.activation(q2_dup[HALF * side:HALF * (side + 1), par, half_of_chunk::2, :],
                                           q2_hi[rows, :, :], ACT.Copy).then_inc(s_q2dup, 1)

                def block_self(it, j):
                    if not it.has(PREP):
                        return
                    b, par = it.batch(PREP), it.par(PREP)
                    if j == 0:
                        act.wait_ge(s_kboth, DUP * (b + 1))
                        if it.has(PREP - 2):
                            act.wait_ge(A.s_scores, unit(b - 2, UNITS - 1))
                    act.activation(k_blk[:, par, :, j, WIN:WIN + SEQ], k_both[:, :, :], ACT.Copy,
                                   scale=head_rows[:, j:j + 1]).then_inc(s_kblk, 1)

                def block_cross(it, j):
                    if not it.has(MID):
                        return
                    b, par = it.batch(MID), it.par(MID)
                    if j == 0:
                        act.wait_ge(s_k2both, DUP * (b + 1))
                        if it.has(MID - 2):
                            act.wait_ge(C.s_scores, unit(b - 2, UNITS - 1))
                    act.activation(k2_blk[:, par, :, j, :], k2_both[:, :, :], ACT.Copy,
                                   scale=head_rows[:, j:j + 1]).then_inc(s_k2blk, 1)

                def body(it):
                    for k in range(UNITS):
                        if k == 7:
                            block_cross(it, 3)
                        for name in JOBS[k]:
                            job(it, name)
                        if k == 7:
                            duplicate_cross(it)
                        exps(A, it, k)
                        exps(C, it, k)
                        if BLOCKS_FROM <= k < BLOCKS_FROM + HU:
                            block_self(it, k - BLOCKS_FROM)
                        for j in {5: [0], 6: [1, 2]}.get(k, []):
                            block_cross(it, j)

                act.wait_ge(s_init, 1)
                pipeline(act, body)

            @block.vector
            def _(dve):
                def wide(v, n):
                    return v.unsqueeze(2).to_broadcast([P, HU, n])

                def shifts(it, k):
                    r, t = k % 2, k // (UNITS // NT)
                    both = it.has(SELF), it.has(CROSS)
                    b, b2 = it.batch(SELF), it.batch(CROSS)
                    s3 = A.s_bank[:, :].rearrange("p (h n) -> p h n", h=HU)
                    y3 = C.y[:, r, :].rearrange("p (h n) -> p h n", h=HU)
                    if both[0]:
                        dve.wait_ge(A.s_scores, unit(b, k))
                        dve.tensor_reduce(out=A.mx[:, r, :], in_=s3, axis=AX.X, op=ALU.max).then_inc(A.s_max, 1)
                    if both[1]:
                        dve.wait_ge(C.s_scores, unit(b2, k))
                        if k >= 2 or it.has(CROSS - 1):
                            dve.wait_ge(C.s_u, unit(b2, k - 2))
                        dve.scalar_tensor_tensor(out=y3,
                                                 in0=C.s_bank[:, 0:HU * CTX].rearrange("p (h n) -> p h n", h=HU),
                                                 scalar=LOGIT,
                                                 in1=mask_c[:, t, :].unsqueeze(1).to_broadcast([P, HU, CTX]),
                                                 op0=ALU.mult, op1=ALU.add).then_inc(C.s_y, 1)
                    if both[0]:
                        dve.wait_ge(A.s_max, unit(b, k))
                        dve.tensor_scalar(A.mshift[:, r, :], A.mx[:, r, :], LOGIT, SHIFT,
                                          ALU.mult, ALU.subtract).then_inc(A.s_shift, 1)
                    if both[1]:
                        dve.wait_ge(C.s_y, unit(b2, k))
                        dve.tensor_reduce(out=C.mx[:, r, :], in_=y3, axis=AX.X, op=ALU.max).then_inc(C.s_max, 1)
                    if both[0]:
                        dve.wait_ge(A.s_shift, unit(b, k))
                        if k >= 2 or it.has(SELF - 1):
                            dve.wait_ge(A.s_t, unit(b, k - 2))
                        dve.scalar_tensor_tensor(out=A.u[:, r, :].rearrange("p (h n) -> p h n", h=HU), in0=s3,
                                                 scalar=LOGIT, in1=wide(A.mshift[:, r, :], P),
                                                 op0=ALU.mult, op1=ALU.subtract).then_inc(A.s_u, 1)
                    if both[1]:
                        dve.wait_ge(C.s_max, unit(b2, k))
                        dve.tensor_scalar(C.mshift[:, r, :], C.mx[:, r, :], SHIFT, None,
                                          ALU.subtract).then_inc(C.s_shift, 1)

                def normalise(it, k):
                    todo = []
                    for att_, job_name in ((A, "B1"), (C, "D1")):
                        off, kk = lag(att_.stage, k, 3)
                        if it.has(off) and kk % (UNITS // NT) == UNITS // NT - 1:
                            todo.append((att_, job_name, off, it.batch(off), kk // (UNITS // NT), kk))
                    o3 = {att_: att_.o_bank[:, 0:HEADS * (HD + 1)].rearrange("p (h d) -> p h d", h=HEADS)
                          for att_ in (A, C)}
                    for att_, job_name, off, b, t, kk in todo:
                        dve.wait_ge(att_.s_pv, unit(b, kk))
                        dve.reciprocal(att_.den[:, :], o3[att_][:, :, HD]).then_inc(att_.s_den, 1)
                    for att_, job_name, off, b, t, kk in todo:
                        dve.wait_ge(att_.s_den, b * NT + (t + 1))
                        if it.has(off - 1):
                            dve.wait_ge(s_job[job_name], b)
                        dve.tensor_tensor(att_.o[:, t, :].rearrange("p (h d) -> p h d", h=HEADS),
                                          o3[att_][:, :, 0:HD],
                                          att_.den[:, :].unsqueeze(2).to_broadcast([P, HEADS, HD]),
                                          ALU.mult).then_inc(att_.s_o, 1)

                def statistics(ln, src, b, scale):
                    for t in range(NT):
                        dve.bn_stats(ln.part[:, t, :], src[:, t, :]).then_inc(ln.s_stats, 1)
                    dve.wait_ge(ln.s_stats, ln.STEPS * b + NT)
                    dve.sem_inc(ln.s_seen, 1)
                    for t in range(NT):
                        dve.bn_aggr(ln.mv[:, t, :], ln.part[:, t, :]).then_inc(ln.s_stats, 1)
                    dve.wait_ge(ln.s_stats, ln.STEPS * b + 2 * NT)
                    dve.tensor_scalar(ln.ve[:, :], ln.mv[:, :, 1], EPS, 1.0 / scale ** 2,
                                      ALU.add, ALU.mult).then_inc(ln.s_stats, 1)

                def apply_norm(ln, dst, src, b):
                    dve.wait_ge(ln.s_rstd, b + 1)
                    for t in range(NT):
                        last = dve.tensor_scalar(dst[:, t, :], src[:, t, :], ln.mv[:, t, 0:1], ln.rstd[:, t:t + 1],
                                                 ALU.subtract, ALU.mult)
                    last.then_inc(ln.s_done, 1)

                def cols(bank, n):
                    return bank[:, 0:NC * n].rearrange("p (c t) -> p c t", c=NC)

                def low(dst, src, hi, scale):
                    return dve.scalar_tensor_tensor(out=dst, in0=src, scalar=scale, in1=hi,
                                                    op0=ALU.mult, op1=ALU.subtract)

                def job(it, name):
                    off = STAGE[name[0]]
                    if not it.has(off):
                        return
                    b, par, bank = it.batch(off), it.par(off), job_bank[name]
                    if name in ("B2", "D2"):
                        dve.wait_ge(s_job[name], b + 1)
                    else:
                        dve.wait_ge(s_hi[name], (2 * b + 2) if name == "X2" else (b + 1))
                    if name == "P1":
                        last = low(xn_t[:, :, 1, :], cols(bank, SEQ), xn_t[:, :, 0, :], 1.0)
                    elif name == "P2":
                        if it.has(off - 2):
                            dve.wait_ge(A.s_scores, unit(b - 2, UNITS - 1))
                        last = low(q_lo[:, par, :, :], cols(bank, SEQ), q_hi[:, :, :], QK / (XN * WS))
                    elif name == "P3":
                        last = low(k_t[:, :, 1, :], cols(bank, SEQ), k_t[:, :, 0, :], QK / (XN * WS))
                    elif name == "P4":
                        last = low(v[:, par, 0, :, :, HD + 1:].rearrange("p t h d -> p (t h) d"),
                                   bank[:, :].rearrange("p (g d) -> p g d", d=HD),
                                   v[:, par, 0, :, :, 0:HD].rearrange("p t h d -> p (t h) d"), VS / (XN * WS))
                    elif name in ("B1", "D1"):
                        o_t = (A if name == "B1" else C).o_t
                        last = low(o_t[:, :, 1, :], cols(bank, SEQ), o_t[:, :, 0, :], 1.0)
                    elif name in ("B2", "D2"):
                        src, dst = (x_mid, x1) if name == "B2" else (x1_back, x2)
                        dve.wait_ge(s_xm if name == "B2" else s_x1b, 16 * (b + 1))
                        if it.has(off - 1):
                            dve.wait_ge(s_x1w if name == "B2" else s_x2w, 16 * b)
                        last = dve.scalar_tensor_tensor(out=dst[:, :, :],
                                                        in0=bank[:, :].rearrange("p (t d) -> p t d", t=NT),
                                                        scalar=1.0 / (VS * WS), in1=src[:, :, :],
                                                        op0=ALU.mult, op1=ALU.add)
                    elif name == "B3":
                        last = low(xn2_t[:, :, 1, :], cols(bank, SEQ), xn2_t[:, :, 0, :], 1.0)
                    elif name == "B4":
                        if it.has(off - 2):
                            dve.wait_ge(C.s_scores, unit(b - 2, UNITS - 1))
                        last = low(q2_lo[:, par, :, :], cols(bank, SEQ), q2_hi[:, :, :], QK / (XN * WS))
                    elif name == "X1":
                        last = low(ctx_t[:, :, 1, :], cols(bank, CTX), ctx_t[:, :, 0, :], VS)
                    elif name == "X2":
                        low(v2_lo[:, par, :, :],
                            bank[0:CTX, NC * CTX:NC * CTX + D].rearrange("p (h d) -> p h d", h=HEADS),
                            v2_hi[:, par, :, 0:HD], VS / (VS * WS))
                        last = low(k2_t[:, :, 1, :], cols(bank, CTX), k2_t[:, :, 0, :], QK / (VS * WS))
                    elif name == "D3":
                        last = dve.tensor_reduce(out=h_max[:, bass.ds(b, 1)], in_=bank[:, :], axis=AX.X, op=ALU.max,
                                                 apply_absolute_value=True)
                    last.then_inc(s_got[name], 1)
                    if name in ("B2", "D2"):
                        dve.wait_ge(s_got[name], b + 1)
                        if name == "B2":
                            statistics(LN2, x1, b, XN)
                        else:
                            statistics(LN3, x2, b, 1.0)

                def body(it):
                    for k in range(UNITS):
                        shifts(it, k)
                        normalise(it, k)
                        for name in JOBS[k]:
                            job(it, name)
                        if k == 3 and it.has(LOAD):
                            b = it.batch(LOAD)
                            dve.wait_ge(s_x[it.par(LOAD)], 16 * (it.nth(LOAD) + 1))
                            statistics(LN1, x_in[:, it.par(LOAD), :, :], b, XN)
                        if k == 7 and it.has(LOAD):
                            b = it.batch(LOAD)
                            if it.has(LOAD - 1):
                                dve.wait_ge(s_job["P1"], b)
                            apply_norm(LN1, xn, x_in[:, it.par(LOAD), :, :], b)
                        if k == 5 and it.has(MID):
                            b = it.batch(MID)
                            if it.has(MID - 1):
                                dve.wait_ge(s_job["B3"], b)
                            apply_norm(LN2, xn2, x1, b)
                        if k == 6 and it.has(END):
                            b = it.batch(END)
                            if it.has(END - 1):
                                dve.wait_ge(s_job["D3"], b)
                            apply_norm(LN3, h, x2, b)

                dve.memset(v[0:WIN, :, 1, 0, :, :], 0.0)
                for n in range(2):
                    dve.memset(v[:, n, 0, :, :, HD:HD + 1].rearrange("p t h d -> p (t h) d"), 1.0)
                dve.memset(v2_hi[:, :, :, HD:HD + 1].rearrange("p a h d -> p (a h) d"), 1.0).then_inc(s_init, 1)
                pipeline(dve, body)

            @block.gpsimd
            def _(pool):
                def rstd(ln, b):
                    pool.wait_ge(ln.s_stats, ln.STEPS * (b + 1))
                    pool.tensor_tensor(ln.rstd[:, :], ln.ve[:, :], half[:, :], ALU.pow).then_inc(ln.s_rstd, 1)

                def subtract_cross(it, k):
                    b, r = it.batch(CROSS), k % 2
                    pool.wait_ge(C.s_shift, unit(b, k))
                    if k >= 2 or it.has(CROSS - 1):
                        pool.wait_ge(C.s_t, unit(b, k - 2))
                    pool.tensor_tensor(C.u[:, r, :].rearrange("p (h n) -> p h n", h=HU),
                                       C.y[:, r, :].rearrange("p (h n) -> p h n", h=HU),
                                       C.mshift[:, r, :].unsqueeze(2).to_broadcast([P, HU, CTX]),
                                       ALU.subtract).then_inc(C.s_u, 1)

                def low_part(att_, it, k):
                    off, kk = lag(att_.stage, k, 2)
                    if not it.has(off):
                        return
                    b, n = it.batch(off), att_.keys
                    pool.wait_ge(att_.s_p32, unit(b, kk))
                    pool.wait_ge(att_.s_hi, unit(b, kk))
                    if kk >= 4 or it.has(off - 1):
                        pool.wait_ge(att_.s_pv, unit(b, kk - 4))
                    pool.tensor_tensor(att_.p_lo[0:n, kk % 4, :], att_.p32[0:n, kk % 2, :], att_.p_hi[0:n, kk % 4, :],
                                       ALU.subtract).then_inc(att_.s_lo, 1)

                def body(it):
                    for k in range(UNITS):
                        low_part(A, it, k)
                        low_part(C, it, k)
                        if it.has(CROSS):
                            subtract_cross(it, k)
                        if k == 4 and it.has(LOAD):
                            rstd(LN1, it.batch(LOAD))
                        if k == 5 and it.has(MID):
                            rstd(LN2, it.batch(MID))
                        if k == 6 and it.has(END):
                            rstd(LN3, it.batch(END))

                pipeline(pool, body)

        att.close()

        class Scales:

            def __init__(self, name):
                self.s_red = sem(f"{name}maximum_over_free_axis_ready")
                self.s_all = sem(f"{name}maximum_over_partitions_ready")
                self.s_scale = sem(f"{name}scales_ready")
                self.steps = self.reds = self.alls = 0

            def step(self, dve, ins):
                self.steps += 1
                ins.then_inc(self.s_scale, 1)
                dve.wait_ge(self.s_scale, self.steps)

            def quant_scale(self, dve, s_out, c_out):
                self.step(dve, dve.tensor_tensor(st(s_out), st(ALL), st(REAL), ALU.mult))
                self.step(dve, dve.tensor_scalar(st(s_out), st(s_out), 1.0 / QMAX, TINY, ALU.mult, ALU.max))
                self.step(dve, dve.reciprocal(st(c_out), st(s_out)))
                self.step(dve, dve.tensor_tensor(st(c_out), st(c_out), st(REAL), ALU.mult))

            def global_max(self, dve, src):
                self.reds += 1
                dve.tensor_reduce(out=st(RED), in_=src, axis=AX.X, op=ALU.max).then_inc(self.s_red, 1)
                dve.wait_ge(self.s_all, self.reds)

            def pool_max(self, pool):
                self.alls += 1
                pool.wait_ge(self.s_red, self.alls)
                pool.partition_all_reduce(st(ALL), st(RED), P, RMAX).then_inc(self.s_all, 1)

        main = Scales("")
        gate_pass = Scales("gate_pass_")

        with ExitStack() as c1:
            GB = GRP // SEQ
            h_in = sb("h_in", [P, 2, GB, NC, SEQ], F32, c1)
            xt = sb("xt", [P, 2, GB, NC, SEQ], F32, c1)
            x_hi = sb("x_hi", [P, 2, GB, NC, SEQ], F16, c1)
            x_lo = sb("x_lo", [P, 2, GB, NC, SEQ], F16, c1)
            s_hl = [sem(f"h_loaded_{n}") for n in range(2)]
            MB = NM // 2
            NB = 2 * NM // MB
            stage = sb("stage", [P, NB, MB, GRP], F32, c1)
            raw_max = sb("raw_max", [P, 2 * NM, NG], F32, c1)
            gate_top = sb("gate_top", [P, NM, NG], F32, c1)
            s_xt = sem("h_rounded")
            s_xh = sem("x_hi_ready")
            s_xl = sem("x_lo_ready")
            s_raw = sem("raw_product_done")
            s_copy = sem("raw_product_copied")
            s_rmax = sem("raw_product_maximum_ready")
            s_top = sem("gate_signed_maximum_ready")
            s_store = [sem(f"raw_stored_{n}") for n in range(NB)]
            M2 = 2 * NM

            with nc.Block() as block:

                @block.vector
                def _(dve):
                    main.step(dve, dve.memset(magic[:, :], MAGIC))
                    main.step(dve, dve.memset(minus_magic[:, :], -MAGIC))
                    main.step(dve, dve.memset(st(REAL), 1.0))
                    main.global_max(dve, h_max[:, :])
                    main.quant_scale(dve, S_H, I_H)

                    def split(g, q, par, first):
                        dve.wait_ge(s_hl[par], 16 * (q + 1))
                        if not first:
                            dve.wait_ge(s_raw, (g - 1) * M2)
                        dve.tensor_scalar(xt[:, par, :, :, :], h_in[:, par, :, :, :], st(I_H), MAGIC,
                                          ALU.mult, ALU.add).then_inc(s_xt, 1)
                        dve.wait_ge(s_xt, g + 1)
                        dve.tensor_scalar(x_hi[:, par, :, :, :], xt[:, par, :, :, :], MAGIC, None,
                                          ALU.subtract).then_inc(s_xh, 1)
                        dve.wait_ge(s_xh, g + 1)
                        dve.scalar_tensor_tensor(out=x_lo[:, par, :, :, :].rearrange("p b c t -> p (b c t)"),
                                                 in0=xt[:, par, :, :, :].rearrange("p b c t -> p (b c t)"),
                                                 scalar=MAGIC,
                                                 in1=x_hi[:, par, :, :, :].rearrange("p b c t -> p (b c t)"),
                                                 op0=ALU.subtract, op1=ALU.subtract).then_inc(s_xl, 1)

                    def maxima(g, par, ms):
                        for m in ms:
                            dve.wait_ge(s_copy, g * M2 + (m + 1))
                            if m >= NM:
                                dve.tensor_reduce(out=gate_top[:, m - NM, bass.ds(g, 1)],
                                                  in_=stage[:, m // MB, m % MB, :], axis=AX.X,
                                                  op=ALU.max).then_inc(s_top, 1)
                            dve.tensor_reduce(out=raw_max[:, m, bass.ds(g, 1)], in_=stage[:, m // MB, m % MB, :],
                                              axis=AX.X, op=ALU.max, apply_absolute_value=True).then_inc(s_rmax, 1)

                    def reduce_and_split(g, q, par, first=False):
                        maxima(g, par, range(6))
                        split(g + 1, q + par, 1 - par, first)
                        maxima(g, par, range(6, M2))

                    split(0, 0, 0, True)
                    reduce_and_split(0, 0, 0, True)
                    reduce_and_split(1, 0, 1)
                    with dve.Fori(1, NG // 2 - 1, 1) as q:
                        reduce_and_split(q * 2, q, 0)
                        reduce_and_split(q * 2 + 1, q, 1)
                    reduce_and_split(NG - 2, NG // 2 - 1, 0)
                    maxima(NG - 1, 1, range(M2))
                    dve.wait_ge(s_rmax, NG * M2)
                    main.step(dve, dve.tensor_scalar(st(REAL), st(S_H), 1.0 / WS, None, ALU.mult))
                    flat = raw_max[:, :, :].rearrange("p m g -> p (m g)")
                    for n, (s_out, c_out) in enumerate(((S_U, C_U), (S_G, C_G))):
                        main.global_max(dve, flat[:, n * NM * NG:(n + 1) * NM * NG])
                        main.quant_scale(dve, s_out, c_out)
                    dve.wait_ge(s_top, NG * NM)
                    main.global_max(dve, gate_top[:, :, :].rearrange("p m g -> p (m g)"))

                @block.gpsimd
                def _(pool):
                    for n in range(4):
                        main.pool_max(pool)

                @block.tensor
                def _(pe):
                    def body(g, par):
                        pe.wait_ge(s_xl, g + 1)
                        for m in range(M2):
                            bank = banks[(M2 * par + m) % 8]
                            if not isinstance(g, int) or g * M2 + m >= 8:
                                pe.wait_ge(s_copy, g * M2 + (m - 7))
                            for c in range(NC):
                                cols = slice(m * P, (m + 1) * P)
                                hi, lo = x_hi[:, par, :, c, :], x_lo[:, par, :, c, :]
                                pe.matmul(bank[:, :], w_gu_t[:, c, 0, cols], hi, start=c == 0, stop=False)
                                pe.matmul(bank[:, :], w_gu_t[:, c, 0, cols], lo, start=False, stop=False)
                                last = pe.matmul(bank[:, :], w_gu_t[:, c, 1, cols], hi, start=False, stop=c == NC - 1)
                            last.then_inc(s_raw, 1)

                    body(0, 0)
                    body(1, 1)
                    with pe.Fori(1, NG // 2, 1) as q:
                        body(q * 2, 0)
                        body(q * 2 + 1, 1)

                @block.scalar
                def _(act):
                    def body(g, par, first):
                        for m in range(M2):
                            q, j = divmod(m, MB)
                            act.wait_ge(s_raw, g * M2 + (m + 1))
                            if j == 0 and not first:
                                act.wait_ge(s_store[q], 16 * g)
                                act.wait_ge(s_rmax, (g - 1) * M2 + MB * (q + 1))
                            act.activation(stage[:, q, j, :], banks[(M2 * par + m) % 8][:, :],
                                           ACT.Copy).then_inc(s_copy, 1)

                    body(0, 0, True)
                    body(1, 1, False)
                    with act.Fori(1, NG // 2, 1) as q:
                        body(q * 2, 0, False)
                        body(q * 2 + 1, 1, False)

                @block.sync
                def _(sp):
                    def load(g, par):
                        sp.dma_start(h_in[:, par, :, :, :], h_d[bass.ds(g * GB, GB)]
                                     .rearrange("b p c t -> p b c t")).then_inc(s_hl[par], 16)

                    def store(g):
                        for q in range(NB):
                            sp.wait_ge(s_copy, g * M2 + MB * (q + 1))
                            m0 = MB * (q % 2)
                            sp.dma_start(raw_d[q // 2, g, m0:m0 + MB].rearrange("m p t -> p m t"), stage[:, q, :, :]).then_inc(s_store[q], 16)

                    load(0, 0)
                    load(1, 1)
                    with sp.Fori(0, NG // 2 - 1, 1) as q:
                        for par in range(2):
                            g = q * 2
                            sp.wait_ge(s_xt, g + (par + 1))
                            load(g + (par + 2), par)
                            store(g + par)
                    store(NG - 2)
                    store(NG - 1)
                    for q in range(NB):
                        sp.wait_ge(s_store[q], 16 * NG)

        mid.close()

        with ExitStack() as c4:
            s_tg = sem("top_gate_steps")

            with nc.Block() as block:

                @block.scalar
                def _(act):
                    act.activation(st(TOP), st(ALL), ACT.Identity, bias=magic[:, 0:1], scale=st(C_G)).then_inc(s_tg, 1)
                    act.wait_ge(s_tg, 2)
                    act.activation(st(TSIG), st(TOP), ACT.Sigmoid, scale=st(S_G)).then_inc(s_tg, 1)

                @block.vector
                def _(dve):
                    dve.wait_ge(s_tg, 1)
                    dve.tensor_scalar(st(TOP), st(TOP), MAGIC, None, ALU.subtract).then_inc(s_tg, 1)
                    main.step(dve, dve.tensor_scalar(st(REAL), st(S_G), 1.0 / SIG, None, ALU.mult))
                    dve.wait_ge(s_tg, 3)
                    main.step(dve, dve.tensor_scalar(st(TSIG), st(TSIG), SIG, MAGIC, ALU.mult, ALU.add))
                    main.step(dve, dve.tensor_scalar(st(TSIG), st(TSIG), MAGIC, SIG - 1, ALU.subtract, ALU.min))
                    main.step(dve, dve.tensor_tensor(st(ALL), st(TOP), st(TSIG), ALU.mult))
                    main.quant_scale(dve, S_P, C_P)
                    main.step(dve, dve.tensor_tensor(st(TOP), st(ALL), st(REAL), ALU.mult))
                    main.step(dve, dve.tensor_scalar(needed[:, :], st(TOP), -NEG_BOUND, None, ALU.is_lt))

        PM = NM // 2
        PIECES = 2 * NG
        W = PM * GRP
        up_d, gate_d = (raw_d[n].rearrange("g (h m) p t -> (g h) p m t", h=2) for n in range(2))
        o_pieces = o_d.rearrange("g (h m) p t -> (g h) p m t", h=2)

        def piece(buf, n):
            return buf[:, n, :].rearrange("p (m t) -> p m t", m=PM)

        for with_up in (False, True):
            tag = "o" if with_up else "gate"
            scales = main if with_up else gate_pass
            with ExitStack() as c2:
                g_in = sb(f"{tag}_g_in", [P, 2, W], F32, c2)
                g_t = sb(f"{tag}_g_t", [P, W], F32, c2)
                g_n = sb(f"{tag}_g_n", [P, 2, W], F32, c2)
                sg = sb(f"{tag}_sig", [P, 2, W], F32, c2)
                prod = sb(f"{tag}_prod", [P, 2, W], F32, c2)
                p_max = sb(f"{tag}_p_max", [P, PIECES], F32, c2)
                s_gl = [sem(f"{tag}_gate_loaded_{n}") for n in range(2)]
                s_gt = sem(f"{tag}_gate_plus_magic")
                s_gn = sem(f"{tag}_gate_integer")
                s_sg = sem(f"{tag}_sigmoid")
                s_sa = sem(f"{tag}_sigmoid_rounded")
                s_sq = sem(f"{tag}_sigmoid_integer")
                s_pr = sem(f"{tag}_product")
                s_fin = sem(f"{tag}_piece_reduced")
                s_oo = sem(f"{tag}_output_ready")
                if with_up:
                    u_in = sb("u_in", [P, 2, W], F32, c2)
                    u_t = sb("u_t", [P, W], F32, c2)
                    u_n = sb("u_n", [P, 2, W], F32, c2)
                    o_sb = sb("o_sb", [P, 2, W], F32, c2)
                    s_ul = [sem(f"up_loaded_{n}") for n in range(2)]
                    s_ut = sem("up_plus_magic")
                    s_un = sem("up_integer")
                    s_g2 = sem("gate_requantised")
                    s_ow = [sem(f"o_stored_{n}") for n in range(2)]

                GATE_IN, GATE, SIGMOID, ROUND, UP_IN, UP, NOW, STORE = 4, 3, 2, 1, 2, 1, 0, -1

                def over_pieces(eng, body):
                    def iteration(pair, n):
                        def at(off):
                            j = pair * 2 + (n + off)
                            if isinstance(pair, int) and not 0 <= j < PIECES:
                                return None
                            return j, (n + off) % 2, pair + (n + off) // 2
                        body(at)

                    for i in range(-GATE_IN, 4):
                        iteration(i // 2, i % 2)
                    with eng.Fori(2, PIECES // 2 - 2, 1) as pair:
                        iteration(pair, 0)
                        iteration(pair, 1)
                    for i in range(PIECES - 4, PIECES - STORE):
                        iteration(i // 2, i % 2)

                def first(j, n=1):
                    return isinstance(j, int) and j < n

                def when_needed(eng):
                    if with_up:
                        return nullcontext()
                    flag = eng.value_load(needed[0:1, 0:1], min_val=0, max_val=1)
                    return eng.If(flag != 0)

                with nc.Block() as block:

                    @block.sync
                    def _(sp):
                        def body(at):
                            if at(GATE_IN):
                                j, n, _ = at(GATE_IN)
                                if not first(j, 2):
                                    sp.wait_ge(s_gt, j - 1)
                                sp.dma_start(piece(g_in, n), gate_d[j]).then_inc(s_gl[n], 16)
                            if with_up and at(UP_IN):
                                j, n, _ = at(UP_IN)
                                if not first(j, 2):
                                    sp.wait_ge(s_ut, j - 1)
                                sp.dma_start(piece(u_in, n), up_d[j]).then_inc(s_ul[n], 16)

                        with when_needed(sp):
                            over_pieces(sp, body)

                    @block.scalar
                    def _(act):
                        def up(j, n, q):
                            act.wait_ge(s_ul[n], 16 * (q + 1))
                            if not first(j):
                                act.wait_ge(s_un, j)
                            act.activation(u_t[:, :], u_in[:, n, :], ACT.Identity, bias=magic[:, 0:1],
                                           scale=st(C_U)).then_inc(s_ut, 1)
                            act.wait_ge(s_ut, j + 1)
                            if not first(j, 2):
                                act.wait_ge(s_oo, j - 1)
                            act.activation(u_n[:, n, :], u_t[:, :], ACT.Identity,
                                           bias=minus_magic[:, 0:1]).then_inc(s_un, 1)

                        def sigmoid(j, n, q):
                            act.wait_ge(s_gn, j + 1)
                            if not first(j, 2):
                                act.wait_ge(s_pr, j - 1)
                            act.activation(sg[:, n, :], g_n[:, n, :], ACT.Sigmoid, scale=st(S_G)).then_inc(s_sg, 1)

                        def gate(j, n, q):
                            act.wait_ge(s_gl[n], 16 * (q + 1))
                            if not first(j):
                                act.wait_ge(s_gn, j)
                            act.activation(g_t[:, :], g_in[:, n, :], ACT.Identity, bias=magic[:, 0:1],
                                           scale=st(C_G)).then_inc(s_gt, 1)

                        def body(at):
                            if with_up and at(UP):
                                up(*at(UP))
                            if at(SIGMOID):
                                sigmoid(*at(SIGMOID))
                            if at(GATE):
                                gate(*at(GATE))
                            if with_up and at(STORE):
                                j, n, _ = at(STORE)
                                act.wait_ge(s_oo, j + 1)
                                act.dma_start(o_pieces[j], piece(o_sb, n)).then_inc(s_ow[n], 16)

                        with when_needed(act):
                            over_pieces(act, body)
                        if with_up:
                            for n in range(2):
                                act.wait_ge(s_ow[n], 16 * (PIECES // 2))

                    @block.gpsimd
                    def _(pool):
                        def body(at):
                            if at(ROUND):
                                j, n, _ = at(ROUND)
                                pool.wait_ge(s_sq, j + 1)
                                if not first(j, 2):
                                    pool.wait_ge(s_fin, j - 1)
                                pool.tensor_tensor(prod[:, n, :], g_n[:, n, :], sg[:, n, :],
                                                   ALU.mult).then_inc(s_pr, 1)

                        with when_needed(pool):
                            over_pieces(pool, body)
                            scales.pool_max(pool)

                    @block.vector
                    def _(dve):
                        def gate(j, n, q):
                            dve.wait_ge(s_gt, j + 1)
                            if not first(j, 2):
                                dve.wait_ge(s_pr, j - 1)
                            dve.tensor_scalar(g_n[:, n, :], g_t[:, :], MAGIC, None, ALU.subtract).then_inc(s_gn, 1)

                        def add_magic(j, n, q):
                            dve.wait_ge(s_sg, j + 1)
                            dve.tensor_scalar(sg[:, n, :], sg[:, n, :], SIG, MAGIC, ALU.mult, ALU.add)\
                               .then_inc(s_sa, 1)

                        def clip(j, n, q):
                            dve.wait_ge(s_sa, j + 1)
                            dve.tensor_scalar(sg[:, n, :], sg[:, n, :], MAGIC, SIG - 1, ALU.subtract, ALU.min)\
                               .then_inc(s_sq, 1)

                        def requantise(j, n, q):
                            dve.wait_ge(s_pr, j + 1)
                            dve.tensor_scalar(prod[:, n, :], prod[:, n, :], st(C_P), MAGIC, ALU.mult, ALU.add)\
                               .then_inc(s_g2, 1)

                        def times_up(j, n, q):
                            dve.wait_ge(s_g2, j + 1)
                            if not first(j, 2):
                                dve.wait_ge(s_ow[n], 16 * q)
                            dve.wait_ge(s_un, j + 1)
                            dve.scalar_tensor_tensor(out=o_sb[:, n, :], in0=prod[:, n, :], scalar=MAGIC,
                                                     in1=u_n[:, n, :], op0=ALU.subtract,
                                                     op1=ALU.mult).then_inc(s_oo, 1)

                        def maximum(j, n, q):
                            dve.wait_ge(s_oo if with_up else s_pr, j + 1)
                            dve.tensor_reduce(out=p_max[:, bass.ds(j, 1)], in_=(o_sb if with_up else prod)[:, n, :],
                                              axis=AX.X, op=ALU.max, apply_absolute_value=True).then_inc(s_fin, 1)

                        STAGES = [(add_magic, ROUND), (requantise, NOW), (clip, ROUND), (times_up, NOW),
                                  (gate, SIGMOID), (maximum, NOW)]
                        if not with_up:
                            STAGES = [(add_magic, ROUND), (gate, SIGMOID), (clip, ROUND), (maximum, NOW)]

                        def body(at):
                            for stage_of, off in STAGES:
                                if at(off):
                                    stage_of(*at(off))

                        with when_needed(dve):
                            over_pieces(dve, body)
                            dve.wait_ge(s_fin, PIECES)
                            if with_up:
                                scales.step(dve, dve.tensor_tensor(st(REAL), st(S_P), st(S_U), ALU.mult))
                                scales.global_max(dve, p_max[:, :])
                                scales.quant_scale(dve, S_O, C_O)
                                scales.step(dve, dve.tensor_scalar(st(S_O), st(S_O), 1.0 / WS, None, ALU.mult))
                            else:
                                scales.step(dve, dve.tensor_scalar(st(REAL), st(S_G), 1.0 / SIG, None, ALU.mult))
                                scales.global_max(dve, p_max[:, :])
                                scales.quant_scale(dve, S_P, C_P)

        GT = GRP // P
        GB = GRP // SEQ
        with ExitStack() as c3:
            o_in = sb("o_in", [P, 2, NM, GRP], F32, c3)
            o_t = sb("o_t", [P, 2, NM, GRP], F32, c3)
            o_hi = sb("o_hi", [P, 2, NM, GRP], F16, c3)
            o_lo = sb("o_lo", [P, 2, NM, GRP], F16, c3)
            x2_in = sb("x2_in", [P, 2, GB, NT, D], F32, c3)
            y = sb("y", [P, 2, GT, D], F32, c3)
            s_ol = [sem(f"o_loaded_{n}") for n in range(2)]
            s_xl2 = [sem(f"x2_loaded_{n}") for n in range(2)]
            s_ot = sem("o_plus_magic")
            s_oh = sem("o_hi_ready")
            s_olo = sem("o_lo_ready")
            s_down = sem("down_product_done")
            s_y = sem("y_ready")
            s_yw = [sem(f"y_stored_{n}") for n in range(2)]

            def pairs(eng, body):
                for n in range(2):
                    body(n, 0, n, True)
                with eng.Fori(1, NG // 2, 1) as q:
                    for n in range(2):
                        body(q * 2 + n, q, n, False)

            with nc.Block() as block:

                @block.sync
                def _(sp):
                    def load_o(g, n):
                        if not (isinstance(g, int) and g < 2):
                            sp.wait_ge(s_ot, g - 1)
                        sp.dma_start(o_in[:, n, :, :], o_d[g].rearrange("m p t -> p m t")).then_inc(s_ol[n], 16)

                    def load_x2(g, n):
                        if not (isinstance(g, int) and g < 2):
                            sp.wait_ge(s_y, (g - 1) * GT)
                        sp.dma_start(x2_in[:, n, :, :, :], x2_d[bass.ds(g * GB, GB)]
                                     .rearrange("b p t d -> p b t d")).then_inc(s_xl2[n], 16)

                    load_o(0, 0)
                    for g in range(2):
                        load_o(g + 1, 1 - g)
                        load_x2(g, g)
                    with sp.Fori(1, NG // 2 - 1, 1) as q:
                        for n in range(2):
                            load_o(q * 2 + (n + 1), 1 - n)
                            load_x2(q * 2 + n, n)
                    load_o(NG - 1, 1)
                    load_x2(NG - 2, 0)
                    load_x2(NG - 1, 1)

                @block.scalar
                def _(act):
                    def body(g, q, n, first):
                        act.wait_ge(s_ol[n], 16 * (q + 1))
                        if not first:
                            act.wait_ge(s_olo, g - 1)
                        act.activation(o_t[:, n, :, :], o_in[:, n, :, :], ACT.Identity, bias=magic[:, 0:1],
                                       scale=st(C_O)).then_inc(s_ot, 1)
                        if not first:
                            store(g - 2, n)

                    def store(g, n):
                        act.wait_ge(s_y, (g + 1) * GT)
                        act.dma_start(out_g[bass.ds(g * GT, GT)].rearrange("t p d -> p t d"),
                                      y[:, n, :, :]).then_inc(s_yw[n], 16)

                    pairs(act, body)
                    store(NG - 2, 0)
                    store(NG - 1, 1)
                    for n in range(2):
                        act.wait_ge(s_yw[n], 16 * (NG // 2))

                @block.vector
                def _(dve):
                    def split(g, q, n, first):
                        dve.wait_ge(s_ot, g + 1)
                        if not first:
                            dve.wait_ge(s_down, (g - 1) * GT)
                        dve.tensor_scalar(o_hi[:, n, :, :], o_t[:, n, :, :], MAGIC, None,
                                          ALU.subtract).then_inc(s_oh, 1)
                        dve.wait_ge(s_oh, g + 1)
                        dve.scalar_tensor_tensor(out=o_lo[:, n, :, :], in0=o_t[:, n, :, :], scalar=MAGIC,
                                                 in1=o_hi[:, n, :, :], op0=ALU.subtract,
                                                 op1=ALU.subtract).then_inc(s_olo, 1)

                    def add(g, q, n, first):
                        dve.wait_ge(s_xl2[n], 16 * (q + 1))
                        if not first:
                            dve.wait_ge(s_yw[n], 16 * q)
                        for t in range(GT):
                            dve.wait_ge(s_down, g * GT + (t + 1))
                            dve.scalar_tensor_tensor(out=y[:, n, t, :], in0=banks[GT * n + t][:, 0:D],
                                                     scalar=st(S_O), in1=x2_in[:, n, t // NT, t % NT, :],
                                                     op0=ALU.mult, op1=ALU.add).then_inc(s_y, 1)

                    split(0, 0, 0, True)
                    split(1, 0, 1, True)
                    add(0, 0, 0, True)
                    split(2, 1, 0, False)
                    add(1, 0, 1, True)
                    with dve.Fori(1, NG // 2 - 1, 1) as q:
                        split(q * 2 + 1, q, 1, False)
                        add(q * 2, q, 0, False)
                        split(q * 2 + 2, q + 1, 0, False)
                        add(q * 2 + 1, q, 1, False)
                    split(NG - 1, NG // 2 - 1, 1, False)
                    add(NG - 2, NG // 2 - 1, 0, False)
                    add(NG - 1, NG // 2 - 1, 1, False)

                @block.tensor
                def _(pe):
                    def body(g, q, n, first):
                        pe.wait_ge(s_olo, g + 1)
                        for t in range(GT):
                            if not first:
                                pe.wait_ge(s_y, (g - 2) * GT + (t + 1))
                            bank = banks[GT * n + t][:, 0:D]
                            for m in range(NM):
                                hi = o_hi[:, n, m, t * P:(t + 1) * P]
                                lo = o_lo[:, n, m, t * P:(t + 1) * P]
                                pe.matmul(bank, hi, w_down_t[:, m, 0, :], start=m == 0, stop=False)
                                pe.matmul(bank, lo, w_down_t[:, m, 0, :], start=False, stop=False)
                                last = pe.matmul(bank, hi, w_down_t[:, m, 1, :], start=False, stop=m == NM - 1)
                            last.then_inc(s_down, 1)

                    pairs(pe, body)


_SELF = ["L0_attn_Wq", "L0_attn_Wk", "L0_attn_Wv", "L0_attn_Wo"]
_SELF_B = ["L0_attn_bq", "L0_attn_bk", "L0_attn_bv", "L0_attn_bo"]
_CROSS = ["L0_xattn_Wq", "L0_xattn_Wk", "L0_xattn_Wv", "L0_xattn_Wo"]
_CROSS_B = ["L0_xattn_bq", "L0_xattn_bk", "L0_xattn_bv", "L0_xattn_bo"]
_FFN = ["L0_ffn_w_gate", "L0_ffn_w_up", "L0_ffn_w_down"]


def kernel(**inputs):
    import numpy as _np
    import concourse.bacc as _bacc
    from concourse import mybir as _mybir
    from concourse.bass_utils import run_bass_kernel_spmd as _run

    nc = _bacc.Bacc("TRN2", target_bir_lowering=False, num_devices=1)
    arrays, aps = {}, {}
    for name in ["x", "ctx_1024", "mask_1x1xSxS2_fk1"] + _SELF + _SELF_B + _CROSS + _CROSS_B + _FFN:
        a = _np.ascontiguousarray(inputs[name])
        arrays[f"in_{name}_dram"] = a
        aps[name] = nc.dram_tensor(f"in_{name}_dram", a.shape, _mybir.dt.from_np(a.dtype), kind="ExternalInput").ap()
    out = nc.dram_tensor("out_0_dram", (BATCH, SEQ, D), _mybir.dt.float32, kind="ExternalOutput").ap()
    decoder_kernel(nc, aps["x"], aps["ctx_1024"], aps["mask_1x1xSxS2_fk1"],
                   [aps[n] for n in _SELF], [aps[n] for n in _SELF_B],
                   [aps[n] for n in _CROSS], [aps[n] for n in _CROSS_B],
                   *[aps[n] for n in _FFN], out)
    r = _run(nc, [arrays], core_ids=[0])
    return r.results[0]["out_0_dram"]
```
